# Optimizing a Trainium2 kernel written in Bass

```python
import numpy as np
import jax
import jax.numpy as jnp

def _softmax(x, axis=-1):
    return jax.nn.softmax(x, axis=axis)

def _gelu(x):
    return jax.nn.gelu(x, approximate=True)

def _silu(x):
    return jax.nn.silu(x)

def _sigmoid(x):
    return jax.nn.sigmoid(x)

def _layernorm(x, axis=-1, eps=1e-05):
    m = jnp.mean(x, axis=axis, keepdims=True)
    v = jnp.var(x, axis=axis, keepdims=True)
    return (x - m) / jnp.sqrt(v + eps)

def _scatter_add(tgt, idx, src, axis=0):
    return tgt.at[idx].add(src)

def _segment_sum(src, seg, n):
    return jax.ops.segment_sum(src, seg, n)
kernel_name = 'mk_gnn_resnorm_d2_gnn_r8_70e4b8'

def setup_inputs(seed: int=0):
    np.random.seed(seed)
    _w = jnp.asarray

    def _rec_inputs():
        import jax
        import jax.numpy as jnp
        _gk = jax.random.key(seed)
        x = 0.0004528 + 0.9998 * jax.random.normal(jax.random.fold_in(_gk, 1), (12500, 16), jnp.float32)
        src = jax.random.randint(jax.random.fold_in(_gk, 2), (400000,), 0, 12500, jnp.int32)
        dst = jax.random.randint(jax.random.fold_in(_gk, 3), (400000,), 0, 12500, jnp.int32)
        _o = jnp.argsort(dst, stable=True)
        src = src[_o]
        dst = dst[_o]
        edge_type_8 = jax.random.randint(jax.random.fold_in(_gk, 12), (400000,), 0, 8, jnp.int32)
        return (x, src, dst, edge_type_8)
    x, src, dst, edge_type_8 = _rec_inputs()

    def _L0_gnn_setup():
        import jax, jax.numpy as jnp
        import numpy as np
        NUM_ENTITIES = 12500
        NUM_RELATIONS = 8
        NUM_CLASSES = 16
        HIDDEN = 16
        NUM_EDGES = 400000

        def rgcn_conv(x, src, dst, edge_type, W, root, bias):
            num_nodes = x.shape[0]
            x_src = x[src]
            msg = jnp.zeros((src.shape[0], W.shape[2]), x.dtype)
            for r in range(NUM_RELATIONS):
                msg = msg + jnp.where((edge_type == r)[:, None], x_src @ W[r], jnp.zeros((), x.dtype))
            cnt = jnp.zeros((num_nodes, NUM_RELATIONS), x.dtype).at[dst, edge_type].add(1.0)
            norm = 1.0 / jnp.maximum(cnt[dst, edge_type], 1.0)
            agg = jax.ops.segment_sum(msg * norm[:, None], dst, num_segments=num_nodes)
            return agg + x @ root + bias
        key = jax.random.key(seed)
        ks = jax.random.split(key, 9)
        s = 1.0 / np.sqrt(HIDDEN)
        edge_index = jax.random.randint(ks[0], (2, NUM_EDGES), 0, NUM_ENTITIES, dtype=jnp.int32)
        edge_type = jax.random.randint(ks[1], (NUM_EDGES,), 0, NUM_RELATIONS, dtype=jnp.int32)
        return {'embed': jax.random.normal(ks[2], (NUM_ENTITIES, HIDDEN), jnp.float32), 'W1': jax.random.normal(ks[3], (NUM_RELATIONS, HIDDEN, HIDDEN), jnp.float32) * s, 'root1': jax.random.normal(ks[4], (HIDDEN, HIDDEN), jnp.float32) * s, 'b1': jnp.zeros((HIDDEN,), jnp.float32), 'W2': jax.random.normal(ks[5], (NUM_RELATIONS, HIDDEN, NUM_CLASSES), jnp.float32) * s, 'root2': jax.random.normal(ks[6], (HIDDEN, NUM_CLASSES), jnp.float32) * s, 'b2': jnp.zeros((NUM_CLASSES,), jnp.float32), 'edge_index': edge_index, 'edge_type': edge_type}
    _L0_gnn_all = _L0_gnn_setup()
    _L0_gnn_in = {k: v for k, v in _L0_gnn_all.items() if k in ('W1', 'root1', 'b1', 'W2', 'root2', 'b2')}
    del _L0_gnn_all

    def _L1_gnn_setup():
        import jax, jax.numpy as jnp
        import numpy as np
        STALK_DIM = 16
        N_NODES = 6250
        N_EDGES = 50000
        HIDDEN = 64
        key = jax.random.key(seed)
        k1, k2, k3, k4 = jax.random.split(key, 4)
        d = STALK_DIM
        x = jax.random.normal(k1, (N_NODES, d), dtype=jnp.float32)
        edge_index = jax.random.randint(k2, (2, N_EDGES), 0, N_NODES, dtype=jnp.int64)
        W1 = jax.random.normal(k3, (HIDDEN, 2 * d), dtype=jnp.float32) * (1.0 / np.sqrt(2 * d))
        b1 = jnp.zeros((HIDDEN,), dtype=jnp.float32)
        W2 = jax.random.normal(k4, (d, HIDDEN), dtype=jnp.float32) * (1.0 / np.sqrt(HIDDEN))
        b2 = jnp.zeros((d,), dtype=jnp.float32)
        return {'x': x, 'edge_index': edge_index, 'W1': W1, 'b1': b1, 'W2': W2, 'b2': b2}
    _L1_gnn_all = _L1_gnn_setup()
    _L1_gnn_in = {k: v for k, v in _L1_gnn_all.items() if k in ('W1', 'b1', 'W2', 'b2')}
    del _L1_gnn_all
    return {'x': x, 'src': src, 'dst': dst, 'edge_type_8': edge_type_8, 'L0_gnn_W1': _L0_gnn_in['W1'], 'L0_gnn_root1': _L0_gnn_in['root1'], 'L0_gnn_b1': _L0_gnn_in['b1'], 'L0_gnn_W2': _L0_gnn_in['W2'], 'L0_gnn_root2': _L0_gnn_in['root2'], 'L0_gnn_b2': _L0_gnn_in['b2'], 'L1_gnn_W1': _L1_gnn_in['W1'], 'L1_gnn_b1': _L1_gnn_in['b1'], 'L1_gnn_W2': _L1_gnn_in['W2'], 'L1_gnn_b2': _L1_gnn_in['b2']}

def reference(x, src, dst, edge_type_8, L0_gnn_W1, L0_gnn_root1, L0_gnn_b1, L0_gnn_W2, L0_gnn_root2, L0_gnn_b2, L1_gnn_W1, L1_gnn_b1, L1_gnn_W2, L1_gnn_b2):
    import jax
    import jax.numpy as jnp

    def _L0_gnn_ref(embed, W1, root1, b1, W2, root2, b2, edge_index, edge_type):
        import jax, jax.numpy as jnp
        import numpy as np
        NUM_ENTITIES = 12500
        NUM_RELATIONS = 8
        NUM_CLASSES = 16
        HIDDEN = 16
        NUM_EDGES = 400000

        def rgcn_conv(x, src, dst, edge_type, W, root, bias):
            num_nodes = x.shape[0]
            x_src = x[src]
            msg = jnp.zeros((src.shape[0], W.shape[2]), x.dtype)
            for r in range(NUM_RELATIONS):
                msg = msg + jnp.where((edge_type == r)[:, None], x_src @ W[r], jnp.zeros((), x.dtype))
            cnt = jnp.zeros((num_nodes, NUM_RELATIONS), x.dtype).at[dst, edge_type].add(1.0)
            norm = 1.0 / jnp.maximum(cnt[dst, edge_type], 1.0)
            agg = jax.ops.segment_sum(msg * norm[:, None], dst, num_segments=num_nodes)
            return agg + x @ root + bias
        src, dst = (edge_index[0], edge_index[1])
        h = rgcn_conv(embed, src, dst, edge_type, W1, root1, b1)
        h = jax.nn.relu(h)
        h = rgcn_conv(h, src, dst, edge_type, W2, root2, b2)
        return jax.nn.log_softmax(h, axis=1)

    def _L1_gnn_ref(x, edge_index, W1, b1, W2, b2):
        import jax, jax.numpy as jnp
        import numpy as np
        STALK_DIM = 16
        N_NODES = 6250
        N_EDGES = 50000
        HIDDEN = 64
        d = x.shape[1]
        n = x.shape[0]
        src, dst = (edge_index[0], edge_index[1])
        xs, xd = (x[src], x[dst])

        def reflection(a, b):
            h = jax.nn.relu(jnp.concatenate([a, b], axis=1) @ W1.T + b1)
            return h @ W2.T + b2

        def householder(v):
            vn = v / jnp.maximum(jnp.linalg.norm(v, axis=1, keepdims=True), 1e-12)
            return jnp.eye(d, dtype=v.dtype)[None] - 2.0 * vn[:, :, None] * vn[:, None, :]
        F_s = householder(reflection(xs, xd))
        F_d = householder(reflection(xd, xs))
        L_sd = -jnp.einsum('eki,ekj->eij', F_s, F_d)
        ones_e = jnp.ones(src.shape[0], dtype=x.dtype)
        deg = jnp.zeros(n, dtype=x.dtype).at[src].add(ones_e).at[dst].add(ones_e)
        deg_inv_sqrt = 1.0 / jnp.sqrt(jnp.maximum(deg, 1e-05))
        coef = deg_inv_sqrt[src] * deg_inv_sqrt[dst]
        msg_s = coef[:, None] * jnp.einsum('eij,ej->ei', L_sd, xd)
        msg_d = coef[:, None] * jnp.einsum('eji,ej->ei', L_sd, xs)
        out = x - jnp.zeros_like(x).at[src].add(msg_s) - jnp.zeros_like(x).at[dst].add(msg_d)
        return jax.nn.relu(out)
    edge_index = jnp.stack([src, dst])
    x = _layernorm(x + _L0_gnn_ref(x, L0_gnn_W1, L0_gnn_root1, L0_gnn_b1, L0_gnn_W2, L0_gnn_root2, L0_gnn_b2, edge_index, edge_type_8), axis=-1)
    x = _layernorm(x + _L1_gnn_ref(x, edge_index, L1_gnn_W1, L1_gnn_b1, L1_gnn_W2, L1_gnn_b2), axis=-1)
    return x

_drawn_inputs = setup_inputs


def setup_inputs(seed=0):
    import zlib

    import numpy as np

    out = dict(_drawn_inputs(seed))
    spreads = {'L0_gnn_b1': (0.0, 0.1),
     'L0_gnn_b2': (0.0, 0.1),
     'L1_gnn_b1': (0.0, 0.713),
     'L1_gnn_b2': (0.0, 0.363)}
    factors = {}
    for name, (base, spread) in spreads.items():
        noise = np.random.default_rng([zlib.crc32(name.encode()), seed]).standard_normal(out[name].shape)
        drawn = base * np.exp(spread * noise) if base else spread * noise
        out[name] = jnp.asarray(drawn.astype(out[name].dtype))
    for name, factor in factors.items():
        out[name] = (out[name] * factor).astype(out[name].dtype)
    return out
```

```python
import numpy as np
import concourse.bass as bass
from concourse import mybir
from contextlib import ExitStack

P = 128
N, D, R, E = 12500, 16, 8, 400000
TG = 25
GE = P * TG
NG = E // GE
UNITS = [(0, 13), (13, 25)]
UMAX = 13
W = 128
NB = -(-N // P)
NP = NB * P
NW = NP // W
NACC = NP + W
CB = 7
CN = CB * P
NC = NB // CB
HID = 64
ROW = D + 1
NT = 5
TROWS = NP + P
CHUNKS = [[(0, 4), (4, 8), (8, 12), (12, 13)], [(0, 4), (4, 8), (8, 12)]]
NCH = sum(len(c) for c in CHUNKS)
PER_TABLE = [[len(range(k, b - a, NT)) for k in range(NT)] for a, b in UNITS]
T_GROUP = [sum(p[k] for p in PER_TABLE) for k in range(NT)]
assert GE * NG == E and NC * CB == NB


class Chain:

    def __init__(self, eng, sem):
        self.eng, self.sem, self.n = eng, sem, 0

    def do(self, ins):
        ins.then_inc(self.sem, 1)
        self.n += 1

    def wait(self):
        self.eng.wait_ge(self.sem, self.n)

    def restart(self):
        if self.n:
            self.wait()
            self.eng.sem_clear(self.sem)
            self.n = 0


def build(nc, x, src, dst, et, l0w1, l0r1, l0b1, l0w2, l0r2, l0b2, l1w1, l1b1, l1w2, l1b2, out):
    f32, i32, bf16 = mybir.dt.float32, mybir.dt.int32, mybir.dt.bfloat16
    ALU, ACT = mybir.AluOpType, mybir.ActivationFunctionType
    AX = mybir.AxisListType.X
    RMAX = bass.bass_isa.ReduceOp.max
    ctx = ExitStack()
    with ctx:
        def sb(name, shape, dt=f32):
            return ctx.enter_context(nc.sbuf_tensor(name, shape, dt))

        def sem(name):
            return ctx.enter_context(nc.semaphore(name))

        h_table = nc.dram_tensor("h_table", [NP, D], f32).ap()
        x1_table = nc.dram_tensor("x1_table", [NP, ROW], f32).ap()
        sums = [nc.dram_tensor(f"sums{k}", [TROWS, D], f32).ap() for k in range(NT)]

        src_i = sb("src_i", [P, NG, TG], i32)
        dst_i = sb("dst_i", [P, NG, TG], i32)
        typ_i = sb("typ_i", [P, NG, TG], i32)
        agg = sb("agg", [P, NACC])
        big = sb("big", [P, NACC])
        cnt = big[0:R, :]
        ident = sb("ident", [P, P])
        iota_w = sb("iota_w", [P, P])
        iota_r = sb("iota_r", [P, R])
        before = sb("before", [P, P])
        expand = sb("expand", [R, P])
        band = sb("band", [R, P])
        ones = sb("ones", [P, P])
        dump = sb("dump", [P, 1])
        first_i = sb("first_i", [1, NG], i32)
        first_f = sb("first_f", [1, NG])
        base_tab = sb("base_tab", [P, NG + NW])
        wrel = [sb(f"wrel{k}", [P, D]) for k in range(2)]
        root = [sb(f"root{k}", [ROW, D]) for k in range(2)]
        w_hid = sb("w_hid", [2 * ROW, 2 * HID])
        b_hid = sb("b_hid", [2 * HID, 1])
        w_out = sb("w_out", [2 * HID, 2 * D])
        b_out = sb("b_out", [P, 2 * D])
        x_node = sb("x_node", [P, NB, D])
        h_node = sb("h_node", [P, NB, D])
        deg = sb("deg", [P, NB])
        stat = [sb(f"stat{k}", [P, NB]) for k in range(2)]
        cnt_c = sb("cnt_c", [R, CN])
        inv_c = sb("inv_c", [R, CN])
        agg_c = sb("agg_c", [P, CN])
        xs_c = sb("xs_c", [P, CB, D])
        xT_c = sb("xT_c", [ROW, CN])
        idx_s = [sb(f"idx_s{u}", [P, UMAX], i32) for u in range(2)]
        idx_d = [sb(f"idx_d{u}", [P, UMAX], i32) for u in range(2)]
        xx = [sb(f"xx{u}", [P, UMAX, 2 * ROW]) for u in range(2)]
        rel = sb("rel", [P, UMAX])
        dst_hot = sb("dst_hot", [P, UMAX, W])
        typ_hot = sb("typ_hot", [P, UMAX, R])
        typ_x = sb("typ_x", [P, UMAX, R, D])
        same = sb("same", [P, UMAX, P])
        same_b = sb("same_b", [P, UMAX, P])
        lo_hot = sb("lo_hot", [P, UMAX, P], bf16)
        hi_hot = sb("hi_hot", [P, UMAX, NB], bf16)
        lo_i = sb("lo_i", [P, UMAX], i32)
        hi_i = sb("hi_i", [P, UMAX], i32)
        red = sb("red", [P, 2])
        red_all = sb("red_all", [P, 2])
        flag_f = sb("flag_f", [1, 2])
        flag_i = sb("flag_i", [1, 1], i32)

        place = [0]

        def carve(*shape):
            size = int(np.prod(shape))
            v = big[:, place[0]:place[0] + size]
            place[0] += size
            names = "abc"[:len(shape)]
            if len(shape) == 1:
                return v
            return v.rearrange(f"p ({' '.join(names)}) -> p {' '.join(names)}", **dict(zip(names, shape)))

        vv = carve(UMAX, 2, D)
        xw = carve(UMAX, 2, D)
        m1 = carve(UMAX, 2, D)
        m2 = carve(UMAX, 2, D)
        m3 = carve(UMAX, D)
        msg = [carve(UMAX, 2, D) for _ in range(2)]
        n2 = carve(UMAX, 2)
        cc = carve(UMAX, 2)
        pv = carve(UMAX, 2)
        rv = carve(UMAX, 2)
        av = carve(UMAX, 2)
        bv = carve(UMAX, 2)
        qv = carve(UMAX)
        srcf = carve(UMAX)
        nbef = carve(UMAX)
        fidx = carve(UMAX)
        xT = [carve(4 * P) for _ in range(2)]
        hid = [carve(4 * P) for _ in range(2)]
        msum = [carve(UMAX, D) for _ in range(2)]
        idx_o = [carve(UMAX).bitcast(i32) for _ in range(2)]
        assert place[0] <= NACC
        tab = [big[:, k * NB * D:(k + 1) * NB * D] for k in range(NT)]
        z_node = x_node

        bank = [ctx.enter_context(nc.psum_tensor(f"bank{k}", [P, 512], f32)) for k in range(8)]
        ps_acc, ps_cnt, ps_hist = bank[0], bank[1], bank[2]
        ps_E = [bank[3], bank[4]]
        ps_xT = [bank[5], bank[6]]
        ps_o = bank[7]
        ps_t = [bank[1], bank[2]]
        ps_h = [bank[3], bank[4]]
        ps_v, ps_r, ps_s = bank[5], bank[6], bank[7]

        s_consts = sem("s_consts")
        s_iota = sem("s_iota")
        s_zeroed = sem("s_zeroed")
        s_loaded = sem("s_loaded")
        s_first = sem("s_first")
        s_row = sem("s_row")
        s_red = sem("s_red")
        s_redall = sem("s_redall")
        s_flag = sem("s_flag")
        s_tick = sem("s_tick")
        s_xfree = [sem(f"s_xfree{u}") for u in range(2)]
        s_idx = sem("s_idx")
        s_gat = [sem(f"s_gat{u}") for u in range(2)]
        s_gatc = [sem(f"s_gatc{u}") for u in range(2)]
        s_hot = sem("s_hot")
        s_acc = sem("s_acc")
        s_hhot = sem("s_hhot")
        s_hist = sem("s_hist")
        s_inv = sem("s_inv")
        s_E = sem("s_E")
        s_aggc = sem("s_aggc")
        s_xsc = sem("s_xsc")
        s_xTp = sem("s_xTp")
        s_xTc = sem("s_xTc")
        s_node = sem("s_node")
        s_hnode = sem("s_hnode")
        s_htab = sem("s_htab")
        s_ztab = sem("s_ztab")
        s_table = [sem(f"s_table{k}") for k in range(NT)]
        s_exp = sem("s_exp")
        s_act = sem("s_act")
        s_tr = sem("s_tr")
        s_xt = sem("s_xt")
        s_hp = sem("s_hp")
        s_hs = sem("s_hs")
        s_vd = sem("s_vd")
        s_vfree = sem("s_vfree")
        s_rr = sem("s_rr")
        s_rused = sem("s_rused")
        s_same = sem("s_same")
        s_msg = sem("s_msg")
        s_sp = sem("s_sp")
        s_ms = sem("s_ms")
        s_idxo = sem("s_idxo")
        s_scat = [sem(f"s_scat{u}") for u in range(2)]
        s_end = sem("s_end")
        s_free = sem("s_free")
        s_sums = sem("s_sums")
        s_out = sem("s_out")
        s_vch = sem("s_vch")

        NLOAD = 24
        block = ctx.enter_context(nc.Block())
        groups = "(g p j) -> p g j"

        def blocks(ap):
            return ap.rearrange("(b p) d -> p b d", p=P)

        @block.sync
        def _(sp):
            def load(o, i):
                sp.dma_start(o, i, allow_slow_non_contiguous=True).then_inc(s_loaded, 16)
                loads.append(1)
            loads = []
            sp.dma_start(first_i[0:1, :], dst.rearrange("(o g e) -> o g e", o=1, e=GE)[:, :, 0],
                         allow_slow_non_contiguous=True).then_inc(s_first, 16)
            load(dst_i[:, :, :], dst.rearrange(groups, p=P, j=TG))
            load(src_i[:, :, :], src.rearrange(groups, p=P, j=TG))
            load(typ_i[:, :, :], et.rearrange(groups, p=P, j=TG))
            sp.wait_ge(s_zeroed, 1)
            load(x_node[:, 0:NB - 1, :], blocks(x[0:(NB - 1) * P, :]))
            load(x_node[0:N - (NB - 1) * P, NB - 1, :], x[(NB - 1) * P:N, :])
            for k, (w, r, b) in enumerate(((l0w1, l0r1, l0b1), (l0w2, l0r2, l0b2))):
                load(wrel[k][:, :], w.rearrange("r d f -> (r d) f"))
                load(root[k][0:D, :], r)
                load(root[k][D:ROW, :], b.rearrange("(o f) -> o f", o=1))
            w1T = l1w1.rearrange("h k -> k h")
            for half, (a, b) in enumerate(((0, ROW), (ROW, 0))):
                load(w_hid[a:a + D, half * HID:(half + 1) * HID], w1T[0:D, :])
                load(w_hid[b:b + D, half * HID:(half + 1) * HID], w1T[D:2 * D, :])
                load(b_hid[half * HID:(half + 1) * HID, :], l1b1.rearrange("(h o) -> h o", o=1))
                load(w_out[half * HID:(half + 1) * HID, half * D:(half + 1) * D], l1w2.rearrange("d h -> h d"))
                load(b_out[:, half * D:(half + 1) * D], l1b2.partition_broadcast(P))
            for k in range(NT):
                load(sums[k].rearrange("(p f) d -> p (f d)", p=P), agg[:, 0:TROWS * D // P])
            assert len(loads) == NLOAD + 2, len(loads)
            sp.wait_ge(s_hnode, NC)
            sp.dma_start(blocks(h_table), h_node[:, :, :]).then_inc(s_htab, 16)
            sp.wait_ge(s_ztab, 1)
            sp.dma_start(blocks(x1_table)[:, :, 0:D], x_node[:, :, :]).then_inc(s_htab, 16)
            sp.dma_start(blocks(x1_table)[:, :, D], deg[:, :], allow_slow_non_contiguous=True).then_inc(s_htab, 16)
            sp.wait_ge(s_end, 1)
            sp.wait_ge(s_free, 1)
            for k in range(NT):
                sp.dma_start(tab[k].rearrange("p (b d) -> p b d", d=D), blocks(sums[k][0:NP, :])).then_inc(s_sums, 16)
            sp.wait_ge(s_out, 1)
            sp.dma_start(blocks(out[0:(NB - 1) * P, :]), x_node[:, 0:NB - 1, :]).then_inc(s_out, 16)
            sp.dma_start(out[(NB - 1) * P:N, :], x_node[0:N - (NB - 1) * P, NB - 1, :]).then_inc(s_out, 16)
            sp.wait_ge(s_out, 33)

        LOADED = 16 * (NLOAD + 2)

        @block.gpsimd
        def _(pool):
            iota = nc.gpsimd.iota
            iota(ident[:, :], [[1, P]], base=0, channel_multiplier=-1,
                 allow_small_or_imprecise_dtypes=True).then_inc(s_iota, 1)
            iota(iota_w[:, :], [[1, P]], base=0, channel_multiplier=0,
                 allow_small_or_imprecise_dtypes=True).then_inc(s_iota, 1)
            iota(iota_r[:, :], [[1, R]], base=0, channel_multiplier=0,
                 allow_small_or_imprecise_dtypes=True).then_inc(s_iota, 1)
            iota(band[:, :], [[1, P]], base=0, channel_multiplier=-D,
                 allow_small_or_imprecise_dtypes=True).then_inc(s_iota, 1)
            iota(dump[:, :], [[0, 1]], base=NP, channel_multiplier=1,
                 allow_small_or_imprecise_dtypes=True).then_inc(s_iota, 1)
            iota(base_tab[:, NG:NG + NW], [[W, NW]], base=0, channel_multiplier=0,
                 allow_small_or_imprecise_dtypes=True).then_inc(s_iota, 1)
            pool.wait_ge(s_red, 1)
            nc.gpsimd.partition_all_reduce(red_all[:, :], red[:, :], P, RMAX).then_inc(s_redall, 1)
            pool.wait_ge(s_loaded, LOADED)

            def gather(to, table, idx):
                return pool.indirect_dma_start(out=to, out_offset=None, in_=table,
                                               in_offset=bass.IndirectOffsetOnAxis(ap=idx, axis=0))

            for k, table in enumerate((x, h_table)):
                if k:
                    pool.wait_ge(s_htab, 16)
                with pool.Fori(0, NG) as g:
                    for u, (a, b) in enumerate(UNITS):
                        pool.wait_ge(s_xfree[u], g + (k * NG + 1))
                        pool.sem_inc(s_tick, 1)
                        nc.gpsimd.tensor_copy(idx_s[u][:, 0:b - a], src_i[:, g, a:b]).then_inc(s_idx, 1)
                        pool.wait_ge(s_idx, 2 * g + (2 * k * NG + u + 1))
                        pool.sem_inc(s_tick, 1)
                        for j in range(b - a):
                            gather(xx[u][:, j, 0:D], table, idx_s[u][:, j:j + 1]).then_inc(s_gat[u], 16)

            pool.wait_ge(s_htab, 48)

            def gather_unit(u, g):
                a, b = UNITS[u]
                pool.wait_ge(s_xfree[u], g + (2 * NG + 1))
                pool.sem_inc(s_tick, 1)
                nc.gpsimd.tensor_copy(idx_s[u][:, 0:b - a], src_i[:, g, a:b]).then_inc(s_idx, 1)
                nc.gpsimd.tensor_copy(idx_d[u][:, 0:b - a], dst_i[:, g, a:b]).then_inc(s_idx, 1)
                pool.wait_ge(s_idx, 4 * g + (4 * NG + 2 * u + 2))
                pool.sem_inc(s_tick, 1)
                for j in range(b - a):
                    gather(xx[u][:, j, 0:ROW], x1_table, idx_s[u][:, j:j + 1]).then_inc(s_gatc[u], 16)
                    gather(xx[u][:, j, ROW:2 * ROW], x1_table, idx_d[u][:, j:j + 1]).then_inc(s_gatc[u], 16)

            def scatter_unit(u, g):
                a, b = UNITS[u]
                pool.wait_ge(s_ms, 2 * g + (u + 2))
                pool.sem_inc(s_tick, 1)
                pool.wait_ge(s_idxo, 2 * g + (u + 1))
                pool.sem_inc(s_tick, 1)
                for j in range(b - a):
                    k = j % NT
                    if j >= NT:
                        done = (PER_TABLE[0][k] if u else 0) + j // NT
                        pool.wait_ge(s_table[k], 16 * T_GROUP[k] * g + 16 * done)
                        pool.sem_inc(s_tick, 1)
                    pool.indirect_dma_start(out=sums[k], out_offset=bass.IndirectOffsetOnAxis(ap=idx_o[u][:, j:j + 1], axis=0),
                                            in_=msum[u][:, j, :], in_offset=None, compute_op=ALU.add).then_inc(s_table[k], 16)

            def scattered(u, g):
                for k in range(NT):
                    done = PER_TABLE[0][k] + (PER_TABLE[1][k] if u else 0)
                    pool.wait_ge(s_table[k], 16 * T_GROUP[k] * g + 16 * done)
                pool.sem_inc(s_scat[u], 1)

            for u in range(2):
                gather_unit(u, 0)
            with pool.Fori(0, NG - 1) as g:
                for u in range(2):
                    scatter_unit(u, g)
                    gather_unit(u, g + 1)
                    scattered(u, g)
            for u in range(2):
                scatter_unit(u, NG - 1)
                scattered(u, NG - 1)
            pool.sem_inc(s_end, 1)

        @block.vector
        def _(dve):
            V = nc.vector
            ch = Chain(dve, s_vch)
            for t in (agg, big, x_node, w_hid, w_out, xT_c, ones, deg):
                ch.do(V.memset(t[:], 1.0 if t in (ones, xT_c) else 0.0))
            ch.wait()
            dve.sem_inc(s_zeroed, 1)
            dve.wait_ge(s_iota, 6)
            ch.do(V.tensor_scalar(before[:, :], ident[:, :], 0.0, None, ALU.is_lt))
            ch.do(V.tensor_scalar(expand[:, :], band[:, :], 0.0, None, ALU.is_ge))
            ch.do(V.tensor_scalar(band[:, :], band[:, :], float(D), None, ALU.is_lt))
            dve.wait_ge(s_first, 16)
            ch.do(V.tensor_copy(first_f[0:1, :], first_i[0:1, :]))
            ch.wait()
            ch.do(V.tensor_tensor(expand[:, :], expand[:, :], band[:, :], ALU.mult))
            ch.do(V.tensor_scalar(ident[:, :], ident[:, :], 0.0, None, ALU.is_equal))
            ch.wait()
            for s in (s_xfree[0], s_xfree[1], s_node, s_vd, s_vfree, s_rused, s_ms, s_scat[0], s_scat[1]):
                dve.sem_inc(s, 1)
            dve.sem_inc(s_consts, 1)
            dve.wait_ge(s_row, 1)
            ch.do(V.tensor_copy(base_tab[:, 0:NG], ps_acc[:, 0:NG]))
            dve.wait_ge(s_loaded, LOADED)
            ch.wait()
            off = typ_x[:, :, :, :].rearrange("p a b c -> p (a b c)")
            part = NG // 5 * TG
            for h in range(5):
                gs = slice(h * NG // 5, (h + 1) * NG // 5)
                o = off[:, 0:part].rearrange("p (g j) -> p g j", j=TG)
                ch.do(V.tensor_tensor(o, dst_i[:, gs, :], base_tab[:, gs].unsqueeze(2).to_broadcast([P, NG // 5, TG]),
                                      ALU.subtract))
                ch.wait()
                ch.do(V.tensor_reduce(stat[0][:, h:h + 1], off[:, 0:part], AX, ALU.max))
                ch.do(V.tensor_reduce(stat[1][:, h:h + 1], off[:, 0:part], AX, ALU.min, negate=True))
                ch.wait()
            ch.do(V.tensor_reduce(red[:, 0:1], stat[0][:, 0:5], AX, ALU.max))
            V.tensor_reduce(red[:, 1:2], stat[1][:, 0:5], AX, ALU.max).then_inc(s_red, 1)
            dve.wait_ge(s_redall, 1)
            ch.do(V.tensor_scalar(flag_f[0:1, 0:1], red_all[0:1, 0:1], float(W - 1), None, ALU.is_le))
            ch.do(V.tensor_scalar(flag_f[0:1, 1:2], red_all[0:1, 1:2], 0.0, None, ALU.is_le))
            ch.wait()
            V.tensor_tensor(flag_i[0:1, :], flag_f[0:1, 0:1], flag_f[0:1, 1:2], ALU.mult).then_inc(s_flag, 1)
            ch.restart()
            dve.wait_ge(s_flag, 1)

            def add_window(u, g, windows, phase, rows):
                a, b = UNITS[u]
                n = b - a

                def step(column, base, count):
                    ch.do(V.tensor_scalar(rel[:, 0:n], dst_i[:, g, a:b], base_tab[:, bass.ds(column, 1)], None,
                                          ALU.subtract))
                    ch.wait()
                    V.tensor_tensor(dst_hot[:, 0:n, :], rel[:, 0:n].unsqueeze(2).to_broadcast([P, n, W]),
                                    iota_w[:, :].unsqueeze(1).to_broadcast([P, n, W]), ALU.is_equal).then_inc(s_hot, 1)
                    dve.wait_ge(s_acc, count + 1)
                    acc = agg[0:rows, bass.ds(base, W)]
                    ch.do(V.tensor_tensor(acc, acc, ps_acc[0:rows, 0:W], ALU.add))
                    if phase == 0:
                        acc = cnt[:, bass.ds(base, W)]
                        ch.do(V.tensor_tensor(acc, acc, ps_cnt[0:R, 0:W], ALU.add))

                if windows == 1:
                    base = dve.value_load(first_i[0:1, bass.ds(g, 1)], min_val=0, max_val=N - 1)
                    step(g, base, 2 * g + (2 * phase * NG + u))
                else:
                    ch.restart()
                    with dve.Fori(0, NW) as w:
                        step(w + NG, w * W, g * (2 * NW) + w + (2 * phase * NG + u) * NW)
                        ch.restart()

            def relational(phase, windows):
                with dve.Fori(0, NG) as g:
                    for u, (a, b) in enumerate(UNITS):
                        n = b - a
                        ch.do(V.tensor_tensor(typ_hot[:, 0:n, :], typ_i[:, g, a:b].unsqueeze(2).to_broadcast([P, n, R]),
                                              iota_r[:, :].unsqueeze(1).to_broadcast([P, n, R]), ALU.is_equal))
                        ch.wait()
                        dve.wait_ge(s_gat[u], g * (16 * n) + 16 * n * (phase * NG + 1))
                        V.tensor_tensor(typ_x[:, 0:n, :, :],
                                        typ_hot[:, 0:n, :].unsqueeze(3).to_broadcast([P, n, R, D]),
                                        xx[u][:, 0:n, 0:D].unsqueeze(2).to_broadcast([P, n, R, D]),
                                        ALU.mult).then_inc(s_xfree[u], 1)
                        if phase == 1:
                            ch.do(V.tensor_scalar(lo_i[:, 0:n], src_i[:, g, a:b], P - 1, None, ALU.bitwise_and))
                            ch.do(V.tensor_scalar(hi_i[:, 0:n], src_i[:, g, a:b], 7, None, ALU.logical_shift_right))
                            ch.wait()
                            ch.do(V.tensor_tensor(lo_hot[:, 0:n, :], lo_i[:, 0:n].unsqueeze(2).to_broadcast([P, n, P]),
                                                  iota_w[:, :].unsqueeze(1).to_broadcast([P, n, P]), ALU.is_equal))
                            V.tensor_tensor(hi_hot[:, 0:n, :], hi_i[:, 0:n].unsqueeze(2).to_broadcast([P, n, NB]),
                                            iota_w[:, 0:NB].unsqueeze(1).to_broadcast([P, n, NB]),
                                            ALU.is_equal).then_inc(s_hhot, 1)
                        add_window(u, g, windows, phase, P)
                        if phase == 1:
                            dve.wait_ge(s_hist, 2 * g + (u + 1))
                            ch.do(V.tensor_tensor(deg[:, :], deg[:, :], ps_hist[:, 0:NB], ALU.add))
                    ch.restart()

            def nodes(phase):
                with dve.Fori(0, NC) as i:
                    ch.do(V.tensor_copy(cnt_c[:, :], cnt[:, bass.ds(i * CN, CN)]))
                    ch.do(V.tensor_scalar(inv_c[:, :], cnt[:, bass.ds(i * CN, CN)], 1.0, None, ALU.max))
                    ch.wait()
                    V.reciprocal(inv_c[:, :], inv_c[:, :]).then_inc(s_inv, 1)
                    dve.wait_ge(s_E, i + (phase * NC + 1))
                    half = CN // 2
                    for h in range(2):
                        last = V.tensor_tensor(agg_c[:, h * half:(h + 1) * half], agg[:, bass.ds(i * CN + h * half, half)],
                                               ps_E[h][:, 0:half], ALU.mult)
                        if h == 0:
                            ch.do(last)
                    last.then_inc(s_aggc, 1)
                    dve.wait_ge(s_node, i + (phase * NC + 2))
                    res = ps_o[:, 0:CB * D].rearrange("p (b d) -> p b d", d=D)
                    o = h_node[:, bass.ds(i * CB, CB), :]
                    if phase == 0:
                        d = deg[:, bass.ds(i * CB, CB)]
                        ch.do(V.tensor_tensor(d, d, ps_o[:, CB * D:CB * D + CB], ALU.add))
                        V.tensor_scalar(o, res, 0.0, None, ALU.max).then_inc(s_hnode, 1)
                    else:
                        ch.do(V.tensor_copy(o, res))
                    ch.restart()

            full = [P, NB, D]

            def wide(s):
                return s[:, :].unsqueeze(2).to_broadcast(full)

            def layer_norm(y, tmp, act_count, extra=None):
                ch.wait()
                ch.do(V.tensor_reduce(stat[0][:, :], y, AX, ALU.add))
                ch.wait()
                ch.do(V.tensor_scalar(stat[0][:, :], stat[0][:, :], 1.0 / D, None, ALU.mult))
                ch.wait()
                ch.do(V.tensor_tensor(y, y, wide(stat[0]), ALU.subtract))
                ch.wait()
                ch.do(V.tensor_tensor(tmp, y, y, ALU.mult))
                ch.wait()
                ch.do(V.tensor_reduce(stat[1][:, :], tmp, AX, ALU.add))
                ch.wait()
                V.tensor_scalar(stat[1][:, :], stat[1][:, :], 1.0 / D, 1e-5, ALU.mult, ALU.add).then_inc(s_exp, 1)
                dve.wait_ge(s_act, act_count)
                ch.do(V.reciprocal(stat[1][:, :], stat[1][:, :]))
                ch.wait()

            def program(windows):
                relational(0, windows)
                nodes(0)
                dve.wait_ge(s_htab, 16)
                ch.do(V.memset(agg[:, :], 0.0))
                ch.restart()
                relational(1, windows)
                nodes(1)
                z, y = h_node[:, :, :], x_node[:, :, :]
                tmp = agg[:, 0:NB * D].rearrange("p (b d) -> p b d", d=D)
                ch.do(V.tensor_reduce(stat[0][:, :], z, AX, ALU.max))
                ch.wait()
                ch.do(V.tensor_tensor(z, z, wide(stat[0]), ALU.subtract))
                ch.wait()
                V.tensor_scalar(deg[:, :], deg[:, :], 1e-5, None, ALU.max).then_inc(s_exp, 1)
                dve.wait_ge(s_act, 2)
                ch.do(V.tensor_reduce(stat[0][:, :], tmp, AX, ALU.add))
                ch.do(V.reciprocal(deg[:, :], deg[:, :]))
                ch.wait()
                ch.do(V.tensor_tensor(y, y, z, ALU.add))
                ch.wait()
                V.tensor_scalar(stat[1][:, :], stat[0][:, :], 1.0, None, ALU.mult).then_inc(s_exp, 1)
                dve.wait_ge(s_act, 3)
                ch.do(V.tensor_tensor(y, y, wide(stat[1]), ALU.subtract))
                layer_norm(y, tmp, 4)
                V.tensor_tensor(y, y, wide(stat[1]), ALU.mult).then_inc(s_ztab, 1)
                dve.wait_ge(s_ztab, 1)
                ch.do(V.memset(agg[0:D, :], 0.0))
                ch.restart()
                with dve.Fori(0, NG) as g:
                    done = 0
                    for u, (a, b) in enumerate(UNITS):
                        sheaf_unit(u, a, b - a, g, done, windows)
                        done += len(CHUNKS[u])
                    ch.restart()
                dve.sem_inc(s_free, 1)
                dve.wait_ge(s_sums, 16 * NT)
                for k in range(1, NT):
                    ch.do(V.tensor_tensor(tab[0], tab[0], tab[k], ALU.add))
                    ch.wait()
                ch.restart()
                with dve.Fori(0, NC) as i:
                    V.tensor_copy(agg_c[0:D, :], agg[0:D, bass.ds(i * CN, CN)]).then_inc(s_aggc, 1)
                    dve.wait_ge(s_node, i + (2 * NC + 2))
                    ch.do(V.tensor_copy(h_node[:, bass.ds(i * CB, CB), :],
                                        ps_o[:, 0:CB * D].rearrange("p (b d) -> p b d", d=D)))
                    ch.restart()
                ch.do(V.tensor_tensor(z, z, tab[0].rearrange("p (b d) -> p b d", d=D), ALU.add))
                ch.wait()
                ch.do(V.tensor_tensor(z, z, wide(deg), ALU.mult))
                ch.wait()
                ch.do(V.tensor_tensor(z, z, y, ALU.add))
                ch.wait()
                ch.do(V.tensor_scalar(z, z, 0.0, None, ALU.max))
                ch.wait()
                ch.do(V.tensor_tensor(y, y, z, ALU.add))
                layer_norm(y, tmp, 5)
                V.tensor_tensor(y, y, wide(stat[1]), ALU.mult).then_inc(s_out, 1)

            def sheaf_unit(u, a, n, g, done, windows):
                ch.do(V.tensor_copy(srcf[:, 0:n], src_i[:, g, a:a + n]))
                ch.wait()
                V.tensor_copy(fidx[:, 0:n], srcf[:, 0:n]).then_inc(s_same, 1)
                for c, (ca, cb) in enumerate(CHUNKS[u]):
                    m = cb - ca
                    dve.wait_ge(s_rr, NCH * g + (done + c + 1))
                    V.tensor_tensor(same[:, ca:cb, :], srcf[:, ca:cb].unsqueeze(2).to_broadcast([P, m, P]),
                                    ps_r[:, 0:m * P].rearrange("p (a e) -> p a e", e=P), ALU.is_equal).then_inc(s_rused, 1)
                dve.wait_ge(s_rused, NCH * g + (done + len(CHUNKS[u]) + 1))
                ch.do(V.tensor_tensor(same_b[:, 0:n, :], same[:, 0:n, :],
                                      before[:, :].unsqueeze(1).to_broadcast([P, n, P]), ALU.mult))
                ch.wait()
                ch.do(V.tensor_reduce(nbef[:, 0:n], same_b[:, 0:n, :], AX, ALU.add))
                ch.do(V.tensor_scalar(fidx[:, 0:n], srcf[:, 0:n], dump[:, 0:1], None, ALU.subtract))
                ch.wait()
                ch.do(V.tensor_scalar(nbef[:, 0:n], nbef[:, 0:n], 0.0, None, ALU.is_equal))
                ch.wait()
                ch.do(V.tensor_tensor(fidx[:, 0:n], fidx[:, 0:n], nbef[:, 0:n], ALU.mult))
                ch.wait()
                dve.wait_ge(s_scat[u], g + 1)
                V.tensor_scalar(idx_o[u][:, 0:n], fidx[:, 0:n], dump[:, 0:1], None, ALU.add).then_inc(s_idxo, 1)
                dve.wait_ge(s_vd, NCH * g + (done + len(CHUNKS[u]) + 1))
                v, xu, mu = vv[:, 0:n], xw[:, 0:n], msg[u][:, 0:n]
                t1, t2, t3 = m1[:, 0:n], m2[:, 0:n], m3[:, 0:n]
                both = [P, n, 2, D]
                xs = xx[u][:, 0:n, :].rearrange("p n (s r) -> p n s r", s=2)
                V.tensor_tensor(v.rearrange("p n s d -> p n (s d)"),
                                ps_v[:, 0:n * 2 * D].rearrange("p (n d) -> p n d", d=2 * D),
                                b_out[:, :].unsqueeze(1).to_broadcast([P, n, 2 * D]), ALU.add).then_inc(s_vfree, 1)
                dve.wait_ge(s_gatc[u], g * (32 * n) + 32 * n)
                V.tensor_tensor(xu, xs[:, :, :, 0:D], xs[:, :, :, D:ROW].to_broadcast(both), ALU.mult).then_inc(s_xfree[u], 1)
                dve.wait_ge(s_vfree, 2 * g + (u + 2))
                ch.do(V.tensor_tensor(t1, v, v, ALU.mult))
                dve.wait_ge(s_xfree[u], g + (2 * NG + 2))
                ch.do(V.tensor_tensor(t2, v, xu, ALU.mult))
                ch.do(V.tensor_tensor(t3, v[:, :, 0, :], v[:, :, 1, :], ALU.mult))
                ch.wait()
                ch.do(V.tensor_reduce(n2[:, 0:n], t1, AX, ALU.add))
                ch.do(V.tensor_reduce(pv[:, 0:n], t2, AX, ALU.add))
                ch.do(V.tensor_reduce(qv[:, 0:n], t3, AX, ALU.add))
                ch.wait()
                for s in range(2):
                    ch.do(V.tensor_tensor(t1[:, :, s, :], v[:, :, s, :], xu[:, :, 1 - s, :], ALU.mult))
                ch.do(V.tensor_scalar(cc[:, 0:n], n2[:, 0:n], 1e-24, 0.5, ALU.max, ALU.mult))
                ch.wait()
                ch.do(V.tensor_reduce(rv[:, 0:n], t1, AX, ALU.add))
                ch.do(V.reciprocal(cc[:, 0:n], cc[:, 0:n]))
                ch.wait()
                ch.do(V.tensor_tensor(av[:, 0:n], cc[:, 0:n], pv[:, 0:n], ALU.mult))
                ch.wait()
                for s in range(2):
                    ch.do(V.tensor_tensor(bv[:, 0:n, s], av[:, 0:n, 1 - s], qv[:, 0:n], ALU.mult))
                ch.do(V.tensor_tensor(t2, v, av[:, 0:n].unsqueeze(3).to_broadcast(both), ALU.mult))
                ch.wait()
                ch.do(V.tensor_tensor(bv[:, 0:n], rv[:, 0:n], bv[:, 0:n], ALU.subtract))
                ch.wait()
                ch.do(V.tensor_tensor(bv[:, 0:n], bv[:, 0:n], cc[:, 0:n], ALU.mult))
                for s in range(2):
                    ch.do(V.tensor_tensor(mu[:, :, s, :], xu[:, :, 1 - s, :], t2[:, :, 1 - s, :], ALU.subtract))
                ch.wait()
                ch.do(V.tensor_tensor(t1, v, bv[:, 0:n].unsqueeze(3).to_broadcast(both), ALU.mult))
                ch.wait()
                V.tensor_tensor(mu, mu, t1, ALU.subtract).then_inc(s_msg, 1)
                add_window(u, g, windows, 2, D)

            fast = dve.value_load(flag_i[0:1, 0:1], min_val=0, max_val=1)
            with dve.If(fast == 1):
                program(1)
            with dve.Else():
                program(NW)

        @block.scalar
        def _(act):
            A = nc.scalar
            for phase in range(2):
                node = (x_node, h_node)[phase]
                act.wait_ge(s_loaded, LOADED)
                if phase == 1:
                    act.wait_ge(s_hnode, NC)
                with act.Fori(0, NC) as i:
                    A.copy(xs_c[:, :, :], node[:, bass.ds(i * CB, CB), :]).then_inc(s_xsc, 1)
                    act.wait_ge(s_xTp, i + (phase * NC + 1))
                    act.sem_inc(s_tick, 1)
                    act.wait_ge(s_node, i + (phase * NC + 1))
                    A.copy(xT_c[0:D, 0:4 * P], ps_xT[0][0:D, :])
                    A.copy(xT_c[0:D, 4 * P:CN], ps_xT[1][0:D, 0:CN - 4 * P]).then_inc(s_xTc, 1)
            tmp = agg[:, 0:NB * D].rearrange("p (b d) -> p b d", d=D)
            act.wait_ge(s_exp, 1)
            A.activation(tmp, h_node[:, :, :], ACT.Exp).then_inc(s_act, 1)
            A.activation(deg[:, :], deg[:, :], ACT.Sqrt).then_inc(s_act, 1)
            act.wait_ge(s_exp, 2)
            A.activation(stat[1][:, :], stat[1][:, :], ACT.Ln).then_inc(s_act, 1)
            act.wait_ge(s_exp, 3)
            A.activation(stat[1][:, :], stat[1][:, :], ACT.Sqrt).then_inc(s_act, 1)
            with act.Fori(0, NG) as g:
                done = 0
                for u, (a, b) in enumerate(UNITS):
                    nch = len(CHUNKS[u])
                    for s in range(nch + 1):
                        if s < nch:
                            m = (CHUNKS[u][s][1] - CHUNKS[u][s][0]) * P
                            act.wait_ge(s_tr, NCH * g + (done + s + 1))
                            A.copy(xT[s % 2][0:2 * ROW, 0:m], ps_t[s % 2][0:2 * ROW, 0:m]).then_inc(s_xt, 1)
                        if s > 0:
                            c = s - 1
                            m = (CHUNKS[u][c][1] - CHUNKS[u][c][0]) * P
                            act.wait_ge(s_hp, NCH * g + (done + c + 1))
                            act.sem_inc(s_tick, 1)
                            act.wait_ge(s_vd, NCH * g + (done + max(c - 1, 0) + 1))
                            A.activation(hid[c % 2][:, 0:m], ps_h[c % 2][:, 0:m], ACT.Relu,
                                         bias=b_hid[:, 0:1]).then_inc(s_hs, 1)
                    act.wait_ge(s_scat[u], g + 1)
                    act.sem_inc(s_tick, 1)
                    act.wait_ge(s_sp, 2 * g + (u + 1))
                    A.copy(msum[u][:, 0:b - a, :],
                           ps_s[:, 0:(b - a) * D].rearrange("p (n d) -> p n d", d=D)).then_inc(s_ms, 1)
                    done += nch
            act.wait_ge(s_exp, 4)
            A.activation(stat[1][:, :], stat[1][:, :], ACT.Sqrt).then_inc(s_act, 1)

        @block.tensor
        def _(pe):
            mm = nc.tensor.matmul
            pe.wait_ge(s_consts, 1)
            mm(ps_acc[:, 0:NG], ones[0:1, :], first_f[0:1, :], start=True, stop=True).then_inc(s_row, 1)
            pe.wait_ge(s_flag, 1)
            pe.wait_ge(s_loaded, LOADED)

            def windows_of(u, g, windows, phase, work):
                if windows == 1:
                    pe.wait_ge(s_hot, 2 * g + (2 * phase * NG + u + 1))
                    pe.sem_inc(s_tick, 1)
                    work()
                else:
                    with pe.Fori(0, NW) as w:
                        pe.wait_ge(s_hot, g * (2 * NW) + w + ((2 * phase * NG + u) * NW + 1))
                        pe.sem_inc(s_tick, 1)
                        work()

            def relational(phase, windows):
                with pe.Fori(0, NG) as g:
                    for u, (a, b) in enumerate(UNITS):
                        n = b - a
                        if phase == 1:
                            pe.wait_ge(s_hhot, 2 * g + (u + 1))
                            pe.sem_inc(s_tick, 1)
                            for j in range(n):
                                last = mm(ps_hist[:, 0:NB], lo_hot[:, j, :], hi_hot[:, j, :], start=j == 0, stop=j == n - 1)
                            last.then_inc(s_hist, 1)

                        def work():
                            if phase == 0:
                                for j in range(n):
                                    mm(ps_cnt[0:R, 0:W], typ_hot[:, j, :], dst_hot[:, j, :], start=j == 0, stop=j == n - 1)
                            for j in range(n):
                                last = mm(ps_acc[:, 0:W], typ_x[:, j, :, :].rearrange("p r d -> p (r d)"),
                                          dst_hot[:, j, :], start=j == 0, stop=j == n - 1)
                            last.then_inc(s_acc, 1)
                        windows_of(u, g, windows, phase, work)

            def nodes(phase):
                with pe.Fori(0, NC) as i:
                    pe.wait_ge(s_xsc, i + (phase * NC + 1))
                    pe.sem_inc(s_tick, 1)
                    for b in range(CB):
                        last = nc.tensor.transpose(ps_xT[b // 4][0:D, (b % 4) * P:(b % 4 + 1) * P], xs_c[:, b, :], ident[:, :])
                    last.then_inc(s_xTp, 1)
                    pe.wait_ge(s_inv, i + (phase * NC + 1))
                    pe.sem_inc(s_tick, 1)
                    for h in range(2):
                        last = mm(ps_E[h][:, 0:CN // 2], expand[:, :], inv_c[:, h * CN // 2:(h + 1) * CN // 2],
                                  start=True, stop=True)
                    last.then_inc(s_E, 1)
                    pe.wait_ge(s_aggc, i + (phase * NC + 1))
                    pe.sem_inc(s_tick, 1)
                    pe.wait_ge(s_xTc, i + (phase * NC + 1))
                    pe.sem_inc(s_tick, 1)
                    for b in range(CB):
                        o = ps_o[:, b * D:(b + 1) * D]
                        mm(o, agg_c[:, b * P:(b + 1) * P], wrel[phase][:, :], start=True, stop=False)
                        last = mm(o, xT_c[:, b * P:(b + 1) * P], root[phase][:, :], start=False, stop=True)
                        if phase == 0:
                            last = mm(ps_o[:, CB * D + b:CB * D + b + 1], cnt_c[:, b * P:(b + 1) * P], ones[0:R, 0:1],
                                      start=True, stop=True)
                    last.then_inc(s_node, 1)

            def sheaf(windows):
                with pe.Fori(0, NG) as g:
                    done = 0
                    for u, (a, b) in enumerate(UNITS):
                        n, nch = b - a, len(CHUNKS[u])
                        pe.wait_ge(s_same, 2 * g + (u + 1))
                        pe.sem_inc(s_tick, 1)
                        for c, (ca, cb) in enumerate(CHUNKS[u]):
                            pe.wait_ge(s_rused, NCH * g + (done + c + 1))
                            pe.sem_inc(s_tick, 1)
                            for j in range(ca, cb):
                                last = mm(ps_r[:, (j - ca) * P:(j - ca + 1) * P], srcf[:, j:j + 1].to_broadcast([P, P]),
                                          ident[:, :], start=True, stop=True)
                            last.then_inc(s_rr, 1)
                        pe.wait_ge(s_gatc[u], g * (32 * n) + 32 * n)
                        pe.sem_inc(s_tick, 1)
                        for s in range(nch + 2):
                            if s < nch:
                                ca, cb = CHUNKS[u][s]
                                for j in range(ca, cb):
                                    last = nc.tensor.transpose(ps_t[s % 2][0:2 * ROW, (j - ca) * P:(j - ca + 1) * P],
                                                               xx[u][:, j, :], ident[:, :])
                                last.then_inc(s_tr, 1)
                            if 0 < s <= nch:
                                c = s - 1
                                m = (CHUNKS[u][c][1] - CHUNKS[u][c][0]) * P
                                pe.wait_ge(s_xt, NCH * g + (done + c + 1))
                                pe.sem_inc(s_tick, 1)
                                mm(ps_h[c % 2][:, 0:m], w_hid[:, :], xT[c % 2][0:2 * ROW, 0:m],
                                   start=True, stop=True).then_inc(s_hp, 1)
                            if s > 1:
                                c = s - 2
                                ca, cb = CHUNKS[u][c]
                                pe.wait_ge(s_hs, NCH * g + (done + c + 1))
                                pe.sem_inc(s_tick, 1)
                                if c == 0:
                                    pe.wait_ge(s_vfree, 2 * g + (u + 1))
                                    pe.sem_inc(s_tick, 1)
                                for j in range(ca, cb):
                                    last = mm(ps_v[:, j * 2 * D:(j + 1) * 2 * D], hid[c % 2][:, (j - ca) * P:(j - ca + 1) * P],
                                              w_out[:, :], start=True, stop=True)
                                last.then_inc(s_vd, 1)
                        pe.wait_ge(s_msg, 2 * g + (u + 1))
                        pe.sem_inc(s_tick, 1)
                        pe.wait_ge(s_ms, 2 * g + (u + 1))
                        pe.sem_inc(s_tick, 1)
                        for j in range(n):
                            last = mm(ps_s[:, j * D:(j + 1) * D], same[:, j, :], msg[u][:, j, 0, :], start=True, stop=True)
                        last.then_inc(s_sp, 1)

                        def work():
                            for j in range(n):
                                last = mm(ps_acc[0:D, 0:W], msg[u][:, j, 1, :], dst_hot[:, j, :], start=j == 0, stop=j == n - 1)
                            last.then_inc(s_acc, 1)
                        windows_of(u, g, windows, 2, work)
                        done += nch

            def program(windows):
                relational(0, windows)
                nodes(0)
                relational(1, windows)
                nodes(1)
                sheaf(windows)
                with pe.Fori(0, NC) as i:
                    pe.wait_ge(s_aggc, i + (2 * NC + 1))
                    pe.sem_inc(s_tick, 1)
                    for b in range(CB):
                        last = nc.tensor.transpose(ps_o[:, b * D:(b + 1) * D], agg_c[0:D, b * P:(b + 1) * P], ident[0:D, 0:D])
                    last.then_inc(s_node, 1)

            fast = pe.value_load(flag_i[0:1, 0:1], min_val=0, max_val=1)
            with pe.If(fast == 1):
                program(1)
            with pe.Else():
                program(NW)


_INS = ['x', 'src', 'dst', 'edge_type_8', 'L0_gnn_W1', 'L0_gnn_root1', 'L0_gnn_b1', 'L0_gnn_W2', 'L0_gnn_root2', 'L0_gnn_b2', 'L1_gnn_W1', 'L1_gnn_b1', 'L1_gnn_W2', 'L1_gnn_b2']


def kernel(**inputs):
    import numpy as _np
    import concourse.bacc as _bacc
    from concourse import mybir as _mybir
    from concourse.bass_utils import run_bass_kernel_spmd as _run

    nc = _bacc.Bacc("TRN2", target_bir_lowering=False, num_devices=1)
    arrays, args = {}, []
    for name in _INS:
        a = _np.ascontiguousarray(inputs[name])
        arrays[f"in_{name}"] = a
        args.append(nc.dram_tensor(f"in_{name}", a.shape, _mybir.dt.from_np(a.dtype), kind="ExternalInput").ap())
    args.append(nc.dram_tensor("out", (12500, 16), _mybir.dt.float32, kind="ExternalOutput").ap())
    build(nc, *args)
    r = _run(nc, [arrays], core_ids=[0])
    return r.results[0]["out"]
```

```python
import numpy as np
import concourse.bass as bass
from concourse import mybir
from contextlib import ExitStack

P = 128
N, D, R, E = 12500, 16, 8, 400000
TG = 25
GE = P * TG
NG = E // GE
UNITS = [(0, 13), (13, 25)]
UMAX = 13
W = 128
NB = -(-N // P)
NP = NB * P
NW = NP // W
NACC = NP + W
CB = 7
CN = CB * P
NC = NB // CB
HID = 64
ROW = D + 1
NT = 5
TROWS = NP + P
CHUNKS = [[(0, 4), (4, 8), (8, 12), (12, 13)], [(0, 4), (4, 8), (8, 12)]]
NCH = sum(len(c) for c in CHUNKS)
SPAN = 7
NBS = NB + SPAN - 1
QUADS = [(j, min(j + 4, TG)) for j in range(0, TG, 4)]
NQ = len(QUADS)
VSPLIT = 16
PER_TABLE = [[len(range(k, b - a, NT)) for k in range(NT)] for a, b in UNITS]
T_GROUP = [sum(p[k] for p in PER_TABLE) for k in range(NT)]
GR = 500 // TG
ROWS = -(-NG // GR)
assert GE * NG == E and NC * CB == NB and NG % 2 == 1


class Chain:

    def __init__(self, eng, sem):
        self.eng, self.sem, self.n = eng, sem, 0

    def do(self, ins):
        ins.then_inc(self.sem, 1)
        self.n += 1

    def wait(self, but=0):
        if self.n > but:
            self.eng.wait_ge(self.sem, self.n - but)

    def restart(self):
        if self.n:
            self.wait()
            self.eng.sem_clear(self.sem)
            self.n = 0


def each_group(eng, body, last=NG):
    with eng.Fori(0, last // 2) as h:
        for b in range(2):
            body(h * 2 + b, b, h)
    if last % 2:
        body(last - 1, 0, last // 2)


def build(nc, x, src, dst, et, l0w1, l0r1, l0b1, l0w2, l0r2, l0b2, l1w1, l1b1, l1w2, l1b2, out):
    f32, i32, bf16 = mybir.dt.float32, mybir.dt.int32, mybir.dt.bfloat16
    ALU, ACT = mybir.AluOpType, mybir.ActivationFunctionType
    AX = mybir.AxisListType.X
    RMAX = bass.bass_isa.ReduceOp.max
    ctx = ExitStack()
    with ctx:
        def sb(name, shape, dt=f32):
            return ctx.enter_context(nc.sbuf_tensor(name, shape, dt))

        def sem(name):
            return ctx.enter_context(nc.semaphore(name))

        def sems(tag, names, pairs=""):
            s = {n: sem(f"{tag}_{n}") for n in names.split()}
            s.update({n: [sem(f"{tag}_{n}{k}") for k in range(2)] for n in pairs.split()})
            return s

        def carver(t):
            at = [0]

            def carve(*shape, dt=f32):
                size = int(np.prod(shape))
                words = size if dt != bf16 else -(-size // 2)
                v = t[:, at[0]:at[0] + words]
                at[0] += words
                assert at[0] <= t.shape[1], (at, t.shape)
                if dt != f32:
                    v = v.bitcast(dt)[:, 0:size]
                if len(shape) == 1:
                    return v
                names = "abcd"[:len(shape)]
                return v.rearrange(f"p ({' '.join(names)}) -> p {' '.join(names)}", **dict(zip(names, shape)))
            return carve

        h_table = nc.dram_tensor("h_table", [NP, D], f32).ap()
        x1_table = nc.dram_tensor("x1_table", [TROWS, ROW], f32).ap()
        sums = [nc.dram_tensor(f"sums{k}", [TROWS, D], f32).ap() for k in range(NT)]
        block_table = nc.dram_tensor("block_table", [NG, 32], i32).ap()

        edges = sb("edges", [P, 3 * NG * TG])
        src_i, dst_i, typ_i = (edges[:, k * NG * TG:(k + 1) * NG * TG].bitcast(i32).rearrange("p (g j) -> p g j", j=TG)
                               for k in range(3))
        fields = edges[:, 0:2 * NG * TG].bitcast(bf16).rearrange("p (g j f) -> p g j f", j=TG, f=4)
        LO, BLK, DST, TYP = range(4)
        src_s = edges[:, 2 * NG * TG:3 * NG * TG].bitcast(i32).rearrange("p (g j) -> p g j", j=TG)
        agg = sb("agg", [P, NACC])
        big = sb("big", [P, NACC])
        cnt = big[0:R, :]
        work = sb("work", [P, 6620])
        ident = sb("ident", [P, P])
        iota_w = sb("iota_w", [P, P])
        iota_r = sb("iota_r", [P, R])
        before = sb("before", [P, P])
        after = sb("after", [P, P])
        after_b = sb("after_b", [P, P], bf16)
        ones_b = sb("ones_b", [P, P], bf16)
        earlier = sb("earlier", [P, TG, TG])
        expand = sb("expand", [R, P])
        ones = sb("ones", [P, P])
        dump = sb("dump", [P, 1])
        first_i = sb("first_i", [1, NG], i32)
        first_f = sb("first_f", [1, NG])
        base_tab = sb("base_tab", [P, NG + NW])
        wrel = [sb(f"wrel{k}", [P, D]) for k in range(2)]
        root = [sb(f"root{k}", [ROW, D]) for k in range(2)]
        w_hid = sb("w_hid", [2 * ROW, 2 * HID])
        b_hid = sb("b_hid", [2 * HID, 1])
        w_out = sb("w_out", [2 * HID, 2 * D])
        b_out = sb("b_out", [P, 2 * D])
        x_node = sb("x_node", [P, NB, D])
        wide_node = sb("wide_node", [P, NBS, D])
        h_node = wide_node[:, 0:NB, :]
        deg = sb("deg", [P, NB])
        stat = [sb(f"stat{k}", [P, NB]) for k in range(2)]
        node_buf = sb("node_buf", [P, 3 * CN])
        cnt_c, inv_c, agg_c = node_buf[0:R, 0:CN], node_buf[0:R, CN:2 * CN], node_buf[:, 2 * CN:3 * CN]
        xs_c = sb("xs_c", [P, CB, D])
        xT_c = sb("xT_c", [ROW, CN])
        red = sb("red", [P, 2])
        red_all = sb("red_all", [P, 2])
        flag_f = sb("flag_f", [1, 2])
        flag_i = sb("flag_i", [1, 2], i32)
        idx = [sb(f"idx{b}", [P, TG], i32) for b in range(2)]
        xx = [sb(f"xx{b}", [P, TG, 2 * ROW]) for b in range(2)]

        carve = carver(work)
        typ_x = carve(UMAX, R, D)
        dst_hot = carve(UMAX, W)
        typ_hot = carve(UMAX, R)
        rel = carve(UMAX)
        lo_hot = carve(TG, P, dt=bf16)
        blk_hot = carve(TG, NB, dt=bf16)
        es = [carve(3, TG, dt=i32) for _ in range(2)]
        lo_i, hi_i, rk_i = (carve(TG, dt=i32) for _ in range(3))
        neg, within, rank = (carve(TG) for _ in range(3))
        fld = carve(TG, 4, dt=bf16)
        tot_T = node_buf[0:NB, TG * NB:TG * NB + P]
        prod = node_buf[:, 0:TG * NB].rearrange("p (j b) -> p j b", b=NB)
        pairs = node_buf[:, 0:TG * TG].rearrange("p (j k) -> p j k", k=TG)
        hi_hot = x_hot = wide_node[:, :, :].rearrange("p b d -> p (b d)")[:, 0:TG * TG * 2].bitcast(bf16).rearrange(
            "p (j r f) -> p j r f", r=TG, f=4)
        row_i = work[0:1, 0:NG * TG].bitcast(i32)
        row_f = work[0:1, NG * TG:2 * NG * TG]
        lo_hot_u, blk_hot_u, lo_u, hi_u = lo_hot[:, 0:UMAX, :], blk_hot[:, 0:UMAX, :], lo_i[:, 0:UMAX], hi_i[:, 0:UMAX]

        carve = carver(big)
        g_vv, g_xw, g_m1, g_m2 = (carve(UMAX, 2, D) for _ in range(4))
        g_m3 = carve(UMAX, D)
        g_msg = [carve(UMAX, 2, D) for _ in range(2)]
        g_small = [carve(UMAX, 2) for _ in range(6)]
        g_qv, srcf, nbef, fidx = (carve(UMAX) for _ in range(4))
        g_xT = [carve(4 * P) for _ in range(2)]
        g_hid = [carve(4 * P) for _ in range(2)]
        msum = [carve(UMAX, D) for _ in range(2)]
        idx_o = [carve(UMAX, dt=i32) for _ in range(2)]
        idx_s = [carve(UMAX, dt=i32) for _ in range(2)]
        idx_d = [carve(UMAX, dt=i32) for _ in range(2)]
        same, same_b = (carve(UMAX, P) for _ in range(2))
        tab = [big[:, k * NB * D:(k + 1) * NB * D] for k in range(NT)]
        carve = carver(big)
        hot = [carve(TG, W) for _ in range(2)]
        src_hot = carve(TG, P)
        msg_blk = carve(TG, SPAN, D)
        f_m1, f_m2 = (msg_blk.rearrange("p j s d -> p (j s d)")[:, k * TG * 2 * D:(k + 1) * TG * 2 * D].rearrange(
            "p (j s d) -> p j s d", s=2, d=D) for k in range(2))
        carve = carver(work)
        f_vv, f_xw = (carve(TG, 2, D) for _ in range(2))
        f_dT, f_xT, f_hid = ([carve(4 * P) for _ in range(2)] for _ in range(3))
        acc_odd = carve(NBS, D)
        acc_src = [wide_node, acc_odd]
        carve = carver(node_buf)
        f_msg = carve(TG, 2, D)
        f_m3 = carve(TG, D)
        f_small = [carve(TG, 2) for _ in range(6)]
        f_qv = carve(TG)
        blk7 = [carve(TG, SPAN) for _ in range(2)]
        f_neg = [carve(TG) for _ in range(2)]
        xwin = [carve(ROW) for _ in range(2)]

        bank = [ctx.enter_context(nc.psum_tensor(f"bank{k}", [P, 512], f32)) for k in range(8)]
        ps_acc, ps_cnt, ps_hist = bank[0], bank[1], bank[2]
        ps_rank, ps_tot, ps_fld = bank[3], bank[4], bank[5]
        ps_E = [bank[3], bank[4]]
        ps_xT = [bank[5], bank[6]]
        ps_o = bank[7]
        ps_t = [bank[1], bank[2]]
        ps_h = [bank[3], bank[4]]
        ps_v, ps_r, ps_s = bank[5], bank[6], bank[7]
        ps_vv = [bank[5], bank[6]]
        ps_x = bank[7]

        s_iota, s_consts, s_zeroed, s_loaded, s_dst, s_first, s_row = (
            sem(n) for n in "s_iota s_consts s_zeroed s_loaded s_dst s_first s_row".split())
        s_red, s_redall, s_flag, s_tick, s_vch, s_ach = (
            sem(n) for n in "s_red s_redall s_flag s_tick s_vch s_ach".split())
        s_orig = [sem(f"s_orig{k}") for k in range(2)]
        s_inv, s_E, s_aggc, s_xsc, s_xTp, s_xTc, s_node, s_hnode = (
            sem(n) for n in "s_inv s_E s_aggc s_xsc s_xTp s_xTc s_node s_hnode".split())
        s_nodes, s_htab, s_ztab, s_xtab, s_exp, s_act, s_end, s_free, s_sums, s_out = (
            sem(n) for n in "s_nodes s_htab s_ztab s_xtab s_exp s_act s_end s_free s_sums s_out".split())
        gen = [sems(f"gen{k}", "idx hot acc hhot hist", "xfree gat") for k in range(2)]
        so = sems("sort", "idx part hot acc nlo lohot hist blkhot tot totc base nrl rlhot fld fldps fldc rows rowsps blk",
                  "es esfree xfree gat")
        fa = sems("rel2", "idx part hot acc", "xfree gat")
        gs = sems("sheafg", "idx hot acc tr xt hp hs vd vfree rr rused same msg sp ms idxo", "xfree gat scat")
        s_table = [sem(f"s_table{k}") for k in range(NT)]
        sh = sems("sheaf", "idx hot acc tr dt xd xdc ttr xt hp hs vd vfree neg srchot msg msgblk sc drained",
                  "xfree gat win winfree")

        NLOAD = 24
        block = ctx.enter_context(nc.Block())
        groups = "(g p j) -> p g j"

        def blocks(ap):
            return ap.rearrange("(b p) d -> p b d", p=P)

        @block.sync
        def _(sp):
            loads = []

            def load(o, i):
                sp.dma_start(o, i, allow_slow_non_contiguous=True).then_inc(s_loaded, 16)
                loads.append(1)
            sp.dma_start(first_i[0:1, :], dst.rearrange("(o g e) -> o g e", o=1, e=GE)[:, :, 0],
                         allow_slow_non_contiguous=True).then_inc(s_first, 16)
            sp.dma_start(dst_i, dst.rearrange(groups, p=P, j=TG)).then_inc(s_dst, 16)
            sp.wait_ge(s_zeroed, 1)
            load(x_node[:, 0:NB - 1, :], blocks(x[0:(NB - 1) * P, :]))
            load(x_node[0:N - (NB - 1) * P, NB - 1, :], x[(NB - 1) * P:N, :])
            for k, (w, r, b) in enumerate(((l0w1, l0r1, l0b1), (l0w2, l0r2, l0b2))):
                load(wrel[k][:, :], w.rearrange("r d f -> (r d) f"))
                load(root[k][0:D, :], r)
                load(root[k][D:ROW, :], b.rearrange("(o f) -> o f", o=1))
            w1T = l1w1.rearrange("h k -> k h")
            for half, (a, b) in enumerate(((0, ROW), (ROW, 0))):
                load(w_hid[a:a + D, half * HID:(half + 1) * HID], w1T[0:D, :])
                load(w_hid[b:b + D, half * HID:(half + 1) * HID], w1T[D:2 * D, :])
                load(b_hid[half * HID:(half + 1) * HID, :], l1b1.rearrange("(h o) -> h o", o=1))
                load(w_out[half * HID:(half + 1) * HID, half * D:(half + 1) * D], l1w2.rearrange("d h -> h d"))
                load(b_out[:, half * D:(half + 1) * D], l1b2.partition_broadcast(P))
            for k in range(NT):
                load(sums[k].rearrange("(p f) d -> p (f d)", p=P), agg[:, 0:TROWS * D // P])
            load(x1_table[NP:TROWS, :], agg[:, 0:ROW])
            assert len(loads) == NLOAD, len(loads)

            def load_edges(n):
                for k, (o, i) in enumerate(((src_i, src), (dst_i, dst), (typ_i, et))):
                    sp.dma_start(o, i.rearrange(groups, p=P, j=TG)).then_inc(s_orig[n], 16)

            sp.wait_ge(s_flag, 1)
            fast = sp.value_load(flag_i[0:1, 0:1], min_val=0, max_val=1)
            with sp.If(fast == 1):
                by_group = [e.rearrange("(g p j) -> g p j", p=P, j=TG) for e in (src, dst, et)]

                def stream(g, b, h):
                    sp.wait_ge(so["esfree"][b], h + 1)
                    for k in range(3):
                        sp.dma_start(es[b][:, k, :], by_group[k][g, :, :]).then_inc(so["es"][b], 16)
                each_group(sp, stream)
                sp.wait_ge(so["rows"], 1)
                sp.dma_start(block_table[:, 0:TG], row_i.rearrange("p (g j) -> p g j", j=TG)).then_inc(so["blk"], 16)
            with sp.Else():
                load_edges(0)
            sp.wait_ge(s_hnode, NC)
            sp.dma_start(blocks(h_table), h_node).then_inc(s_htab, 16)
            sp.wait_ge(s_flag, 2)
            fast2 = sp.value_load(flag_i[0:1, 1:2], min_val=0, max_val=1)
            with sp.If(fast2 == 1):
                sp.sem_inc(s_tick, 1)
            with sp.Else():
                load_edges(1)
            sp.wait_ge(s_ztab, 1)
            sp.dma_start(blocks(x1_table[0:NP, :])[:, :, 0:D], x_node[:, :, :]).then_inc(s_xtab, 16)
            sp.dma_start(blocks(x1_table[0:NP, :])[:, :, D], deg[:, :], allow_slow_non_contiguous=True).then_inc(s_xtab, 16)
            with sp.If(fast2 == 1):
                sp.wait_ge(s_xtab, 32)

                def window(g, b, h):
                    sp.wait_ge(sh["winfree"][b], h + 1)
                    base = sp.value_load(first_i[0:1, bass.ds(g, 1)], min_val=0, max_val=N - 1)
                    sp.dma_start(xwin[b], x1_table[bass.ds(base, W), :]).then_inc(sh["win"][b], 16)
                each_group(sp, window)
            with sp.Else():
                sp.wait_ge(s_end, 1)
                sp.wait_ge(s_free, 1)
                for k in range(NT):
                    sp.dma_start(tab[k].rearrange("p (b d) -> p b d", d=D), blocks(sums[k][0:NP, :])).then_inc(s_sums, 16)
            sp.wait_ge(s_out, 1)
            sp.dma_start(blocks(out[0:(NB - 1) * P, :]), x_node[:, 0:NB - 1, :]).then_inc(s_out, 16)
            sp.dma_start(out[(NB - 1) * P:N, :], x_node[0:N - (NB - 1) * P, NB - 1, :]).then_inc(s_out, 16)
            sp.wait_ge(s_out, 33)

        LOADED = 16 * NLOAD

        @block.gpsimd
        def _(pool):
            def iota(t, pattern, base=0, mult=0):
                nc.gpsimd.iota(t, pattern, base=base, channel_multiplier=mult,
                               allow_small_or_imprecise_dtypes=True).then_inc(s_iota, 1)
            iota(ident[:, :], [[1, P]], mult=-1)
            iota(iota_w[:, :], [[1, P]])
            iota(iota_r[:, :], [[1, R]])
            iota(expand[:, :], [[1, P]], mult=-D)
            iota(dump[:, :], [[0, 1]], base=NP, mult=1)
            iota(base_tab[:, NG:NG + NW], [[W, NW]])
            iota(earlier[:, :, :], [[-1, TG], [1, TG]])

            def worst(n):
                pool.wait_ge(s_red, n)
                nc.gpsimd.partition_all_reduce(red_all[:, :], red[:, :], P, RMAX).then_inc(s_redall, 1)

            worst(1)
            pool.wait_ge(s_loaded, LOADED)
            pool.wait_ge(s_flag, 1)

            def gather(to, table, at):
                return pool.indirect_dma_start(out=to, out_offset=None, in_=table,
                                               in_offset=bass.IndirectOffsetOnAxis(ap=at, axis=0))

            def rows_general(s, table):
                with pool.Fori(0, NG) as g:
                    for u, (a, b) in enumerate(UNITS):
                        pool.wait_ge(s["xfree"][u], g + 1)
                        pool.sem_inc(s_tick, 1)
                        nc.gpsimd.tensor_copy(idx[u][:, 0:b - a], src_i[:, g, a:b]).then_inc(s["idx"], 1)
                        pool.wait_ge(s["idx"], 2 * g + (u + 1))
                        pool.sem_inc(s_tick, 1)
                        for j in range(b - a):
                            gather(xx[u][:, j, 0:D], table, idx[u][:, j:j + 1]).then_inc(s["gat"][u], 16)

            def rows_by_group(s, table, cols, indices):
                def group(g, b, h):
                    pool.wait_ge(s["xfree"][b], h + 1)
                    pool.sem_inc(s_tick, 1)
                    if indices is None:
                        pool.wait_ge(s["es"][b], 48 * h + 48)
                        pool.sem_inc(s_tick, 1)
                    at = es[b][:, 0, :] if indices is None else indices[:, g, :]
                    nc.gpsimd.tensor_copy(idx[b][:, :], at).then_inc(s["idx"], 1)
                    pool.wait_ge(s["idx"], g + 1)
                    pool.sem_inc(s_tick, 1)
                    for j in range(TG):
                        gather(xx[b][:, j, 0:cols], table, idx[b][:, j:j + 1]).then_inc(s["gat"][b], 16)
                each_group(pool, group)

            fast = pool.value_load(flag_i[0:1, 0:1], min_val=0, max_val=1)
            with pool.If(fast == 1):
                rows_by_group(so, x, D, None)
                worst(2)
            with pool.Else():
                pool.wait_ge(s_orig[0], 48)
                rows_general(gen[0], x)
            pool.wait_ge(s_flag, 2)
            pool.wait_ge(s_htab, 16)
            fast2 = pool.value_load(flag_i[0:1, 1:2], min_val=0, max_val=1)
            with pool.If(fast2 == 1):
                rows_by_group(fa, h_table, D, src_s)
                pool.wait_ge(s_xtab, 32)
                rows_by_group(sh, x1_table, ROW, src_s)
            with pool.Else():
                pool.wait_ge(s_orig[1], 48)
                rows_general(gen[1], h_table)
                pool.wait_ge(s_xtab, 32)

                def gather_unit(u, g):
                    a, b = UNITS[u]
                    pool.wait_ge(gs["xfree"][u], g + 1)
                    pool.sem_inc(s_tick, 1)
                    nc.gpsimd.tensor_copy(idx_s[u], src_i[:, g, a:a + b - a] if b - a == UMAX else src_i[:, g, a - 1:b]
                                          ).then_inc(gs["idx"], 1)
                    nc.gpsimd.tensor_copy(idx_d[u], dst_i[:, g, a:b] if b - a == UMAX else dst_i[:, g, a - 1:b]
                                          ).then_inc(gs["idx"], 1)
                    pool.wait_ge(gs["idx"], 4 * g + (2 * u + 2))
                    pool.sem_inc(s_tick, 1)
                    o = UMAX - (b - a)
                    for j in range(b - a):
                        gather(xx[u][:, j, 0:ROW], x1_table, idx_s[u][:, o + j:o + j + 1]).then_inc(gs["gat"][u], 16)
                        gather(xx[u][:, j, ROW:2 * ROW], x1_table, idx_d[u][:, o + j:o + j + 1]).then_inc(gs["gat"][u], 16)

                def scatter_unit(u, g):
                    a, b = UNITS[u]
                    pool.wait_ge(gs["ms"], 2 * g + (u + 2))
                    pool.sem_inc(s_tick, 1)
                    pool.wait_ge(gs["idxo"], 2 * g + (u + 1))
                    pool.sem_inc(s_tick, 1)
                    for j in range(b - a):
                        k = j % NT
                        if j >= NT:
                            done = (PER_TABLE[0][k] if u else 0) + j // NT
                            pool.wait_ge(s_table[k], 16 * T_GROUP[k] * g + 16 * done)
                            pool.sem_inc(s_tick, 1)
                        pool.indirect_dma_start(out=sums[k], in_=msum[u][:, j, :], in_offset=None, compute_op=ALU.add,
                                                out_offset=bass.IndirectOffsetOnAxis(ap=idx_o[u][:, j:j + 1], axis=0)
                                                ).then_inc(s_table[k], 16)

                def scattered(u, g):
                    for k in range(NT):
                        done = PER_TABLE[0][k] + (PER_TABLE[1][k] if u else 0)
                        pool.wait_ge(s_table[k], 16 * T_GROUP[k] * g + 16 * done)
                    pool.sem_inc(gs["scat"][u], 1)

                for u in range(2):
                    gather_unit(u, 0)
                with pool.Fori(0, NG - 1) as g:
                    for u in range(2):
                        scatter_unit(u, g)
                        gather_unit(u, g + 1)
                        scattered(u, g)
                for u in range(2):
                    scatter_unit(u, NG - 1)
                    scattered(u, NG - 1)
                pool.sem_inc(s_end, 1)

        @block.vector
        def _(dve):
            V = nc.vector
            ch = Chain(dve, s_vch)
            for t in (agg, big, x_node, w_hid, w_out, xT_c, ones, ones_b, deg):
                ch.do(V.memset(t[:], 1.0 if t in (ones, ones_b, xT_c) else 0.0))
            ch.wait()
            dve.sem_inc(s_zeroed, 1)
            dve.wait_ge(s_iota, 7)
            band = node_buf[0:R, 0:P]
            ch.do(V.tensor_scalar(before[:, :], ident[:, :], 0.0, None, ALU.is_lt))
            ch.do(V.tensor_scalar(after[:, :], ident[:, :], 0.0, None, ALU.is_gt))
            ch.do(V.tensor_scalar(after_b[:, :], ident[:, :], 0.0, None, ALU.is_gt))
            ch.do(V.tensor_scalar(earlier[:, :, :], earlier[:, :, :], 0.0, None, ALU.is_lt))
            ch.do(V.tensor_scalar(band, expand[:, :], float(D), None, ALU.is_lt))
            ch.wait()
            ch.do(V.tensor_scalar(expand[:, :], expand[:, :], 0.0, None, ALU.is_ge))
            dve.wait_ge(s_first, 16)
            ch.do(V.tensor_copy(first_f[0:1, :], first_i[0:1, :]))
            ch.wait()
            ch.do(V.tensor_tensor(expand[:, :], expand[:, :], band, ALU.mult))
            ch.do(V.tensor_scalar(ident[:, :], ident[:, :], 0.0, None, ALU.is_equal))
            ch.wait()
            for s in (gen[0], gen[1], so, fa, gs, sh):
                for t in s["xfree"]:
                    dve.sem_inc(t, 1)
            for s in (s_node, gs["vd"], gs["vfree"], gs["rused"], gs["ms"], *gs["scat"], *so["esfree"],
                      *sh["winfree"], sh["vd"], sh["vfree"], sh["sc"]):
                dve.sem_inc(s, 1)
            dve.sem_inc(s_consts, 1)
            dve.wait_ge(s_row, 1)
            ch.do(V.tensor_copy(base_tab[:, 0:NG], ps_acc[:, 0:NG]))
            dve.wait_ge(s_dst, 16)
            dve.wait_ge(s_loaded, LOADED)
            ch.wait()
            PART = 5
            part = NG // PART * TG
            off = work[:, 0:part]

            def flag(k, greatest, extra=None):
                ch.wait()
                ch.do(V.tensor_reduce(red[:, 0:1], stat[0][:, 0:PART], AX, ALU.max))
                ch.do(V.tensor_reduce(red[:, 1:2], stat[1][:, 0:PART], AX, ALU.max))
                ch.wait()
                dve.sem_inc(s_red, 1)
                dve.wait_ge(s_redall, k + 1)
                ch.do(V.tensor_scalar(flag_f[0:1, 0:1], red_all[0:1, 0:1], float(greatest), None, ALU.is_le))
                ch.do(V.tensor_scalar(flag_f[0:1, 1:2], red_all[0:1, 1:2], 0.0, None, ALU.is_le))
                ch.wait()
                ch.do(V.tensor_tensor(flag_i[0:1, k:k + 1], flag_f[0:1, 0:1], flag_f[0:1, 1:2], ALU.mult))
                ch.restart()
                dve.sem_inc(s_flag, 1)

            for h in range(PART):
                gr = slice(h * NG // PART, (h + 1) * NG // PART)
                ch.do(V.tensor_tensor(off.rearrange("p (g j) -> p g j", j=TG), dst_i[:, gr, :],
                                      base_tab[:, gr].unsqueeze(2).to_broadcast([P, NG // PART, TG]), ALU.subtract))
                ch.wait()
                ch.do(V.tensor_reduce(stat[0][:, h:h + 1], off, AX, ALU.max))
                ch.do(V.tensor_reduce(stat[1][:, h:h + 1], off, AX, ALU.min, negate=True))
                ch.wait()
            flag(0, W - 1)

            def one_hot(o, values, n, width, grid):
                return V.tensor_tensor(o, values.unsqueeze(2).to_broadcast([P, n, width]),
                                       grid.unsqueeze(1).to_broadcast([P, n, width]), ALU.is_equal)

            def by_relation(n, typ, rows, free):
                V.tensor_tensor(typ_x[:, 0:n, :, :], typ_hot[:, 0:n, :].unsqueeze(3).to_broadcast([P, n, R, D]),
                                rows.unsqueeze(2).to_broadcast([P, n, R, D]), ALU.mult).then_inc(free, 1)

            def drain(base, count, s_acc, rows, counts):
                dve.wait_ge(s_acc, count)
                acc = agg[0:rows, bass.ds(base, W)]
                ch.do(V.tensor_tensor(acc, acc, ps_acc[0:rows, 0:W], ALU.add))
                if counts:
                    acc = cnt[:, bass.ds(base, W)]
                    ch.do(V.tensor_tensor(acc, acc, ps_cnt[0:R, 0:W], ALU.add))

            def all_windows(u, g, s, rows, counts):
                a, b = UNITS[u]
                n = b - a
                ch.restart()
                with dve.Fori(0, NW) as w:
                    ch.do(V.tensor_scalar(rel[:, 0:n], dst_i[:, g, a:b], base_tab[:, bass.ds(w + NG, 1)], None,
                                          ALU.subtract))
                    ch.wait()
                    one_hot(dst_hot[:, 0:n, :], rel[:, 0:n], n, W, iota_w[:, :]).then_inc(s["hot"], 1)
                    drain(w * W, g * (2 * NW) + w + (u * NW + 1), s["acc"], rows, counts)
                    ch.restart()

            def relational_general(phase):
                s = gen[phase]
                with dve.Fori(0, NG) as g:
                    for u, (a, b) in enumerate(UNITS):
                        n = b - a
                        ch.do(one_hot(typ_hot[:, 0:n, :], typ_i[:, g, a:b], n, R, iota_r[:, :]))
                        ch.wait()
                        dve.wait_ge(s["gat"][u], g * (16 * n) + 16 * n)
                        by_relation(n, None, xx[u][:, 0:n, 0:D], s["xfree"][u])
                        if phase == 0:
                            ch.do(V.tensor_scalar(lo_u[:, 0:n], src_i[:, g, a:b], P - 1, None, ALU.bitwise_and))
                            ch.do(V.tensor_scalar(hi_u[:, 0:n], src_i[:, g, a:b], 7, None, ALU.logical_shift_right))
                            ch.wait()
                            ch.do(one_hot(lo_hot_u[:, 0:n, :], lo_u[:, 0:n], n, P, iota_w[:, :]))
                            one_hot(blk_hot_u[:, 0:n, :], hi_u[:, 0:n], n, NB, iota_w[:, 0:NB]).then_inc(s["hhot"], 1)
                        all_windows(u, g, s, P, phase == 0)
                        if phase == 0:
                            dve.wait_ge(s["hist"], 2 * g + (u + 1))
                            ch.do(V.tensor_tensor(deg[:, :], deg[:, :], ps_hist[:, 0:NB], ALU.add))
                    ch.restart()

            def relational_and_sort():
                def group(g, b, h):
                    half = h
                    e_src, e_dst, e_typ = (es[b][:, k, :] for k in range(3))
                    dve.wait_ge(so["es"][b], 48 * half + 48)
                    ch.do(V.tensor_scalar(lo_i, e_src, P - 1, None, ALU.bitwise_and))
                    ch.do(V.tensor_scalar(hi_i, e_src, 7, None, ALU.logical_shift_right))
                    ch.do(V.tensor_scalar(fld[:, :, DST], e_dst, base_tab[:, bass.ds(g, 1)], None, ALU.subtract))
                    ch.do(V.tensor_copy(fld[:, :, TYP], e_typ))
                    ch.wait()
                    ch.do(V.tensor_copy(fld[:, :, LO], lo_i))
                    ch.do(V.tensor_copy(fld[:, :, BLK], hi_i))
                    V.tensor_scalar(neg, lo_i, -1.0, None, ALU.mult).then_inc(so["nlo"], 1)
                    one_hot(blk_hot, hi_i, TG, NB, iota_w[:, 0:NB]).then_inc(so["blkhot"], 1)
                    ch.do(V.tensor_tensor(pairs, hi_i.unsqueeze(2).to_broadcast([P, TG, TG]),
                                          hi_i.unsqueeze(1).to_broadcast([P, TG, TG]), ALU.is_equal))
                    ch.wait()
                    ch.do(V.tensor_tensor(pairs, pairs, earlier[:, :, :], ALU.mult))
                    ch.wait()
                    ch.do(V.tensor_reduce(within, pairs, AX, ALU.add))
                    base = dve.value_load(first_i[0:1, bass.ds(g, 1)], min_val=0, max_val=N - 1)

                    def layer(u):
                        a, c = UNITS[u]
                        n = c - a
                        ch.do(one_hot(typ_hot[:, 0:n, :], e_typ[:, a:c], n, R, iota_r[:, :]))
                        ch.wait()
                        dve.wait_ge(so["gat"][b], 16 * TG * half + 16 * TG)
                        by_relation(n, None, xx[b][:, a:c, 0:D], so["part"] if u == 0 else so["xfree"][b])
                        one_hot(dst_hot[:, 0:n, :], fld[:, a:c, DST], n, W, iota_w[:, :]).then_inc(so["hot"], 1)
                        if u:
                            dve.sem_inc(so["esfree"][b], 1)

                    layer(0)
                    ch.wait()
                    dve.wait_ge(so["base"], g + 1)
                    ch.do(V.tensor_tensor(prod, blk_hot, ps_rank[:, 0:NB].unsqueeze(1).to_broadcast([P, TG, NB]), ALU.mult))
                    ch.wait()
                    ch.do(V.tensor_reduce(rank, prod, AX, ALU.add))
                    ch.wait()
                    ch.do(V.tensor_tensor(rk_i, rank, within, ALU.add))
                    ch.wait()
                    ch.do(V.tensor_scalar(lo_i, rk_i, P - 1, None, ALU.bitwise_and))
                    ch.do(V.tensor_scalar(hi_i, rk_i, 7, None, ALU.logical_shift_right))
                    ch.wait()
                    dve.wait_ge(so["lohot"], 2 * g + 1)
                    V.tensor_scalar(neg, lo_i, -1.0, None, ALU.mult).then_inc(so["nrl"], 1)
                    ch.do(V.tensor_tensor(pairs, hi_i.unsqueeze(2).to_broadcast([P, TG, TG]),
                                          iota_w[:, 0:TG].unsqueeze(1).to_broadcast([P, TG, TG]), ALU.is_equal))
                    ch.wait()
                    V.tensor_tensor(x_hot, pairs.unsqueeze(3).to_broadcast([P, TG, TG, 4]),
                                    fld.unsqueeze(2).to_broadcast([P, TG, TG, 4]), ALU.mult).then_inc(so["fld"], 1)
                    drain(base, 2 * g + 1, so["acc"], P, True)
                    layer(1)
                    dve.wait_ge(so["hist"], g + 1)
                    ch.do(V.tensor_tensor(deg[:, :], deg[:, :], ps_hist[:, 0:NB], ALU.add))
                    drain(base, 2 * g + 2, so["acc"], P, True)
                    ch.restart()
                each_group(dve, group)
                dve.wait_ge(so["fldc"], NG)
                blk = fields[:, :, :, BLK]
                ch.do(V.tensor_copy(row_i.rearrange("p (g j) -> p g j", j=TG), fields[0:1, :, :, BLK]))
                ch.do(V.tensor_copy(row_f.rearrange("p (g j) -> p g j", j=TG), fields[0:1, :, :, BLK]))
                ch.do(V.scalar_tensor_tensor(src_s, fields[:, :, :, BLK], float(P), fields[:, :, :, LO], ALU.mult, ALU.add))
                ch.wait()
                dve.sem_inc(so["rows"], 1)
                dve.wait_ge(so["rowsps"], 1)
                for k in range(ROWS):
                    a, b = k * GR, min((k + 1) * GR, NG)
                    ch.do(V.tensor_tensor(blk[:, a:b, :], blk[:, a:b, :],
                                          bank[k][:, 0:(b - a) * TG].rearrange("p (g j) -> p g j", j=TG), ALU.subtract))
                ch.wait()
                all_blk = fields.rearrange("p g j f -> p (g j) f")[:, :, BLK]
                for k in range(PART):
                    part_k = all_blk[:, k * part:(k + 1) * part]
                    ch.do(V.tensor_reduce(stat[0][:, k:k + 1], part_k, AX, ALU.max))
                    ch.do(V.tensor_reduce(stat[1][:, k:k + 1], part_k, AX, ALU.min, negate=True))
                dve.wait_ge(so["blk"], 16)
                flag(1, SPAN - 1)

            def relational_sorted():
                def group(g, b, h):
                    base = dve.value_load(first_i[0:1, bass.ds(g, 1)], min_val=0, max_val=N - 1)
                    for u, (a, c) in enumerate(UNITS):
                        n = c - a
                        ch.do(one_hot(typ_hot[:, 0:n, :], fields[:, g, a:c, TYP], n, R, iota_r[:, :]))
                        ch.wait()
                        dve.wait_ge(fa["gat"][b], 16 * TG * h + 16 * TG)
                        by_relation(n, None, xx[b][:, a:c, 0:D], fa["part"] if u == 0 else fa["xfree"][b])
                        one_hot(dst_hot[:, 0:n, :], fields[:, g, a:c, DST], n, W, iota_w[:, :]).then_inc(fa["hot"], 1)
                        drain(base, 2 * g + (u + 1), fa["acc"], P, False)
                    ch.restart()
                each_group(dve, group)

            def nodes(phase):
                with dve.Fori(0, NC) as i:
                    ch.do(V.tensor_copy(cnt_c, cnt[:, bass.ds(i * CN, CN)]))
                    ch.do(V.tensor_scalar(inv_c, cnt[:, bass.ds(i * CN, CN)], 1.0, None, ALU.max))
                    ch.wait()
                    V.reciprocal(inv_c, inv_c).then_inc(s_inv, 1)
                    dve.wait_ge(s_E, i + (phase * NC + 1))
                    half = CN // 2
                    for h in range(2):
                        last = V.tensor_tensor(agg_c[:, h * half:(h + 1) * half], agg[:, bass.ds(i * CN + h * half, half)],
                                               ps_E[h][:, 0:half], ALU.mult)
                        if h == 0:
                            ch.do(last)
                    last.then_inc(s_aggc, 1)
                    dve.wait_ge(s_node, i + (phase * NC + 2))
                    res = ps_o[:, 0:CB * D].rearrange("p (b d) -> p b d", d=D)
                    o = h_node[:, bass.ds(i * CB, CB), :]
                    if phase == 0:
                        d = deg[:, bass.ds(i * CB, CB)]
                        ch.do(V.tensor_tensor(d, d, ps_o[:, CB * D:CB * D + CB], ALU.add))
                        V.tensor_scalar(o, res, 0.0, None, ALU.max).then_inc(s_hnode, 1)
                    else:
                        ch.do(V.tensor_copy(o, res))
                    ch.restart()

            full = [P, NB, D]

            def wide(s):
                return s[:, :].unsqueeze(2).to_broadcast(full)

            def layer_norm(y, tmp, act_count):
                ch.wait()
                ch.do(V.tensor_reduce(stat[0][:, :], y, AX, ALU.add))
                ch.wait()
                ch.do(V.tensor_scalar(stat[0][:, :], stat[0][:, :], 1.0 / D, None, ALU.mult))
                ch.wait()
                ch.do(V.tensor_tensor(y, y, wide(stat[0]), ALU.subtract))
                ch.wait()
                ch.do(V.tensor_tensor(tmp, y, y, ALU.mult))
                ch.wait()
                ch.do(V.tensor_reduce(stat[1][:, :], tmp, AX, ALU.add))
                ch.wait()
                V.tensor_scalar(stat[1][:, :], stat[1][:, :], 1.0 / D, 1e-5, ALU.mult, ALU.add).then_inc(s_exp, 1)
                dve.wait_ge(s_act, act_count)
                ch.do(V.reciprocal(stat[1][:, :], stat[1][:, :]))
                ch.wait()

            z, y = h_node, x_node[:, :, :]
            tmp = agg[:, 0:NB * D].rearrange("p (b d) -> p b d", d=D)

            def softmax_and_norm():
                ch.do(V.tensor_reduce(stat[0][:, :], z, AX, ALU.max))
                ch.wait()
                ch.do(V.tensor_tensor(z, z, wide(stat[0]), ALU.subtract))
                ch.wait()
                V.tensor_scalar(deg[:, :], deg[:, :], 1e-5, None, ALU.max).then_inc(s_exp, 1)
                dve.wait_ge(s_act, 2)
                ch.do(V.tensor_reduce(stat[0][:, :], tmp, AX, ALU.add))
                ch.do(V.reciprocal(deg[:, :], deg[:, :]))
                ch.wait()
                ch.do(V.tensor_tensor(y, y, z, ALU.add))
                ch.wait()
                V.tensor_scalar(stat[1][:, :], stat[0][:, :], 1.0, None, ALU.mult).then_inc(s_exp, 1)
                dve.wait_ge(s_act, 3)
                ch.do(V.tensor_tensor(y, y, wide(stat[1]), ALU.subtract))
                layer_norm(y, tmp, 4)
                ch.do(V.tensor_tensor(y, y, wide(stat[1]), ALU.mult))
                ch.wait()
                ch.do(V.memset(agg[0:D, :], 0.0))
                ch.restart()
                dve.sem_inc(s_ztab, 1)

            def reflections(n, v, xu, mu, t1, t2, t3, small, q):
                n2, c, pv, rv, av, bv = (t[:, 0:n] for t in small)
                both = [P, n, 2, D]
                ch.do(V.tensor_tensor(t1, v, v, ALU.mult))
                ch.do(V.tensor_tensor(t2, v, xu, ALU.mult))
                ch.do(V.tensor_tensor(t3, v[:, :, 0, :], v[:, :, 1, :], ALU.mult))
                ch.wait(2)
                ch.do(V.tensor_reduce(n2, t1, AX, ALU.add))
                ch.wait(2)
                ch.do(V.tensor_reduce(pv, t2, AX, ALU.add))
                ch.wait(2)
                ch.do(V.tensor_reduce(q, t3, AX, ALU.add))
                for s in range(2):
                    ch.wait(1)
                    ch.do(V.tensor_tensor(t1[:, :, s, :], v[:, :, s, :], xu[:, :, 1 - s, :], ALU.mult))
                ch.do(V.tensor_scalar(c, n2, 1e-24, 0.5, ALU.max, ALU.mult))
                ch.wait(1)
                ch.do(V.tensor_reduce(rv, t1, AX, ALU.add))
                ch.wait(1)
                ch.do(V.reciprocal(c, c))
                ch.wait()
                ch.do(V.tensor_tensor(av, c, pv, ALU.mult))
                ch.wait()
                ch.do(V.tensor_tensor(t2, v, av.unsqueeze(3).to_broadcast(both), ALU.mult))
                for s in range(2):
                    ch.do(V.tensor_tensor(bv[:, :, s], av[:, :, 1 - s], q, ALU.mult))
                ch.wait()
                ch.do(V.tensor_tensor(bv, rv, bv, ALU.subtract))
                ch.do(V.tensor_tensor(mu[:, :, 0, :], xu[:, :, 1, :], t2[:, :, 1, :], ALU.subtract))
                ch.wait(1)
                ch.do(V.tensor_tensor(bv, bv, c, ALU.mult))
                ch.do(V.tensor_tensor(mu[:, :, 1, :], xu[:, :, 0, :], t2[:, :, 0, :], ALU.subtract))
                ch.wait(1)
                ch.do(V.tensor_tensor(t1, v, bv.unsqueeze(3).to_broadcast(both), ALU.mult))
                ch.wait()
                ch.do(V.tensor_tensor(mu, mu, t1, ALU.subtract))

            def sheaf_general():
                with dve.Fori(0, NG) as g:
                    done = 0
                    for u, (a, b) in enumerate(UNITS):
                        sheaf_unit(u, a, b - a, g, done)
                        done += len(CHUNKS[u])
                    ch.restart()
                dve.sem_inc(s_free, 1)
                dve.wait_ge(s_sums, 16 * NT)
                for k in range(1, NT):
                    ch.do(V.tensor_tensor(tab[0], tab[0], tab[k], ALU.add))
                    ch.wait()
                ch.do(V.tensor_copy(z, tab[0].rearrange("p (b d) -> p b d", d=D)))
                ch.restart()

            def sheaf_unit(u, a, n, g, done):
                ch.do(V.tensor_copy(srcf[:, 0:n], src_i[:, g, a:a + n]))
                ch.wait()
                dve.sem_inc(gs["same"], 1)
                for c, (ca, cb) in enumerate(CHUNKS[u]):
                    m = cb - ca
                    dve.wait_ge(gs["rr"], NCH * g + (done + c + 1))
                    V.tensor_tensor(same[:, ca:cb, :], srcf[:, ca:cb].unsqueeze(2).to_broadcast([P, m, P]),
                                    ps_r[:, 0:m * P].rearrange("p (a e) -> p a e", e=P), ALU.is_equal).then_inc(gs["rused"], 1)
                dve.wait_ge(gs["rused"], NCH * g + (done + len(CHUNKS[u]) + 1))
                ch.do(V.tensor_tensor(same_b[:, 0:n, :], same[:, 0:n, :],
                                      before[:, :].unsqueeze(1).to_broadcast([P, n, P]), ALU.mult))
                ch.wait()
                ch.do(V.tensor_reduce(nbef[:, 0:n], same_b[:, 0:n, :], AX, ALU.add))
                ch.do(V.tensor_scalar(fidx[:, 0:n], srcf[:, 0:n], dump[:, 0:1], None, ALU.subtract))
                ch.wait()
                ch.do(V.tensor_scalar(nbef[:, 0:n], nbef[:, 0:n], 0.0, None, ALU.is_equal))
                ch.wait()
                ch.do(V.tensor_tensor(fidx[:, 0:n], fidx[:, 0:n], nbef[:, 0:n], ALU.mult))
                ch.wait()
                dve.wait_ge(gs["scat"][u], g + 1)
                V.tensor_scalar(idx_o[u][:, 0:n], fidx[:, 0:n], dump[:, 0:1], None, ALU.add).then_inc(gs["idxo"], 1)
                dve.wait_ge(gs["vd"], NCH * g + (done + len(CHUNKS[u]) + 1))
                v, xu, mu = g_vv[:, 0:n], g_xw[:, 0:n], g_msg[u][:, 0:n]
                xs = xx[u][:, 0:n, :].rearrange("p n (s r) -> p n s r", s=2)
                V.tensor_tensor(v.rearrange("p n s d -> p n (s d)"),
                                ps_v[:, 0:n * 2 * D].rearrange("p (n d) -> p n d", d=2 * D),
                                b_out[:, :].unsqueeze(1).to_broadcast([P, n, 2 * D]), ALU.add).then_inc(gs["vfree"], 1)
                dve.wait_ge(gs["gat"][u], g * (32 * n) + 32 * n)
                V.tensor_tensor(xu, xs[:, :, :, 0:D], xs[:, :, :, D:ROW].to_broadcast([P, n, 2, D]),
                                ALU.mult).then_inc(gs["xfree"][u], 1)
                dve.wait_ge(gs["xfree"][u], g + 2)
                reflections(n, v, xu, mu, g_m1[:, 0:n], g_m2[:, 0:n], g_m3[:, 0:n], g_small, g_qv[:, 0:n])
                ch.wait()
                dve.sem_inc(gs["msg"], 1)
                all_windows(u, g, gs, D, False)

            def sheaf_sorted():
                ch.do(V.memset(wide_node[:, :, :], 0.0))
                ch.do(V.memset(acc_odd, 0.0))
                ch.wait()

                def front(g, b, h):
                    ch.do(V.tensor_scalar(f_neg[b], fields[:, g, :, LO], -1.0, None, ALU.mult))
                    ch.do(one_hot(blk7[b], fields[:, g, :, BLK], TG, SPAN, iota_w[:, 0:SPAN]))
                    one_hot(hot[b], fields[:, g, :, DST], TG, W, iota_w[:, :]).then_inc(sh["hot"], 1)

                def back(g, b, h):
                    _, regs = nc.values_load_multi_w_load_instructions(
                        block_table[bass.ds(g, 1), 0:TG], engines=[mybir.EngineType.DVE], min_val=0, max_val=NB - 1,
                        skip_runtime_bounds_check_because="a node's number shifted right by 7 is below NB")
                    base = dve.value_load(first_i[0:1, bass.ds(g, 1)], min_val=0, max_val=N - 1)
                    dve.wait_ge(sh["vd"], NQ * g + (NQ + 1))
                    v2 = f_vv.rearrange("p n s d -> p n (s d)")
                    for k, (a, c) in enumerate(((0, VSPLIT), (VSPLIT, TG))):
                        n = c - a
                        ch.do(V.tensor_tensor(v2[:, a:c, :], ps_vv[k][:, 0:n * 2 * D].rearrange("p (n d) -> p n d", d=2 * D),
                                              b_out[:, :].unsqueeze(1).to_broadcast([P, n, 2 * D]), ALU.add))
                    xs = xx[b][:, :, :].rearrange("p n (s r) -> p n s r", s=2)
                    ch.do(V.tensor_tensor(f_xw, xs[:, :, :, 0:D], xs[:, :, :, D:ROW].to_broadcast([P, TG, 2, D]), ALU.mult))
                    ch.wait()
                    dve.sem_inc(sh["vfree"], 1)
                    dve.sem_inc(sh["xfree"][b], 1)
                    reflections(TG, f_vv, f_xw, f_msg, f_m1, f_m2, f_m3, f_small, f_qv)
                    ch.wait()
                    dve.sem_inc(sh["msg"], 1)
                    V.tensor_tensor(msg_blk, blk7[b].unsqueeze(3).to_broadcast([P, TG, SPAN, D]),
                                    f_msg[:, :, 0, :].unsqueeze(2).to_broadcast([P, TG, SPAN, D]),
                                    ALU.mult).then_inc(sh["msgblk"], 1)
                    drain(base, g + 1, sh["acc"], D, False)
                    for q, (a, c) in enumerate(QUADS):
                        dve.wait_ge(sh["sc"], NQ * g + (q + 2))
                        for j in range(a, c):
                            acc = acc_src[j % 2].rearrange("p b d -> p (b d)") if j % 2 else \
                                wide_node[:, :, :].rearrange("p b d -> p (b d)")
                            acc = acc[:, bass.ds(regs[j] * D, SPAN * D)]
                            ch.wait(1)
                            last = V.tensor_tensor(acc, acc, ps_h[q % 2][:, (j - a) * SPAN * D:(j - a + 1) * SPAN * D], ALU.add)
                            ch.do(last)
                        ch.wait()
                        dve.sem_inc(sh["drained"], 1)
                    ch.restart()

                front(0, 0, 0)
                ch.restart()

                def turn(g, b, h):
                    front(g + 1, 1 - b, h + b)
                    back(g, b, h)
                each_group(dve, turn, NG - 1)
                back(NG - 1, 0, NG // 2)
                ch.do(V.tensor_tensor(wide_node[:, :, :], wide_node[:, :, :], acc_odd, ALU.add))
                ch.restart()

            fast = dve.value_load(flag_i[0:1, 0:1], min_val=0, max_val=1)
            with dve.If(fast == 1):
                relational_and_sort()
            with dve.Else():
                dve.wait_ge(s_orig[0], 48)
                ch.do(V.memset(flag_i[0:1, 1:2], 0))
                ch.restart()
                relational_general(0)
                dve.sem_inc(s_flag, 1)
            dve.sem_inc(s_nodes, 1)
            nodes(0)
            dve.wait_ge(s_htab, 16)
            ch.do(V.memset(agg[:, :], 0.0))
            ch.restart()
            fast2 = dve.value_load(flag_i[0:1, 1:2], min_val=0, max_val=1)
            with dve.If(fast2 == 1):
                relational_sorted()
            with dve.Else():
                dve.wait_ge(s_orig[1], 48)
                relational_general(1)
            dve.sem_inc(s_nodes, 1)
            nodes(1)
            softmax_and_norm()
            with dve.If(fast2 == 1):
                sheaf_sorted()
            with dve.Else():
                sheaf_general()
            with dve.Fori(0, NC) as i:
                V.tensor_copy(agg_c[0:D, :], agg[0:D, bass.ds(i * CN, CN)]).then_inc(s_aggc, 1)
                dve.wait_ge(s_node, i + (2 * NC + 2))
                o = h_node[:, bass.ds(i * CB, CB), :]
                ch.do(V.tensor_tensor(o, o, ps_o[:, 0:CB * D].rearrange("p (b d) -> p b d", d=D), ALU.add))
                ch.restart()
            ch.do(V.tensor_tensor(z, z, wide(deg), ALU.mult))
            ch.wait()
            ch.do(V.tensor_tensor(z, z, y, ALU.add))
            ch.wait()
            ch.do(V.tensor_scalar(z, z, 0.0, None, ALU.max))
            ch.wait()
            ch.do(V.tensor_tensor(y, y, z, ALU.add))
            layer_norm(y, tmp, 5)
            V.tensor_tensor(y, y, wide(stat[1]), ALU.mult).then_inc(s_out, 1)

        @block.scalar
        def _(act):
            A = nc.scalar
            ch = Chain(act, s_ach)

            def one_hot(o, negated, done):
                for j in range(TG):
                    ch.do(A.activation(o[:, j, :], iota_w[:, :], ACT.Square, bias=negated[:, j:j + 1]))
                ch.wait()
                A.activation(o, o, ACT.Relu, bias=1.0, scale=-1.0).then_inc(done, 1)

            act.wait_ge(s_consts, 1)
            act.wait_ge(s_loaded, LOADED)
            act.wait_ge(s_flag, 1)
            fast = act.value_load(flag_i[0:1, 0:1], min_val=0, max_val=1)
            with act.If(fast == 1):
                def group(g, b, h):
                    act.wait_ge(so["tot"], g + 1)
                    A.copy(tot_T, ps_tot[0:NB, 0:P]).then_inc(so["totc"], 1)
                    act.wait_ge(so["nlo"], g + 1)
                    act.sem_inc(s_tick, 1)
                    one_hot(lo_hot, neg, so["lohot"])
                    act.wait_ge(so["hist"], g + 1)
                    act.sem_inc(s_tick, 1)
                    act.wait_ge(so["nrl"], g + 1)
                    act.sem_inc(s_tick, 1)
                    one_hot(lo_hot, neg, so["lohot"])
                    act.wait_ge(so["fldps"], g + 1)
                    act.sem_inc(s_tick, 1)
                    ch.restart()
                    A.copy(fields[:, g, :, :], ps_fld[:, 0:TG * 4].rearrange("p (j f) -> p j f", f=4)).then_inc(so["fldc"], 1)
                each_group(act, group)
            with act.Else():
                act.sem_inc(s_tick, 1)
            for phase in range(2):
                node = (x_node, wide_node)[phase]
                act.wait_ge(s_nodes, phase + 1)
                if phase == 1:
                    act.wait_ge(s_hnode, NC)
                with act.Fori(0, NC) as i:
                    A.copy(xs_c[:, :, :], node[:, bass.ds(i * CB, CB), :]).then_inc(s_xsc, 1)
                    act.wait_ge(s_xTp, i + (phase * NC + 1))
                    act.sem_inc(s_tick, 1)
                    act.wait_ge(s_node, i + (phase * NC + 1))
                    A.copy(xT_c[0:D, 0:4 * P], ps_xT[0][0:D, :])
                    A.copy(xT_c[0:D, 4 * P:CN], ps_xT[1][0:D, 0:CN - 4 * P]).then_inc(s_xTc, 1)
            tmp = agg[:, 0:NB * D].rearrange("p (b d) -> p b d", d=D)
            act.wait_ge(s_exp, 1)
            A.activation(tmp, h_node, ACT.Exp).then_inc(s_act, 1)
            A.activation(deg[:, :], deg[:, :], ACT.Sqrt).then_inc(s_act, 1)
            act.wait_ge(s_exp, 2)
            A.activation(stat[1][:, :], stat[1][:, :], ACT.Ln).then_inc(s_act, 1)
            act.wait_ge(s_exp, 3)
            A.activation(stat[1][:, :], stat[1][:, :], ACT.Sqrt).then_inc(s_act, 1)
            act.wait_ge(s_ztab, 1)
            fast2 = act.value_load(flag_i[0:1, 1:2], min_val=0, max_val=1)
            with act.If(fast2 == 1):
                def front(g, b, h):
                    for q, (a, c) in enumerate(QUADS):
                        m = (c - a) * P
                        act.wait_ge(sh["tr"], NQ * g + (q + 1))
                        A.copy(f_dT[q % 2][:, 0:m], ps_t[q % 2][:, 0:m]).then_inc(sh["dt"], 1)
                    act.wait_ge(sh["xd"], g + 1)
                    A.copy(xx[b][:, :, ROW:2 * ROW], ps_x[:, 0:TG * ROW].rearrange("p (n r) -> p n r", r=ROW)).then_inc(sh["xdc"], 1)
                    for s in range(NQ + 1):
                        if s < NQ:
                            m = (QUADS[s][1] - QUADS[s][0]) * P
                            act.wait_ge(sh["ttr"], NQ * g + (s + 1))
                            A.copy(f_xT[s % 2][0:2 * ROW, 0:m], ps_t[s % 2][0:2 * ROW, 0:m]).then_inc(sh["xt"], 1)
                        if s > 0:
                            c = s - 1
                            m = (QUADS[c][1] - QUADS[c][0]) * P
                            act.wait_ge(sh["hp"], NQ * g + (c + 1))
                            act.sem_inc(s_tick, 1)
                            act.wait_ge(sh["vd"], NQ * g + (max(c - 1, 0) + 1))
                            A.activation(f_hid[c % 2][:, 0:m], ps_h[c % 2][:, 0:m], ACT.Relu,
                                         bias=b_hid[:, 0:1]).then_inc(sh["hs"], 1)

                def back(g, b, h):
                    act.wait_ge(sh["hot"], g + 1)
                    act.sem_inc(s_tick, 1)
                    act.wait_ge(sh["sc"], NQ * g + 1)
                    act.sem_inc(s_tick, 1)
                    one_hot(src_hot, f_neg[b], sh["srchot"])
                    ch.restart()

                front(0, 0, 0)

                def turn(g, b, h):
                    back(g, b, h)
                    front(g + 1, 1 - b, h + b)
                each_group(act, turn, NG - 1)
                back(NG - 1, 0, NG // 2)
            with act.Else():
                with act.Fori(0, NG) as g:
                    done = 0
                    for u, (a, b) in enumerate(UNITS):
                        nch = len(CHUNKS[u])
                        for s in range(nch + 1):
                            if s < nch:
                                m = (CHUNKS[u][s][1] - CHUNKS[u][s][0]) * P
                                act.wait_ge(gs["tr"], NCH * g + (done + s + 1))
                                A.copy(g_xT[s % 2][0:2 * ROW, 0:m], ps_t[s % 2][0:2 * ROW, 0:m]).then_inc(gs["xt"], 1)
                            if s > 0:
                                c = s - 1
                                m = (CHUNKS[u][c][1] - CHUNKS[u][c][0]) * P
                                act.wait_ge(gs["hp"], NCH * g + (done + c + 1))
                                act.sem_inc(s_tick, 1)
                                act.wait_ge(gs["vd"], NCH * g + (done + max(c - 1, 0) + 1))
                                A.activation(g_hid[c % 2][:, 0:m], ps_h[c % 2][:, 0:m], ACT.Relu,
                                             bias=b_hid[:, 0:1]).then_inc(gs["hs"], 1)
                        act.wait_ge(gs["scat"][u], g + 1)
                        act.sem_inc(s_tick, 1)
                        act.wait_ge(gs["sp"], 2 * g + (u + 1))
                        A.copy(msum[u][:, 0:b - a, :],
                               ps_s[:, 0:(b - a) * D].rearrange("p (n d) -> p n d", d=D)).then_inc(gs["ms"], 1)
                        done += nch
            act.wait_ge(s_exp, 4)
            A.activation(stat[1][:, :], stat[1][:, :], ACT.Sqrt).then_inc(s_act, 1)

        @block.tensor
        def _(pe):
            mm = nc.tensor.matmul

            def wait(s, value):
                pe.wait_ge(s, value)
                pe.sem_inc(s_tick, 1)

            pe.wait_ge(s_consts, 1)
            mm(ps_acc[:, 0:NG], ones[0:1, :], first_f[0:1, :], start=True, stop=True).then_inc(s_row, 1)
            pe.wait_ge(s_flag, 1)
            pe.wait_ge(s_loaded, LOADED)

            def sums_by_relation(n, counts, s_acc):
                if counts:
                    for j in range(n):
                        mm(ps_cnt[0:R, 0:W], typ_hot[:, j, :], dst_hot[:, j, :], start=j == 0, stop=j == n - 1)
                for j in range(n):
                    last = mm(ps_acc[:, 0:W], typ_x[:, j, :, :].rearrange("p r d -> p (r d)"),
                              dst_hot[:, j, :], start=j == 0, stop=j == n - 1)
                last.then_inc(s_acc, 1)

            def relational_general(phase):
                s = gen[phase]
                with pe.Fori(0, NG) as g:
                    for u, (a, b) in enumerate(UNITS):
                        n = b - a
                        if phase == 0:
                            wait(s["hhot"], 2 * g + (u + 1))
                            for j in range(n):
                                last = mm(ps_hist[:, 0:NB], lo_hot_u[:, j, :], blk_hot_u[:, j, :], start=j == 0, stop=j == n - 1)
                            last.then_inc(s["hist"], 1)
                        with pe.Fori(0, NW) as w:
                            wait(s["hot"], g * (2 * NW) + w + (u * NW + 1))
                            sums_by_relation(n, phase == 0, s["acc"])

            def relational_and_sort():
                def group(g, b, h):
                    def layer(u):
                        wait(so["hot"], 2 * g + (u + 1))
                        sums_by_relation(UNITS[u][1] - UNITS[u][0], True, so["acc"])

                    wait(so["blkhot"], g + 1)
                    for j in range(TG):
                        last = mm(ps_tot[0:NB, 0:P], blk_hot[:, j, :], ones_b[:, :], start=j == 0, stop=j == TG - 1)
                    last.then_inc(so["tot"], 1)
                    for j in range(TG):
                        mm(ps_rank[:, 0:NB], after_b[:, :], blk_hot[:, j, :], start=j == 0, stop=False)
                    wait(so["totc"], g + 1)
                    mm(ps_rank[:, 0:NB], tot_T, after[0:NB, 0:NB], start=False, stop=True).then_inc(so["base"], 1)
                    layer(0)
                    wait(so["lohot"], 2 * g + 1)
                    for j in range(TG):
                        last = mm(ps_hist[:, 0:NB], lo_hot[:, j, :], blk_hot[:, j, :], start=j == 0, stop=j == TG - 1)
                    last.then_inc(so["hist"], 1)
                    wait(so["fld"], g + 1)
                    wait(so["lohot"], 2 * g + 2)
                    for j in range(TG):
                        last = mm(ps_fld[:, 0:TG * 4], lo_hot[:, j, :], x_hot[:, j, :, :].rearrange("p r f -> p (r f)"),
                                  start=j == 0, stop=j == TG - 1)
                    last.then_inc(so["fldps"], 1)
                    layer(1)
                each_group(pe, group)
                wait(so["rows"], 1)
                for k in range(ROWS):
                    a, b = k * GR * TG, min((k + 1) * GR, NG) * TG
                    last = mm(bank[k][:, 0:b - a], ones[0:1, :], row_f[0:1, a:b], start=True, stop=True)
                last.then_inc(so["rowsps"], 1)

            def relational_sorted():
                with pe.Fori(0, NG) as g:
                    for u, (a, c) in enumerate(UNITS):
                        wait(fa["hot"], 2 * g + (u + 1))
                        sums_by_relation(c - a, False, fa["acc"])

            def nodes(phase):
                with pe.Fori(0, NC) as i:
                    wait(s_xsc, i + (phase * NC + 1))
                    for b in range(CB):
                        last = nc.tensor.transpose(ps_xT[b // 4][0:D, (b % 4) * P:(b % 4 + 1) * P], xs_c[:, b, :], ident[:, :])
                    last.then_inc(s_xTp, 1)
                    wait(s_inv, i + (phase * NC + 1))
                    for h in range(2):
                        last = mm(ps_E[h][:, 0:CN // 2], expand[:, :], inv_c[:, h * CN // 2:(h + 1) * CN // 2],
                                  start=True, stop=True)
                    last.then_inc(s_E, 1)
                    wait(s_aggc, i + (phase * NC + 1))
                    wait(s_xTc, i + (phase * NC + 1))
                    for b in range(CB):
                        o = ps_o[:, b * D:(b + 1) * D]
                        mm(o, agg_c[:, b * P:(b + 1) * P], wrel[phase][:, :], start=True, stop=False)
                        last = mm(o, xT_c[:, b * P:(b + 1) * P], root[phase][:, :], start=False, stop=True)
                        if phase == 0:
                            last = mm(ps_o[:, CB * D + b:CB * D + b + 1], cnt_c[:, b * P:(b + 1) * P], ones[0:R, 0:1],
                                      start=True, stop=True)
                    last.then_inc(s_node, 1)

            def hidden_layers(tiles, s, rows, xT, hid, at, n0, n_all, v_at, v_wait):
                nch = len(tiles)
                for k in range(nch + 2):
                    if k < nch:
                        ca, cb = tiles[k]
                        for j in range(ca, cb):
                            last = nc.tensor.transpose(ps_t[k % 2][0:2 * ROW, (j - ca) * P:(j - ca + 1) * P],
                                                       rows[:, j, :], ident[:, :])
                        last.then_inc(s[at], 1)
                    if 0 < k <= nch:
                        c = k - 1
                        m = (tiles[c][1] - tiles[c][0]) * P
                        wait(s["xt"], n_all + (n0 + c + 1))
                        mm(ps_h[c % 2][:, 0:m], w_hid[:, :], xT[c % 2][0:2 * ROW, 0:m],
                           start=True, stop=True).then_inc(s["hp"], 1)
                    if k > 1:
                        c = k - 2
                        ca, cb = tiles[c]
                        wait(s["hs"], n_all + (n0 + c + 1))
                        if c == 0:
                            wait(s["vfree"], v_wait)
                        for j in range(ca, cb):
                            last = mm(v_at(j), hid[c % 2][:, (j - ca) * P:(j - ca + 1) * P], w_out[:, :], start=True, stop=True)
                        last.then_inc(s["vd"], 1)

            def sheaf_general():
                with pe.Fori(0, NG) as g:
                    done = 0
                    for u, (a, b) in enumerate(UNITS):
                        n = b - a
                        wait(gs["same"], 2 * g + (u + 1))
                        for c, (ca, cb) in enumerate(CHUNKS[u]):
                            wait(gs["rused"], NCH * g + (done + c + 1))
                            for j in range(ca, cb):
                                last = mm(ps_r[:, (j - ca) * P:(j - ca + 1) * P], srcf[:, j:j + 1].to_broadcast([P, P]),
                                          ident[:, :], start=True, stop=True)
                            last.then_inc(gs["rr"], 1)
                        wait(gs["gat"][u], g * (32 * n) + 32 * n)
                        hidden_layers(CHUNKS[u], gs, xx[u], g_xT, g_hid, "tr", done, NCH * g,
                                      lambda j: ps_v[:, j * 2 * D:(j + 1) * 2 * D], 2 * g + (u + 1))
                        wait(gs["msg"], 2 * g + (u + 1))
                        wait(gs["ms"], 2 * g + (u + 1))
                        for j in range(n):
                            last = mm(ps_s[:, j * D:(j + 1) * D], same[:, j, :], g_msg[u][:, j, 0, :], start=True, stop=True)
                        last.then_inc(gs["sp"], 1)
                        with pe.Fori(0, NW) as w:
                            wait(gs["hot"], g * (2 * NW) + w + (u * NW + 1))
                            for j in range(n):
                                last = mm(ps_acc[0:D, 0:W], g_msg[u][:, j, 1, :], dst_hot[:, j, :], start=j == 0, stop=j == n - 1)
                            last.then_inc(gs["acc"], 1)
                        done += len(CHUNKS[u])

            def sheaf_sorted():
                def front(g, b, h):
                    wait(sh["hot"], g + 1)
                    wait(sh["win"][b], 16 * h + 16)
                    for q in range(NQ + 1):
                        if q < NQ:
                            a, c = QUADS[q]
                            for j in range(a, c):
                                last = nc.tensor.transpose(ps_t[q % 2][:, (j - a) * P:(j - a + 1) * P], hot[b][:, j, :], ident[:, :])
                            last.then_inc(sh["tr"], 1)
                        if q:
                            a, c = QUADS[q - 1]
                            wait(sh["dt"], NQ * g + q)
                            for j in range(a, c):
                                last = mm(ps_x[:, j * ROW:(j + 1) * ROW], f_dT[(q - 1) % 2][:, (j - a) * P:(j - a + 1) * P],
                                          xwin[b], start=True, stop=True)
                    last.then_inc(sh["xd"], 1)
                    wait(sh["gat"][b], 16 * TG * h + 16 * TG)
                    wait(sh["xdc"], g + 1)
                    pe.sem_inc(sh["winfree"][b], 1)
                    hidden_layers(QUADS, sh, xx[b], f_xT, f_hid, "ttr", 0, NQ * g,
                                  lambda j: ps_vv[j // VSPLIT][:, (j % VSPLIT) * 2 * D:(j % VSPLIT + 1) * 2 * D], g + 1)

                def back(g, b, h):
                    wait(sh["msg"], g + 1)
                    for j in range(TG):
                        last = mm(ps_acc[0:D, 0:W], f_msg[:, j, 1, :], hot[b][:, j, :], start=j == 0, stop=j == TG - 1)
                    last.then_inc(sh["acc"], 1)
                    wait(sh["msgblk"], g + 1)
                    wait(sh["srchot"], g + 1)
                    for q, (a, c) in enumerate(QUADS):
                        if q > 1:
                            wait(sh["drained"], NQ * g + (q - 1))
                        for j in range(a, c):
                            last = mm(ps_h[q % 2][:, (j - a) * SPAN * D:(j - a + 1) * SPAN * D], src_hot[:, j, :],
                                      msg_blk[:, j, :, :].rearrange("p s d -> p (s d)"), start=True, stop=True)
                        last.then_inc(sh["sc"], 1)
                    wait(sh["drained"], NQ * g + NQ)

                front(0, 0, 0)

                def turn(g, b, h):
                    front(g + 1, 1 - b, h + b)
                    back(g, b, h)
                each_group(pe, turn, NG - 1)
                back(NG - 1, 0, NG // 2)

            fast = pe.value_load(flag_i[0:1, 0:1], min_val=0, max_val=1)
            with pe.If(fast == 1):
                relational_and_sort()
            with pe.Else():
                relational_general(0)
            wait(s_nodes, 1)
            nodes(0)
            wait(s_flag, 2)
            fast2 = pe.value_load(flag_i[0:1, 1:2], min_val=0, max_val=1)
            with pe.If(fast2 == 1):
                relational_sorted()
            with pe.Else():
                relational_general(1)
            wait(s_nodes, 2)
            nodes(1)
            with pe.If(fast2 == 1):
                sheaf_sorted()
            with pe.Else():
                sheaf_general()
            with pe.Fori(0, NC) as i:
                wait(s_aggc, i + (2 * NC + 1))
                for b in range(CB):
                    last = nc.tensor.transpose(ps_o[:, b * D:(b + 1) * D], agg_c[0:D, b * P:(b + 1) * P], ident[0:D, 0:D])
                last.then_inc(s_node, 1)



_INS = ['x', 'src', 'dst', 'edge_type_8', 'L0_gnn_W1', 'L0_gnn_root1', 'L0_gnn_b1', 'L0_gnn_W2', 'L0_gnn_root2', 'L0_gnn_b2', 'L1_gnn_W1', 'L1_gnn_b1', 'L1_gnn_W2', 'L1_gnn_b2']


def kernel(**inputs):
    import numpy as _np
    import concourse.bacc as _bacc
    from concourse import mybir as _mybir
    from concourse.bass_utils import run_bass_kernel_spmd as _run

    nc = _bacc.Bacc("TRN2", target_bir_lowering=False, num_devices=1)
    arrays, args = {}, []
    for name in _INS:
        a = _np.ascontiguousarray(inputs[name])
        arrays[f"in_{name}"] = a
        args.append(nc.dram_tensor(f"in_{name}", a.shape, _mybir.dt.from_np(a.dtype), kind="ExternalInput").ap())
    args.append(nc.dram_tensor("out", (12500, 16), _mybir.dt.float32, kind="ExternalOutput").ap())
    build(nc, *args)
    r = _run(nc, [arrays], core_ids=[0])
    return r.results[0]["out"]
```

```python
import numpy as np
import concourse.bass as bass
from concourse import mybir
from contextlib import ExitStack

P = 128
N, D, R, E = 12500, 16, 8, 400000
TG = 25
GE = P * TG
NG = E // GE
UNITS = [(0, 13), (13, 25)]
UMAX, UMIN = 13, 12
DQ = UMIN // 4
W = 128
NB = -(-N // P)
NP = NB * P
NW = NP // W
NACC = NP + W
CB = 7
CN = CB * P
NC = NB // CB
HID = 64
ROW = D + 1
XS = 2 * D
XY = XS + D
XROW = XY + 3 * D // 2
NT = 5
TROWS = NP + P
CHUNKS = [[(0, 4), (4, 8), (8, 12), (12, 13)], [(0, 4), (4, 8), (8, 12)]]
NCH = sum(len(c) for c in CHUNKS)
SPAN = 7
NBS = NB + SPAN - 1
CUTS = [0, 4, 7, 11, 14, 18, 21, TG]
SUMMED = list(zip(CUTS, CUTS[1:]))
QUADS = [(j, min(j + 4, TG)) for j in range(0, TG, 4)]
NQ = len(QUADS)
VSPLIT = 16
PER_TABLE = [[len(range(k, b - a, NT)) for k in range(NT)] for a, b in UNITS]
T_GROUP = [sum(p[k] for p in PER_TABLE) for k in range(NT)]
GR = 500 // TG
ROWS = -(-NG // GR)
assert GE * NG == E and NC * CB == NB and NG % 2 == 1


class Chain:

    def __init__(self, eng, sem):
        self.eng, self.sem, self.n = eng, sem, 0

    def do(self, ins):
        ins.then_inc(self.sem, 1)
        self.n += 1

    def wait(self, but=0):
        if self.n > but:
            self.eng.wait_ge(self.sem, self.n - but)

    def restart(self):
        if self.n:
            self.wait()
            self.eng.sem_clear(self.sem)
            self.n = 0


def each_group(eng, body, last=NG):
    with eng.Fori(0, last // 2) as h:
        for b in range(2):
            body(h * 2 + b, b, h)
    if last % 2:
        body(last - 1, 0, last // 2)


def build(nc, x, src, dst, et, l0w1, l0r1, l0b1, l0w2, l0r2, l0b2, l1w1, l1b1, l1w2, l1b2, out):
    f32, i32, bf16 = mybir.dt.float32, mybir.dt.int32, mybir.dt.bfloat16
    ALU, ACT = mybir.AluOpType, mybir.ActivationFunctionType
    AX = mybir.AxisListType.X
    RMAX = bass.bass_isa.ReduceOp.max
    ctx = ExitStack()
    with ctx:
        def sb(name, shape, dt=f32):
            return ctx.enter_context(nc.sbuf_tensor(name, shape, dt))

        def sem(name):
            return ctx.enter_context(nc.semaphore(name))

        def sems(tag, names, pairs=""):
            s = {n: sem(f"{tag}_{n}") for n in names.split()}
            s.update({n: [sem(f"{tag}_{n}{k}") for k in range(2)] for n in pairs.split()})
            return s

        def carver(t):
            at = [0]

            def carve(*shape, dt=f32):
                size = int(np.prod(shape))
                words = size if dt != bf16 else -(-size // 2)
                v = t[:, at[0]:at[0] + words]
                at[0] += words
                assert at[0] <= t.shape[1], (at, t.shape)
                if dt != f32:
                    v = v.bitcast(dt)[:, 0:size]
                if len(shape) == 1:
                    return v
                names = "abcd"[:len(shape)]
                return v.rearrange(f"p ({' '.join(names)}) -> p {' '.join(names)}", **dict(zip(names, shape)))
            return carve

        h_table = nc.dram_tensor("h_table", [NP, D], f32).ap()
        x1_table = nc.dram_tensor("x1_table", [NP, XY], f32).ap()
        win_table = nc.dram_tensor("win_table", [TROWS, XROW], f32).ap()
        x1_plain = nc.dram_tensor("x1_plain", [NP, ROW], f32).ap()
        sums = [nc.dram_tensor(f"sums{k}", [TROWS, D], f32).ap() for k in range(NT)]
        block_table = nc.dram_tensor("block_table", [NG, 32], i32).ap()

        edges = sb("edges", [P, 3 * NG * TG])
        src_i, dst_i, typ_i = (edges[:, k * NG * TG:(k + 1) * NG * TG].bitcast(i32).rearrange("p (g j) -> p g j", j=TG)
                               for k in range(3))
        fields = edges[:, 0:2 * NG * TG].bitcast(bf16).rearrange("p (g j f) -> p g j f", j=TG, f=4)
        LO, BLK, DST, TYP = range(4)
        src_s = edges[:, 2 * NG * TG:3 * NG * TG].bitcast(i32).rearrange("p (g j) -> p g j", j=TG)
        agg = sb("agg", [P, NACC])
        big = sb("big", [P, NACC])
        cnt = big[0:R, :]
        work = sb("work", [P, 7070])
        ident = sb("ident", [P, P])
        iota_w = sb("iota_w", [P, P])
        iota_r = sb("iota_r", [P, R])
        before = sb("before", [P, P])
        after = sb("after", [P, P])
        after_b = sb("after_b", [P, P], bf16)
        ones_b = sb("ones_b", [P, P], bf16)
        ident_b = sb("ident_b", [P, P], bf16)
        earlier = sb("earlier", [P, TG, TG], bf16)
        expand = sb("expand", [R, P])
        ones = sb("ones", [P, P])
        dump = sb("dump", [P, 1])
        first_i = sb("first_i", [1, NG], i32)
        first_f = sb("first_f", [1, NG])
        base_tab = sb("base_tab", [P, NG + NW])
        wrel = [sb(f"wrel{k}", [P, D]) for k in range(2)]
        root = [sb(f"root{k}", [ROW, D]) for k in range(2)]
        w_hid = sb("w_hid", [2 * ROW, 2 * HID])
        w_split = [sb(f"w_split{k}", [P, 2 * HID], bf16) for k in range(2)]
        part_of = sb("part_of", [P, 4])
        b_hid = sb("b_hid", [2 * HID, 1])
        w_out = sb("w_out", [2 * HID, 2 * D])
        b_out = sb("b_out", [P, 2 * D])
        x_node = sb("x_node", [P, NB, D])
        wide_node = sb("wide_node", [P, NBS, D])
        h_node = wide_node[:, 0:NB, :]
        deg = sb("deg", [P, NB])
        stat = [sb(f"stat{k}", [P, NB]) for k in range(2)]
        node_buf = sb("node_buf", [P, 3 * CN])
        cnt_c, inv_c, agg_c = node_buf[0:R, 0:CN], node_buf[0:R, CN:2 * CN], node_buf[:, 2 * CN:3 * CN]
        xs_c = sb("xs_c", [P, CB, D])
        xT_c = sb("xT_c", [ROW, CN])
        red = sb("red", [P, 2])
        red_all = sb("red_all", [P, 2])
        flag_f = sb("flag_f", [1, 2])
        flag_i = sb("flag_i", [1, 2], i32)
        idx = [sb(f"idx{b}", [P, TG], i32) for b in range(2)]
        xx_both = sb("xx_both", [P, 2 * TG * 2 * ROW])
        xx = [xx_both[:, b * TG * 2 * ROW:(b + 1) * TG * 2 * ROW].rearrange("p (j r) -> p j r", r=2 * ROW) for b in range(2)]

        TYPX1 = UMAX * (R * D + W + R + 1) + UMIN * P // 2
        carve = carver(work)
        typ_x = carve(UMAX, R, D)
        dst_hot = carve(UMAX, W)
        typ_hot = carve(UMAX, R)
        rel = carve(UMAX)
        lo_hot = carve(TG, P, dt=bf16)
        rank_hot = xx_both[:, 0:TG * P // 2].bitcast(bf16).rearrange("p (j c) -> p j c", c=P)
        blk_hot = carve(TG, NB, dt=bf16)
        xx_sorted = [carve(TG, D) for _ in range(2)]
        carve = carver(wide_node[:, :, :].rearrange("p b d -> p (b d)")[:, 2 * TG * TG:])
        es = [carve(3, TG, dt=i32) for _ in range(2)]
        lo_i, hi_i, rk_i = (carve(TG, dt=i32) for _ in range(3))
        neg, neg_rank, within, rank = (carve(TG) for _ in range(4))
        fld = carve(TG, 4, dt=bf16)
        tot_T = node_buf[0:NB, TG * NB:TG * NB + P]
        prod = node_buf[:, 0:TG * NB].rearrange("p (j b) -> p j b", b=NB)
        pairs = node_buf[:, 0:TG * TG].rearrange("p (j k) -> p j k", k=TG)
        hi_hot = x_hot = wide_node[:, :, :].rearrange("p b d -> p (b d)")[:, 0:TG * TG * 2].bitcast(bf16).rearrange(
            "p (j r f) -> p j r f", r=TG, f=4)
        row_i = work[0:1, 0:NG * TG].bitcast(i32)
        row_f = work[0:1, NG * TG:2 * NG * TG]
        lo_hot_u, blk_hot_u, lo_u, hi_u = lo_hot[:, 0:UMAX, :], blk_hot[:, 0:UMAX, :], lo_i[:, 0:UMAX], hi_i[:, 0:UMAX]

        turned = xx_both[:, 0:DQ * 4 * P].rearrange("p (q e) -> p q e", e=4 * P)
        carve = carver(work[:, TYPX1:])
        typ_x1 = carve(UMIN, R, D)
        carve = carver(node_buf)
        dst_hot1 = carve(UMIN, W)
        picked = [node_buf[:, q * 4 * SPAN * D:(q + 1) * 4 * SPAN * D].rearrange("p (j s d) -> p j s d", s=SPAN, d=D)
                  for q in range(DQ)]
        dense_x = carve(UMIN, D)
        dense_blk = carve(UMIN, SPAN)
        dense_neg = carve(UMIN)

        carve = carver(big)
        g_vv, g_xw, g_m1, g_m2 = (carve(UMAX, 2, D) for _ in range(4))
        g_m3 = carve(UMAX, D)
        g_msg = [carve(UMAX, 2, D) for _ in range(2)]
        g_small = [carve(UMAX, 2) for _ in range(6)]
        g_qv, srcf, nbef, fidx = (carve(UMAX) for _ in range(4))
        g_xT = [carve(4 * P) for _ in range(2)]
        g_hid = [carve(4 * P) for _ in range(2)]
        msum = [carve(UMAX, D) for _ in range(2)]
        idx_o = [carve(UMAX, dt=i32) for _ in range(2)]
        idx_s = [carve(UMAX, dt=i32) for _ in range(2)]
        idx_d = [carve(UMAX, dt=i32) for _ in range(2)]
        same, same_b = (carve(UMAX, P) for _ in range(2))
        tab = [big[:, k * NB * D:(k + 1) * NB * D] for k in range(NT)]
        node_rows = big[:, 0:NB * XROW].rearrange("p (b f) -> p b f", f=XROW)
        rest = big[:, NB * XROW:NB * (XROW + D)].rearrange("p (b d) -> p b d", d=D)
        carve = carver(big)
        hot = [carve(TG, W, dt=bf16) for _ in range(2)]
        src_hot = carve(TG, P)
        msg_blk = carve(TG, SPAN, D)
        f_m1, f_m2 = (msg_blk.rearrange("p j s d -> p (j s d)")[:, k * TG * 2 * D:(k + 1) * TG * 2 * D].rearrange(
            "p (j s d) -> p j s d", s=2, d=D) for k in range(2))
        scaled_rows = [carve(TG, 2, D) for _ in range(2)]
        w_four = big[:, 0:2 * HID]
        w_rest = big[:, 2 * HID:4 * HID]
        w_part = [big[:, (4 + k) * HID:(5 + k) * HID].bitcast(bf16) for k in range(3)]
        carve = carver(work)
        f_vv = carve(TG, 2, D)
        f_dT, f_xT = ([carve(4 * P, dt=bf16) for _ in range(2)] for _ in range(2))
        f_hid = [carve(4 * P) for _ in range(2)]
        acc_odd = carve(NBS, D)
        rows = [xx_both[:, 0:TG * XY].rearrange("p (j f) -> p j f", f=XY), carve(TG, XY)]
        acc_w = carve(D)
        msg_rest = carve(TG, D)
        acc_src = [wide_node[:, :, :], acc_odd]
        carve = carver(node_buf)
        f_msg = carve(TG, 2, D)
        f_m3 = carve(TG, D)
        f_small = [carve(TG, 2) for _ in range(6)]
        f_qv = carve(TG)
        blk7 = [carve(TG, SPAN) for _ in range(2)]
        f_neg = [carve(TG) for _ in range(2)]
        xwin = [carve(XROW) for _ in range(2)]
        msg_part = carve(TG, 3, D, dt=bf16)

        bank = [ctx.enter_context(nc.psum_tensor(f"bank{k}", [P, 512], f32)) for k in range(8)]
        ps_acc, ps_cnt, ps_hist = bank[0], bank[1], bank[2]
        ps_rank, ps_tot, ps_fld = bank[3], bank[4], bank[5]
        ps_E = [bank[3], bank[4]]
        ps_xT = [bank[5], bank[6]]
        ps_o = bank[7]
        ps_t = [bank[1], bank[2]]
        ps_h = [bank[3], bank[4]]
        ps_v, ps_r, ps_s = bank[5], bank[6], bank[7]
        ps_acc1 = bank[7]
        ps_lo, ps_rows = [bank[1], bank[2], bank[6]], [bank[3], bank[4], bank[5]]
        ps_dT, ps_rT, ps_hid, ps_vv, ps_y = bank[1], bank[2], bank[3], [bank[4], bank[5]], bank[6]
        ps_accw, ps_accT = bank[0][:, 0:D], bank[0][0:D, D:D + W]
        ps_sum = [bank[7], bank[0][:, D + W:D + W + 3 * SPAN * D]]

        s_iota, s_consts, s_zeroed, s_loaded, s_dst, s_first, s_row = (
            sem(n) for n in "s_iota s_consts s_zeroed s_loaded s_dst s_first s_row".split())
        s_red, s_redall, s_flag, s_tick, s_vch, s_ach = (
            sem(n) for n in "s_red s_redall s_flag s_tick s_vch s_ach".split())
        s_orig = [sem(f"s_orig{k}") for k in range(2)]
        s_inv, s_E, s_aggc, s_xsc, s_xTp, s_xTc, s_node, s_hnode = (
            sem(n) for n in "s_inv s_E s_aggc s_xsc s_xTp s_xTc s_node s_hnode".split())
        s_nodes, s_htab, s_ztab, s_rows, s_xtab, s_exp, s_act, s_end, s_free, s_sums, s_out = (
            sem(n) for n in "s_nodes s_htab s_ztab s_rows s_xtab s_exp s_act s_end s_free s_sums s_out".split())
        gen = [sems(f"gen{k}", "idx hot acc hhot hist", "xfree gat") for k in range(2)]
        so = sems("sort", "idx part hot acc nlo lohot hist blkhot tot totc base nrl rlhot fld fldps fldc rows rowsps blk",
                  "es esfree xfree gat")
        fa = sems("rel2", "idx part hot acc neg lohot tr trc rows", "xfree gat")
        gs = sems("sheafg", "idx hot acc tr xt hp hs vd vfree rr rused same msg sp ms idxo", "xfree gat scat")
        s_table = [sem(f"s_table{k}") for k in range(NT)]
        sh = sems("sheaf", "idx hot tr dt xd xdc ttr xt hp hs vd vfree neg srchot msg msgblk acc accc accT accd sc drained",
                  "xfree gat win winfree")

        NLOAD = 40
        block = ctx.enter_context(nc.Block())
        groups = "(g p j) -> p g j"

        def blocks(ap):
            return ap.rearrange("(b p) d -> p b d", p=P)

        @block.sync
        def _(sp):
            loads = []

            def load(o, i):
                sp.dma_start(o, i, allow_slow_non_contiguous=True).then_inc(s_loaded, 16)
                loads.append(1)
            sp.dma_start(first_i[0:1, :], dst.rearrange("(o g e) -> o g e", o=1, e=GE)[:, :, 0],
                         allow_slow_non_contiguous=True).then_inc(s_first, 16)
            sp.dma_start(dst_i, dst.rearrange(groups, p=P, j=TG)).then_inc(s_dst, 16)
            sp.wait_ge(s_zeroed, 1)
            load(x_node[:, 0:NB - 1, :], blocks(x[0:(NB - 1) * P, :]))
            load(x_node[0:N - (NB - 1) * P, NB - 1, :], x[(NB - 1) * P:N, :])
            for k, (w, r, b) in enumerate(((l0w1, l0r1, l0b1), (l0w2, l0r2, l0b2))):
                load(wrel[k][:, :], w.rearrange("r d f -> (r d) f"))
                load(root[k][0:D, :], r)
                load(root[k][D:ROW, :], b.rearrange("(o f) -> o f", o=1))
            w1T = l1w1.rearrange("h k -> k h")
            for half, (a, b) in enumerate(((0, ROW), (ROW, 0))):
                load(w_hid[a:a + D, half * HID:(half + 1) * HID], w1T[0:D, :])
                load(w_hid[b:b + D, half * HID:(half + 1) * HID], w1T[D:2 * D, :])
                for k in range(4):
                    for end, i in enumerate((half, 1 - half)):
                        load(w_four[end * 4 * D + k * D:end * 4 * D + (k + 1) * D, half * HID:(half + 1) * HID],
                             w1T[i * D:(i + 1) * D, :])
                load(b_hid[half * HID:(half + 1) * HID, :], l1b1.rearrange("(h o) -> h o", o=1))
                load(w_out[half * HID:(half + 1) * HID, half * D:(half + 1) * D], l1w2.rearrange("d h -> h d"))
                load(b_out[:, half * D:(half + 1) * D], l1b2.partition_broadcast(P))
            for k in range(NT):
                load(sums[k].rearrange("(p f) d -> p (f d)", p=P), agg[:, 0:TROWS * D // P])
            load(win_table[NP:TROWS, :], agg[:, 0:XROW])
            assert len(loads) == NLOAD, len(loads)

            def load_edges(n):
                for k, (o, i) in enumerate(((src_i, src), (dst_i, dst), (typ_i, et))):
                    sp.dma_start(o, i.rearrange(groups, p=P, j=TG)).then_inc(s_orig[n], 16)

            sp.wait_ge(s_flag, 1)
            fast = sp.value_load(flag_i[0:1, 0:1], min_val=0, max_val=1)
            with sp.If(fast == 1):
                by_group = [e.rearrange("(g p j) -> g p j", p=P, j=TG) for e in (src, dst, et)]

                def stream(g, b, h):
                    sp.wait_ge(so["esfree"][b], h + 1)
                    for k in range(3):
                        sp.dma_start(es[b][:, k, :], by_group[k][g, :, :]).then_inc(so["es"][b], 16)
                each_group(sp, stream)
                sp.wait_ge(so["rows"], 1)
                sp.dma_start(block_table[:, 0:TG], row_i.rearrange("p (g j) -> p g j", j=TG)).then_inc(so["blk"], 16)
            with sp.Else():
                load_edges(0)
            sp.wait_ge(s_hnode, NC)
            sp.dma_start(blocks(h_table), h_node).then_inc(s_htab, 16)
            sp.wait_ge(s_flag, 2)
            fast2 = sp.value_load(flag_i[0:1, 1:2], min_val=0, max_val=1)
            with sp.If(fast2 == 1):
                sp.sem_inc(s_tick, 1)
            with sp.Else():
                load_edges(1)
            sp.wait_ge(s_ztab, 1)
            with sp.If(fast2 == 1):
                sp.wait_ge(s_rows, 1)
                sp.dma_start(blocks(x1_table), node_rows[:, :, 0:XY]).then_inc(s_xtab, 16)
                sp.dma_start(blocks(win_table[0:NP, :]), node_rows).then_inc(s_xtab, 16)
                sp.wait_ge(s_xtab, 32)

                def window(g, b, h):
                    sp.wait_ge(sh["winfree"][b], h + 1)
                    base = sp.value_load(first_i[0:1, bass.ds(g, 1)], min_val=0, max_val=N - 1)
                    sp.dma_start(xwin[b], win_table[bass.ds(base, W), :]).then_inc(sh["win"][b], 16)
                each_group(sp, window)
            with sp.Else():
                sp.dma_start(blocks(x1_plain)[:, :, 0:D], x_node[:, :, :]).then_inc(s_xtab, 16)
                sp.dma_start(blocks(x1_plain)[:, :, D], deg[:, :], allow_slow_non_contiguous=True).then_inc(s_xtab, 16)
                sp.wait_ge(s_end, 1)
                sp.wait_ge(s_free, 1)
                for k in range(NT):
                    sp.dma_start(tab[k].rearrange("p (b d) -> p b d", d=D), blocks(sums[k][0:NP, :])).then_inc(s_sums, 16)
            sp.wait_ge(s_out, 1)
            sp.dma_start(blocks(out[0:(NB - 1) * P, :]), x_node[:, 0:NB - 1, :]).then_inc(s_out, 16)
            sp.dma_start(out[(NB - 1) * P:N, :], x_node[0:N - (NB - 1) * P, NB - 1, :]).then_inc(s_out, 16)
            sp.wait_ge(s_out, 33)

        LOADED = 16 * NLOAD

        @block.gpsimd
        def _(pool):
            def iota(t, pattern, base=0, mult=0):
                nc.gpsimd.iota(t, pattern, base=base, channel_multiplier=mult,
                               allow_small_or_imprecise_dtypes=True).then_inc(s_iota, 1)
            iota(ident[:, :], [[1, P]], mult=-1)
            iota(iota_w[:, :], [[1, P]])
            iota(iota_r[:, :], [[1, R]])
            iota(expand[:, :], [[1, P]], mult=-D)
            iota(dump[:, :], [[0, 1]], base=NP, mult=1)
            iota(base_tab[:, NG:NG + NW], [[W, NW]])
            iota(earlier[:, :, :], [[-1, TG], [1, TG]])

            def worst(n):
                pool.wait_ge(s_red, n)
                nc.gpsimd.partition_all_reduce(red_all[:, :], red[:, :], P, RMAX).then_inc(s_redall, 1)

            worst(1)
            pool.wait_ge(s_loaded, LOADED)
            pool.wait_ge(s_flag, 1)

            def gather(to, table, at):
                return pool.indirect_dma_start(out=to, out_offset=None, in_=table,
                                               in_offset=bass.IndirectOffsetOnAxis(ap=at, axis=0))

            def rows_general(s, table):
                with pool.Fori(0, NG) as g:
                    for u, (a, b) in enumerate(UNITS):
                        pool.wait_ge(s["xfree"][u], g + 1)
                        pool.sem_inc(s_tick, 1)
                        nc.gpsimd.tensor_copy(idx[u][:, 0:b - a], src_i[:, g, a:b]).then_inc(s["idx"], 1)
                        pool.wait_ge(s["idx"], 2 * g + (u + 1))
                        pool.sem_inc(s_tick, 1)
                        for j in range(b - a):
                            gather(xx[u][:, j, 0:D], table, idx[u][:, j:j + 1]).then_inc(s["gat"][u], 16)

            def rows_by_group(s, table, cols, indices, to, tiles=TG):
                def group(g, b, h):
                    pool.wait_ge(s["xfree"][b], h + 1)
                    pool.sem_inc(s_tick, 1)
                    if indices is None:
                        pool.wait_ge(s["es"][b], 48 * h + 48)
                        pool.sem_inc(s_tick, 1)
                    at = es[b][:, 0, :] if indices is None else indices[:, g, :]
                    nc.gpsimd.tensor_copy(idx[b][:, :], at).then_inc(s["idx"], 1)
                    pool.wait_ge(s["idx"], g + 1)
                    pool.sem_inc(s_tick, 1)
                    for j in range(tiles):
                        gather(to[b][:, j, 0:cols], table, idx[b][:, j:j + 1]).then_inc(s["gat"][b], 16)
                each_group(pool, group)

            fast = pool.value_load(flag_i[0:1, 0:1], min_val=0, max_val=1)
            with pool.If(fast == 1):
                rows_by_group(so, x, D, None, xx_sorted)
                worst(2)
            with pool.Else():
                pool.wait_ge(s_orig[0], 48)
                rows_general(gen[0], x)
            pool.wait_ge(s_flag, 2)
            pool.wait_ge(s_htab, 16)
            fast2 = pool.value_load(flag_i[0:1, 1:2], min_val=0, max_val=1)
            with pool.If(fast2 == 1):
                rows_by_group(fa, h_table, D, src_s, xx_sorted, UMAX)
                pool.wait_ge(s_xtab, 32)
                rows_by_group(sh, x1_table, XY, src_s, rows)
            with pool.Else():
                pool.wait_ge(s_orig[1], 48)
                rows_general(gen[1], h_table)
                pool.wait_ge(s_xtab, 32)

                def gather_unit(u, g):
                    a, b = UNITS[u]
                    pool.wait_ge(gs["xfree"][u], g + 1)
                    pool.sem_inc(s_tick, 1)
                    nc.gpsimd.tensor_copy(idx_s[u], src_i[:, g, a:a + b - a] if b - a == UMAX else src_i[:, g, a - 1:b]
                                          ).then_inc(gs["idx"], 1)
                    nc.gpsimd.tensor_copy(idx_d[u], dst_i[:, g, a:b] if b - a == UMAX else dst_i[:, g, a - 1:b]
                                          ).then_inc(gs["idx"], 1)
                    pool.wait_ge(gs["idx"], 4 * g + (2 * u + 2))
                    pool.sem_inc(s_tick, 1)
                    o = UMAX - (b - a)
                    for j in range(b - a):
                        gather(xx[u][:, j, 0:ROW], x1_plain, idx_s[u][:, o + j:o + j + 1]).then_inc(gs["gat"][u], 16)
                        gather(xx[u][:, j, ROW:2 * ROW], x1_plain, idx_d[u][:, o + j:o + j + 1]).then_inc(gs["gat"][u], 16)

                def scatter_unit(u, g):
                    a, b = UNITS[u]
                    pool.wait_ge(gs["ms"], 2 * g + (u + 2))
                    pool.sem_inc(s_tick, 1)
                    pool.wait_ge(gs["idxo"], 2 * g + (u + 1))
                    pool.sem_inc(s_tick, 1)
                    for j in range(b - a):
                        k = j % NT
                        if j >= NT:
                            done = (PER_TABLE[0][k] if u else 0) + j // NT
                            pool.wait_ge(s_table[k], 16 * T_GROUP[k] * g + 16 * done)
                            pool.sem_inc(s_tick, 1)
                        pool.indirect_dma_start(out=sums[k], in_=msum[u][:, j, :], in_offset=None, compute_op=ALU.add,
                                                out_offset=bass.IndirectOffsetOnAxis(ap=idx_o[u][:, j:j + 1], axis=0)
                                                ).then_inc(s_table[k], 16)

                def scattered(u, g):
                    for k in range(NT):
                        done = PER_TABLE[0][k] + (PER_TABLE[1][k] if u else 0)
                        pool.wait_ge(s_table[k], 16 * T_GROUP[k] * g + 16 * done)
                    pool.sem_inc(gs["scat"][u], 1)

                for u in range(2):
                    gather_unit(u, 0)
                with pool.Fori(0, NG - 1) as g:
                    for u in range(2):
                        scatter_unit(u, g)
                        gather_unit(u, g + 1)
                        scattered(u, g)
                for u in range(2):
                    scatter_unit(u, NG - 1)
                    scattered(u, NG - 1)
                pool.sem_inc(s_end, 1)

        @block.vector
        def _(dve):
            V = nc.vector
            ch = Chain(dve, s_vch)

            def in_parts(v, parts, rest):
                ch.do(V.tensor_copy(parts[0], v))
                ch.wait()
                ch.do(V.tensor_tensor(rest, v, parts[0], ALU.subtract))
                ch.wait()
                ch.do(V.tensor_copy(parts[1], rest))
                ch.wait()
                ch.do(V.tensor_tensor(parts[2], rest, parts[1], ALU.subtract))

            for t in (agg, big, x_node, w_hid, w_out, xT_c, ones, ones_b, deg):
                ch.do(V.memset(t[:], 1.0 if t in (ones, ones_b, xT_c) else 0.0))
            ch.wait()
            dve.sem_inc(s_zeroed, 1)
            dve.wait_ge(s_iota, 7)
            band = node_buf[0:R, 0:P]
            ch.do(V.tensor_scalar(before[:, :], ident[:, :], 0.0, None, ALU.is_lt))
            ch.do(V.tensor_scalar(after[:, :], ident[:, :], 0.0, None, ALU.is_gt))
            ch.do(V.tensor_scalar(after_b[:, :], ident[:, :], 0.0, None, ALU.is_gt))
            ch.do(V.tensor_scalar(earlier[:, :, :], earlier[:, :, :], 0.0, None, ALU.is_lt))
            ch.do(V.tensor_scalar(band, expand[:, :], float(D), None, ALU.is_lt))
            ch.wait()
            ch.do(V.tensor_scalar(expand[:, :], expand[:, :], 0.0, None, ALU.is_ge))
            dve.wait_ge(s_first, 16)
            ch.do(V.tensor_copy(first_f[0:1, :], first_i[0:1, :]))
            ch.wait()
            ch.do(V.tensor_tensor(expand[:, :], expand[:, :], band, ALU.mult))
            ch.do(V.tensor_scalar(ident[:, :], ident[:, :], 0.0, None, ALU.is_equal))
            ch.wait()
            ch.do(V.tensor_copy(ident_b[:, :], ident[:, :]))
            ch.wait()
            for s in (gen[0], gen[1], so, fa, gs, sh):
                for t in s["xfree"]:
                    dve.sem_inc(t, 1)
            for s in (s_node, gs["vd"], gs["vfree"], gs["rused"], gs["ms"], *gs["scat"], *so["esfree"], so["fldps"],
                      *sh["winfree"], sh["vfree"], sh["xdc"]):
                dve.sem_inc(s, 1)
            dve.sem_inc(sh["drained"], 2 * NQ)
            dve.sem_inc(s_consts, 1)
            dve.wait_ge(s_row, 1)
            ch.do(V.tensor_copy(base_tab[:, 0:NG], ps_acc[:, 0:NG]))
            dve.wait_ge(s_dst, 16)
            dve.wait_ge(s_loaded, LOADED)
            in_parts(w_four, w_part, w_rest)
            place, is_w3 = part_of[:, 0:1], part_of[:, 1:2]
            ch.do(V.tensor_scalar(place, dump[:, 0:1], -float(NP), None, ALU.add))
            ch.wait()
            ch.do(V.tensor_scalar(part_of[:, 1:2], place, 3.0 * D, None, ALU.is_ge))
            ch.do(V.tensor_scalar(part_of[:, 2:3], place, 4.0 * D, None, ALU.is_lt))
            ch.do(V.tensor_scalar(part_of[:, 3:4], place, 7.0 * D, None, ALU.is_ge))
            ch.wait()
            ch.do(V.tensor_tensor(is_w3, is_w3, part_of[:, 2:3], ALU.mult))
            ch.wait()
            ch.do(V.tensor_tensor(is_w3, is_w3, part_of[:, 3:4], ALU.add))
            ch.wait()
            ch.do(V.tensor_scalar(part_of[:, 2:3], is_w3, -1.0, 1.0, ALU.mult, ALU.add))
            ch.do(V.tensor_scalar(w_four, w_part[2], is_w3, None, ALU.mult))
            ch.wait()
            ch.do(V.tensor_scalar(w_rest, w_part[0], part_of[:, 2:3], None, ALU.mult))
            ch.do(V.tensor_scalar(w_split[1][:, :], w_part[1], part_of[:, 2:3], None, ALU.mult))
            ch.wait()
            ch.do(V.tensor_tensor(w_split[0][:, :], w_rest, w_four, ALU.add))
            ch.wait()
            ch.do(V.memset(big[:, 0:8 * HID], 0.0))
            ch.wait()
            PART = 5
            part = NG // PART * TG
            off = work[:, 0:part]

            def flag(k, greatest, extra=None):
                ch.wait()
                ch.do(V.tensor_reduce(red[:, 0:1], stat[0][:, 0:PART], AX, ALU.max))
                ch.do(V.tensor_reduce(red[:, 1:2], stat[1][:, 0:PART], AX, ALU.max))
                ch.wait()
                dve.sem_inc(s_red, 1)
                dve.wait_ge(s_redall, k + 1)
                ch.do(V.tensor_scalar(flag_f[0:1, 0:1], red_all[0:1, 0:1], float(greatest), None, ALU.is_le))
                ch.do(V.tensor_scalar(flag_f[0:1, 1:2], red_all[0:1, 1:2], 0.0, None, ALU.is_le))
                ch.wait()
                ch.do(V.tensor_tensor(flag_i[0:1, k:k + 1], flag_f[0:1, 0:1], flag_f[0:1, 1:2], ALU.mult))
                ch.restart()
                dve.sem_inc(s_flag, 1)

            for h in range(PART):
                gr = slice(h * NG // PART, (h + 1) * NG // PART)
                ch.do(V.tensor_tensor(off.rearrange("p (g j) -> p g j", j=TG), dst_i[:, gr, :],
                                      base_tab[:, gr].unsqueeze(2).to_broadcast([P, NG // PART, TG]), ALU.subtract))
                ch.wait()
                ch.do(V.tensor_reduce(stat[0][:, h:h + 1], off, AX, ALU.max))
                ch.do(V.tensor_reduce(stat[1][:, h:h + 1], off, AX, ALU.min, negate=True))
                ch.wait()
            flag(0, W - 1)

            def one_hot(o, values, n, width, grid):
                return V.tensor_tensor(o, values.unsqueeze(2).to_broadcast([P, n, width]),
                                       grid.unsqueeze(1).to_broadcast([P, n, width]), ALU.is_equal)

            def by_relation(n, to, rows, free):
                V.tensor_tensor(to[:, 0:n, :, :], typ_hot[:, 0:n, :].unsqueeze(3).to_broadcast([P, n, R, D]),
                                rows.unsqueeze(2).to_broadcast([P, n, R, D]), ALU.mult).then_inc(free, 1)

            def drain(base, count, s_acc, rows, counts, ps_acc=ps_acc):
                dve.wait_ge(s_acc, count)
                acc = agg[0:rows, bass.ds(base, W)]
                ch.do(V.tensor_tensor(acc, acc, ps_acc[0:rows, 0:W], ALU.add))
                if counts:
                    acc = cnt[:, bass.ds(base, W)]
                    ch.do(V.tensor_tensor(acc, acc, ps_cnt[0:R, 0:W], ALU.add))

            def all_windows(u, g, s, rows, counts):
                a, b = UNITS[u]
                n = b - a
                ch.restart()
                with dve.Fori(0, NW) as w:
                    ch.do(V.tensor_scalar(rel[:, 0:n], dst_i[:, g, a:b], base_tab[:, bass.ds(w + NG, 1)], None,
                                          ALU.subtract))
                    ch.wait()
                    one_hot(dst_hot[:, 0:n, :], rel[:, 0:n], n, W, iota_w[:, :]).then_inc(s["hot"], 1)
                    drain(w * W, g * (2 * NW) + w + (u * NW + 1), s["acc"], rows, counts)
                    ch.restart()

            def relational_general(phase):
                s = gen[phase]
                with dve.Fori(0, NG) as g:
                    for u, (a, b) in enumerate(UNITS):
                        n = b - a
                        ch.do(one_hot(typ_hot[:, 0:n, :], typ_i[:, g, a:b], n, R, iota_r[:, :]))
                        ch.wait()
                        dve.wait_ge(s["gat"][u], g * (16 * n) + 16 * n)
                        by_relation(n, typ_x, xx[u][:, 0:n, 0:D], s["xfree"][u])
                        if phase == 0:
                            ch.do(V.tensor_scalar(lo_u[:, 0:n], src_i[:, g, a:b], P - 1, None, ALU.bitwise_and))
                            ch.do(V.tensor_scalar(hi_u[:, 0:n], src_i[:, g, a:b], 7, None, ALU.logical_shift_right))
                            ch.wait()
                            ch.do(one_hot(lo_hot_u[:, 0:n, :], lo_u[:, 0:n], n, P, iota_w[:, :]))
                            one_hot(blk_hot_u[:, 0:n, :], hi_u[:, 0:n], n, NB, iota_w[:, 0:NB]).then_inc(s["hhot"], 1)
                        all_windows(u, g, s, P, phase == 0)
                        if phase == 0:
                            dve.wait_ge(s["hist"], 2 * g + (u + 1))
                            ch.do(V.tensor_tensor(deg[:, :], deg[:, :], ps_hist[:, 0:NB], ALU.add))
                    ch.restart()

            def relational_and_sort():
                def group(g, b, h):
                    half = h
                    e_src, e_dst, e_typ = (es[b][:, k, :] for k in range(3))
                    dve.wait_ge(so["es"][b], 48 * half + 48)
                    ch.do(V.tensor_scalar(lo_i, e_src, P - 1, None, ALU.bitwise_and))
                    ch.do(V.tensor_scalar(hi_i, e_src, 7, None, ALU.logical_shift_right))
                    ch.do(V.tensor_scalar(fld[:, :, DST], e_dst, base_tab[:, bass.ds(g, 1)], None, ALU.subtract))
                    ch.do(V.tensor_copy(fld[:, :, TYP], e_typ))
                    ch.wait()
                    ch.do(V.tensor_copy(fld[:, :, LO], lo_i))
                    ch.do(V.tensor_copy(fld[:, :, BLK], hi_i))
                    V.tensor_scalar(neg, lo_i, -1.0, None, ALU.mult).then_inc(so["nlo"], 1)
                    one_hot(blk_hot, hi_i, TG, NB, iota_w[:, 0:NB]).then_inc(so["blkhot"], 1)
                    base = dve.value_load(first_i[0:1, bass.ds(g, 1)], min_val=0, max_val=N - 1)

                    def layer(u):
                        a, c = UNITS[u]
                        n = c - a
                        ch.do(one_hot(typ_hot[:, 0:n, :], e_typ[:, a:c], n, R, iota_r[:, :]))
                        ch.wait()
                        dve.wait_ge(so["gat"][b], 16 * TG * half + 16 * TG)
                        by_relation(n, typ_x, xx_sorted[b][:, a:c, :], so["part"] if u == 0 else so["xfree"][b])
                        one_hot(dst_hot[:, 0:n, :], fld[:, a:c, DST], n, W, iota_w[:, :]).then_inc(so["hot"], 1)
                        if u:
                            dve.sem_inc(so["esfree"][b], 1)

                    layer(0)
                    ch.do(V.tensor_tensor(pairs, hi_i.unsqueeze(2).to_broadcast([P, TG, TG]),
                                          hi_i.unsqueeze(1).to_broadcast([P, TG, TG]), ALU.is_equal))
                    ch.wait()
                    ch.do(V.tensor_tensor(pairs, pairs, earlier[:, :, :], ALU.mult))
                    ch.wait()
                    ch.do(V.tensor_reduce(within, pairs, AX, ALU.add))
                    dve.wait_ge(so["tot"], g + 1)
                    V.tensor_copy(tot_T, ps_tot[0:NB, 0:P]).then_inc(so["totc"], 1)
                    drain(base, 2 * g + 1, so["acc"], P, True)
                    layer(1)
                    ch.wait()
                    dve.wait_ge(so["base"], g + 1)
                    ch.do(V.tensor_tensor(prod, blk_hot, ps_rank[:, 0:NB].unsqueeze(1).to_broadcast([P, TG, NB]), ALU.mult))
                    ch.wait()
                    ch.do(V.tensor_reduce(rank, prod, AX, ALU.add))
                    ch.wait()
                    ch.do(V.tensor_tensor(rk_i, rank, within, ALU.add))
                    ch.wait()
                    ch.do(V.tensor_scalar(lo_i, rk_i, P - 1, None, ALU.bitwise_and))
                    ch.do(V.tensor_scalar(hi_i, rk_i, 7, None, ALU.logical_shift_right))
                    ch.wait()
                    dve.wait_ge(so["fldps"], g + 1)
                    dve.sem_inc(s_tick, 1)
                    V.tensor_scalar(neg_rank, lo_i, -1.0, None, ALU.mult).then_inc(so["nrl"], 1)
                    ch.do(V.tensor_tensor(pairs, hi_i.unsqueeze(2).to_broadcast([P, TG, TG]),
                                          iota_w[:, 0:TG].unsqueeze(1).to_broadcast([P, TG, TG]), ALU.is_equal))
                    ch.wait()
                    V.tensor_tensor(x_hot, pairs.unsqueeze(3).to_broadcast([P, TG, TG, 4]),
                                    fld.unsqueeze(2).to_broadcast([P, TG, TG, 4]), ALU.mult).then_inc(so["fld"], 1)
                    dve.wait_ge(so["hist"], g + 1)
                    ch.do(V.tensor_tensor(deg[:, :], deg[:, :], ps_hist[:, 0:NB], ALU.add))
                    dve.wait_ge(so["fld"], g + 1)
                    dve.sem_inc(s_tick, 1)
                    drain(base, 2 * g + 2, so["acc"], P, True)
                    ch.restart()
                each_group(dve, group)
                dve.wait_ge(so["fldc"], NG)
                blk = fields[:, :, :, BLK]
                ch.do(V.tensor_copy(row_i.rearrange("p (g j) -> p g j", j=TG), fields[0:1, :, :, BLK]))
                ch.do(V.tensor_copy(row_f.rearrange("p (g j) -> p g j", j=TG), fields[0:1, :, :, BLK]))
                ch.do(V.scalar_tensor_tensor(src_s, fields[:, :, :, BLK], float(P), fields[:, :, :, LO], ALU.mult, ALU.add))
                ch.wait()
                dve.sem_inc(so["rows"], 1)
                dve.wait_ge(so["rowsps"], 1)
                for k in range(ROWS):
                    a, b = k * GR, min((k + 1) * GR, NG)
                    ch.do(V.tensor_tensor(blk[:, a:b, :], blk[:, a:b, :],
                                          bank[k][:, 0:(b - a) * TG].rearrange("p (g j) -> p g j", j=TG), ALU.subtract))
                ch.wait()
                all_blk = fields.rearrange("p g j f -> p (g j) f")[:, :, BLK]
                for k in range(PART):
                    part_k = all_blk[:, k * part:(k + 1) * part]
                    ch.do(V.tensor_reduce(stat[0][:, k:k + 1], part_k, AX, ALU.max))
                    ch.do(V.tensor_reduce(stat[1][:, k:k + 1], part_k, AX, ALU.min, negate=True))
                dve.wait_ge(so["blk"], 16)
                flag(1, SPAN - 1)

            def relational_sorted():
                second = UNITS[1][0]
                ch.do(V.memset(wide_node[:, NB:NBS, :], 0.0))
                ch.wait()

                def negate(g):
                    V.tensor_scalar(dense_neg, fields[:, g, second:TG, LO], -1.0, None, ALU.mult).then_inc(fa["neg"], 1)

                def sums(g, u):
                    base = dve.value_load(first_i[0:1, bass.ds(g, 1)], min_val=0, max_val=N - 1)
                    drain(base, 2 * g + (u + 1), fa["acc"], P, False, (ps_acc, ps_acc1)[u])

                def group(g, b, h, before=None, more=True):
                    def half(u, x_rows, free):
                        a, c = UNITS[u]
                        n = c - a
                        ch.do(one_hot(typ_hot[:, 0:n, :], fields[:, g, a:c, TYP], n, R, iota_r[:, :]))
                        ch.wait()
                        if u == 0:
                            dve.wait_ge(fa["gat"][b], 16 * UMAX * h + 16 * UMAX)
                        by_relation(n, (typ_x, typ_x1)[u], x_rows, free)
                        one_hot((dst_hot, dst_hot1)[u][:, 0:n, :], fields[:, g, a:c, DST], n, W, iota_w[:, :]).then_inc(fa["hot"], 1)

                    if more:
                        dve.wait_ge(fa["lohot"], g + 1)
                        dve.sem_inc(s_tick, 1)
                        negate(g + 1)
                    ch.do(one_hot(dense_blk, fields[:, g, second:TG, BLK], UMIN, SPAN, iota_w[:, 0:SPAN]))
                    half(0, xx_sorted[b][:, 0:UMAX, :], fa["xfree"][b])
                    if before is not None:
                        sums(before, 1)
                    dve.wait_ge(fa["rows"], g + 1)
                    for q in range(DQ):
                        ch.do(V.tensor_tensor(picked[q], ps_rows[q][:, 0:4 * SPAN * D].rearrange("p (j s d) -> p j s d", s=SPAN, d=D),
                                              dense_blk[:, 4 * q:4 * q + 4, :].unsqueeze(3).to_broadcast([P, 4, SPAN, D]), ALU.mult))
                    for q in range(DQ):
                        ch.wait(2)
                        ch.do(V.tensor_reduce(dense_x[:, 4 * q:4 * q + 4, :], picked[q].rearrange("p j s d -> p j d s"), AX, ALU.add))
                    ch.wait()
                    half(1, dense_x, fa["part"])
                    sums(g, 0)
                    ch.restart()
                negate(0)
                ch.restart()
                group(0, 0, 0)
                each_group(dve, lambda i, b, h: group(i + 1, 1 - b, h + b, before=i), NG - 2)
                group(NG - 1, 0, NG // 2, before=NG - 2, more=False)
                sums(NG - 1, 1)
                ch.restart()

            def nodes(phase):
                def inverse(i):
                    ch.do(V.tensor_scalar(inv_c, cnt[:, bass.ds(i * CN, CN)], 1.0, None, ALU.max))
                    ch.wait()
                    V.reciprocal(inv_c, inv_c).then_inc(s_inv, 1)

                def step(i, more=True):
                    ch.do(V.tensor_copy(cnt_c, cnt[:, bass.ds(i * CN, CN)]))
                    dve.wait_ge(s_E, i + (phase * NC + 1))
                    half = CN // 2
                    for h in range(2):
                        last = V.tensor_tensor(agg_c[:, h * half:(h + 1) * half], agg[:, bass.ds(i * CN + h * half, half)],
                                               ps_E[h][:, 0:half], ALU.mult)
                        if h == 0:
                            ch.do(last)
                    last.then_inc(s_aggc, 1)
                    if more:
                        inverse(i + 1)
                    dve.wait_ge(s_node, i + (phase * NC + 2))
                    res = ps_o[:, 0:CB * D].rearrange("p (b d) -> p b d", d=D)
                    o = h_node[:, bass.ds(i * CB, CB), :]
                    if phase == 0:
                        d = deg[:, bass.ds(i * CB, CB)]
                        ch.do(V.tensor_tensor(d, d, ps_o[:, CB * D:CB * D + CB], ALU.add))
                        V.tensor_scalar(o, res, 0.0, None, ALU.max).then_inc(s_hnode, 1)
                    else:
                        ch.do(V.tensor_copy(o, res))
                    ch.restart()

                inverse(0)
                ch.restart()
                with dve.Fori(0, NC - 1) as i:
                    step(i)
                step(NC - 1, more=False)

            full = [P, NB, D]

            def wide(s):
                return s[:, :].unsqueeze(2).to_broadcast(full)

            def layer_norm(y, tmp, act_count):
                ch.wait()
                ch.do(V.tensor_reduce(stat[0][:, :], y, AX, ALU.add))
                ch.wait()
                ch.do(V.tensor_scalar(stat[0][:, :], stat[0][:, :], 1.0 / D, None, ALU.mult))
                ch.wait()
                ch.do(V.tensor_tensor(y, y, wide(stat[0]), ALU.subtract))
                ch.wait()
                ch.do(V.tensor_tensor(tmp, y, y, ALU.mult))
                ch.wait()
                ch.do(V.tensor_reduce(stat[1][:, :], tmp, AX, ALU.add))
                ch.wait()
                V.tensor_scalar(stat[1][:, :], stat[1][:, :], 1.0 / D, 1e-5, ALU.mult, ALU.add).then_inc(s_exp, 1)
                dve.wait_ge(s_act, act_count)
                ch.do(V.reciprocal(stat[1][:, :], stat[1][:, :]))
                ch.wait()

            z, y = h_node, x_node[:, :, :]
            tmp = agg[:, 0:NB * D].rearrange("p (b d) -> p b d", d=D)

            def softmax_and_norm():
                ch.do(V.tensor_reduce(stat[0][:, :], z, AX, ALU.max))
                ch.wait()
                ch.do(V.tensor_tensor(z, z, wide(stat[0]), ALU.subtract))
                ch.wait()
                V.tensor_scalar(deg[:, :], deg[:, :], 1e-5, None, ALU.max).then_inc(s_exp, 1)
                dve.wait_ge(s_act, 2)
                ch.do(V.tensor_reduce(stat[0][:, :], tmp, AX, ALU.add))
                ch.do(V.reciprocal(deg[:, :], deg[:, :]))
                ch.wait()
                ch.do(V.tensor_tensor(y, y, z, ALU.add))
                ch.wait()
                V.tensor_scalar(stat[1][:, :], stat[0][:, :], 1.0, None, ALU.mult).then_inc(s_exp, 1)
                dve.wait_ge(s_act, 3)
                ch.do(V.tensor_tensor(y, y, wide(stat[1]), ALU.subtract))
                layer_norm(y, tmp, 4)
                ch.do(V.tensor_tensor(y, y, wide(stat[1]), ALU.mult))
                ch.wait()
                ch.do(V.memset(agg[0:D, :], 0.0))
                ch.restart()
                dve.sem_inc(s_ztab, 1)

            def reflections(n, v, xu, mu, t1, t2, t3, small, q):
                n2, c, pv, rv, av, bv = (t[:, 0:n] for t in small)
                both = [P, n, 2, D]
                ch.do(V.tensor_tensor(t1, v, v, ALU.mult))
                ch.do(V.tensor_tensor(t2, v, xu, ALU.mult))
                ch.do(V.tensor_tensor(t3, v[:, :, 0, :], v[:, :, 1, :], ALU.mult))
                ch.wait(2)
                ch.do(V.tensor_reduce(n2, t1, AX, ALU.add))
                ch.wait(2)
                ch.do(V.tensor_reduce(pv, t2, AX, ALU.add))
                ch.wait(2)
                ch.do(V.tensor_reduce(q, t3, AX, ALU.add))
                for s in range(2):
                    ch.wait(1)
                    ch.do(V.tensor_tensor(t1[:, :, s, :], v[:, :, s, :], xu[:, :, 1 - s, :], ALU.mult))
                ch.do(V.tensor_scalar(c, n2, 1e-24, 0.5, ALU.max, ALU.mult))
                ch.wait(1)
                ch.do(V.tensor_reduce(rv, t1, AX, ALU.add))
                ch.wait(1)
                ch.do(V.reciprocal(c, c))
                ch.wait()
                ch.do(V.tensor_tensor(av, c, pv, ALU.mult))
                ch.wait()
                ch.do(V.tensor_tensor(t2, v, av.unsqueeze(3).to_broadcast(both), ALU.mult))
                for s in range(2):
                    ch.do(V.tensor_tensor(bv[:, :, s], av[:, :, 1 - s], q, ALU.mult))
                ch.wait()
                ch.do(V.tensor_tensor(bv, rv, bv, ALU.subtract))
                ch.do(V.tensor_tensor(mu[:, :, 0, :], xu[:, :, 1, :], t2[:, :, 1, :], ALU.subtract))
                ch.wait(1)
                ch.do(V.tensor_tensor(bv, bv, c, ALU.mult))
                ch.do(V.tensor_tensor(mu[:, :, 1, :], xu[:, :, 0, :], t2[:, :, 0, :], ALU.subtract))
                ch.wait(1)
                ch.do(V.tensor_tensor(t1, v, bv.unsqueeze(3).to_broadcast(both), ALU.mult))
                ch.wait()
                ch.do(V.tensor_tensor(mu, mu, t1, ALU.subtract))

            def sheaf_general():
                with dve.Fori(0, NG) as g:
                    done = 0
                    for u, (a, b) in enumerate(UNITS):
                        sheaf_unit(u, a, b - a, g, done)
                        done += len(CHUNKS[u])
                    ch.restart()
                dve.sem_inc(s_free, 1)
                dve.wait_ge(s_sums, 16 * NT)
                for k in range(1, NT):
                    ch.do(V.tensor_tensor(tab[0], tab[0], tab[k], ALU.add))
                    ch.wait()
                ch.do(V.tensor_copy(z, tab[0].rearrange("p (b d) -> p b d", d=D)))
                ch.restart()

            def sheaf_unit(u, a, n, g, done):
                ch.do(V.tensor_copy(srcf[:, 0:n], src_i[:, g, a:a + n]))
                ch.wait()
                dve.sem_inc(gs["same"], 1)
                for c, (ca, cb) in enumerate(CHUNKS[u]):
                    m = cb - ca
                    dve.wait_ge(gs["rr"], NCH * g + (done + c + 1))
                    V.tensor_tensor(same[:, ca:cb, :], srcf[:, ca:cb].unsqueeze(2).to_broadcast([P, m, P]),
                                    ps_r[:, 0:m * P].rearrange("p (a e) -> p a e", e=P), ALU.is_equal).then_inc(gs["rused"], 1)
                dve.wait_ge(gs["rused"], NCH * g + (done + len(CHUNKS[u]) + 1))
                ch.do(V.tensor_tensor(same_b[:, 0:n, :], same[:, 0:n, :],
                                      before[:, :].unsqueeze(1).to_broadcast([P, n, P]), ALU.mult))
                ch.wait()
                ch.do(V.tensor_reduce(nbef[:, 0:n], same_b[:, 0:n, :], AX, ALU.add))
                ch.do(V.tensor_scalar(fidx[:, 0:n], srcf[:, 0:n], dump[:, 0:1], None, ALU.subtract))
                ch.wait()
                ch.do(V.tensor_scalar(nbef[:, 0:n], nbef[:, 0:n], 0.0, None, ALU.is_equal))
                ch.wait()
                ch.do(V.tensor_tensor(fidx[:, 0:n], fidx[:, 0:n], nbef[:, 0:n], ALU.mult))
                ch.wait()
                dve.wait_ge(gs["scat"][u], g + 1)
                V.tensor_scalar(idx_o[u][:, 0:n], fidx[:, 0:n], dump[:, 0:1], None, ALU.add).then_inc(gs["idxo"], 1)
                dve.wait_ge(gs["vd"], NCH * g + (done + len(CHUNKS[u]) + 1))
                v, xu, mu = g_vv[:, 0:n], g_xw[:, 0:n], g_msg[u][:, 0:n]
                xs = xx[u][:, 0:n, :].rearrange("p n (s r) -> p n s r", s=2)
                V.tensor_tensor(v.rearrange("p n s d -> p n (s d)"),
                                ps_v[:, 0:n * 2 * D].rearrange("p (n d) -> p n d", d=2 * D),
                                b_out[:, :].unsqueeze(1).to_broadcast([P, n, 2 * D]), ALU.add).then_inc(gs["vfree"], 1)
                dve.wait_ge(gs["gat"][u], g * (32 * n) + 32 * n)
                V.tensor_tensor(xu, xs[:, :, :, 0:D], xs[:, :, :, D:ROW].to_broadcast([P, n, 2, D]),
                                ALU.mult).then_inc(gs["xfree"][u], 1)
                dve.wait_ge(gs["xfree"][u], g + 2)
                reflections(n, v, xu, mu, g_m1[:, 0:n], g_m2[:, 0:n], g_m3[:, 0:n], g_small, g_qv[:, 0:n])
                ch.wait()
                dve.sem_inc(gs["msg"], 1)
                all_windows(u, g, gs, D, False)

            def sheaf_sorted():
                parts = node_rows.bitcast(bf16)
                scaled = node_rows[:, :, XS:XY]
                ch.do(V.tensor_tensor(scaled, y, wide(deg), ALU.mult))
                in_parts(y, [parts[:, :, k * D:(k + 1) * D] for k in range(3)], rest)
                ch.wait()
                ch.do(V.tensor_copy(parts[:, :, 3 * D:4 * D], parts[:, :, 0:D]))
                in_parts(scaled, [parts[:, :, 2 * XY + k * D:2 * XY + (k + 1) * D] for k in range(3)], rest)
                ch.wait()
                dve.sem_inc(s_rows, 1)
                ch.do(V.memset(wide_node[:, :, :], 0.0))
                ch.do(V.memset(acc_odd, 0.0))
                ch.wait()

                def negate(g, b):
                    V.tensor_scalar(f_neg[b], fields[:, g, :, LO], -1.0, None, ALU.mult).then_inc(sh["neg"], 1)

                negate(0, 0)
                dve.wait_ge(s_xtab, 32)

                def front(g, b):
                    ch.do(one_hot(blk7[b], fields[:, g, :, BLK], TG, SPAN, iota_w[:, 0:SPAN]))
                    one_hot(hot[b], fields[:, g, :, DST], TG, W, iota_w[:, :]).then_inc(sh["hot"], 1)

                def first_blocks(g, a, c):
                    return list(nc.values_load_multi_w_load_instructions(
                        block_table[bass.ds(g, 1), a:c], engines=[mybir.EngineType.DVE], min_val=0, max_val=NB - 1,
                        skip_runtime_bounds_check_because="a node's number shifted right by 7 is below NB")[1])

                def back(g, b, h, ahead=2):
                    dve.wait_ge(sh["vd"], NQ * g + NQ)
                    v2 = f_vv.rearrange("p n s d -> p n (s d)")
                    for k, (a, c) in enumerate(((0, VSPLIT), (VSPLIT, TG))):
                        n = c - a
                        ch.do(V.tensor_tensor(v2[:, a:c, :], ps_vv[k][:, 0:n * 2 * D].rearrange("p (n d) -> p n d", d=2 * D),
                                              b_out[:, :].unsqueeze(1).to_broadcast([P, n, 2 * D]), ALU.add))
                    ch.wait()
                    dve.sem_inc(sh["vfree"], 1)
                    dve.wait_ge(sh["xdc"], g + 2)
                    reflections(TG, f_vv, scaled_rows[b], f_msg, f_m1, f_m2, f_m3, f_small, f_qv)
                    ch.wait()
                    in_parts(f_msg[:, :, 1, :], [msg_part[:, :, k, :] for k in range(3)], msg_rest)
                    ch.wait()
                    dve.sem_inc(sh["msg"], 1)
                    V.tensor_tensor(msg_blk, blk7[b].unsqueeze(3).to_broadcast([P, TG, SPAN, D]),
                                    f_msg[:, :, 0, :].unsqueeze(2).to_broadcast([P, TG, SPAN, D]),
                                    ALU.mult).then_inc(sh["msgblk"], 1)
                    regs = first_blocks(g, 0, TG // 2)
                    if ahead == 2:
                        dve.wait_ge(sh["acc"], g + 1)
                        dve.sem_inc(s_tick, 1)
                        dve.wait_ge(sh["msgblk"], g + 1)
                        dve.sem_inc(s_tick, 1)
                        front(g + 2, b)
                    if ahead:
                        negate(g + 1, 1 - b)
                    regs += first_blocks(g, TG // 2, TG)
                    base = dve.value_load(first_i[0:1, bass.ds(g, 1)], min_val=0, max_val=N - 1)
                    dve.wait_ge(sh["accT"], g + 1)
                    acc = agg[0:D, bass.ds(base, W)]
                    V.tensor_tensor(acc, acc, ps_accT, ALU.add).then_inc(sh["accd"], 1)
                    for q, (a, c) in enumerate(SUMMED):
                        dve.wait_ge(sh["sc"], NQ * g + (q + 1))
                        for j in range(a, c):
                            acc = acc_src[j % 2].rearrange("p b d -> p (b d)")[:, bass.ds(regs[j] * D, SPAN * D)]
                            ch.wait(1)
                            ch.do(V.tensor_tensor(acc, acc, ps_sum[q % 2][:, (j - a) * SPAN * D:(j - a + 1) * SPAN * D], ALU.add))
                        ch.wait()
                        dve.sem_inc(sh["drained"], 1)
                    ch.restart()

                front(0, 0)
                front(1, 1)
                ch.restart()
                each_group(dve, back, NG - 2)
                back(NG - 2, 1, NG // 2 - 1, ahead=1)
                back(NG - 1, 0, NG // 2, ahead=0)
                ch.do(V.tensor_tensor(wide_node[:, :, :], wide_node[:, :, :], acc_odd, ALU.add))
                ch.restart()

            fast = dve.value_load(flag_i[0:1, 0:1], min_val=0, max_val=1)
            with dve.If(fast == 1):
                relational_and_sort()
            with dve.Else():
                dve.wait_ge(s_orig[0], 48)
                ch.do(V.memset(flag_i[0:1, 1:2], 0))
                ch.restart()
                relational_general(0)
                dve.sem_inc(s_flag, 1)
            dve.sem_inc(s_nodes, 1)
            nodes(0)
            dve.wait_ge(s_htab, 16)
            ch.do(V.memset(agg[:, :], 0.0))
            ch.restart()
            fast2 = dve.value_load(flag_i[0:1, 1:2], min_val=0, max_val=1)
            with dve.If(fast2 == 1):
                relational_sorted()
            with dve.Else():
                dve.wait_ge(s_orig[1], 48)
                relational_general(1)
            dve.sem_inc(s_nodes, 1)
            nodes(1)
            softmax_and_norm()
            with dve.If(fast2 == 1):
                sheaf_sorted()
            with dve.Else():
                sheaf_general()
            with dve.Fori(0, NC) as i:
                V.tensor_copy(agg_c[0:D, :], agg[0:D, bass.ds(i * CN, CN)]).then_inc(s_aggc, 1)
                dve.wait_ge(s_node, i + (2 * NC + 2))
                o = h_node[:, bass.ds(i * CB, CB), :]
                ch.do(V.tensor_tensor(o, o, ps_o[:, 0:CB * D].rearrange("p (b d) -> p b d", d=D), ALU.add))
                ch.restart()
            ch.do(V.tensor_tensor(z, z, wide(deg), ALU.mult))
            ch.wait()
            ch.do(V.tensor_tensor(z, z, y, ALU.add))
            ch.wait()
            ch.do(V.tensor_scalar(z, z, 0.0, None, ALU.max))
            ch.wait()
            ch.do(V.tensor_tensor(y, y, z, ALU.add))
            layer_norm(y, tmp, 5)
            V.tensor_tensor(y, y, wide(stat[1]), ALU.mult).then_inc(s_out, 1)

        @block.scalar
        def _(act):
            A = nc.scalar
            ch = Chain(act, s_ach)

            def one_hot(o, negated, done):
                for j in range(TG):
                    ch.do(A.activation(o[:, j, :], iota_w[:, :], ACT.Square, bias=negated[:, j:j + 1]))
                ch.wait()
                A.activation(o, o, ACT.Relu, bias=1.0, scale=-1.0).then_inc(done, 1)

            act.wait_ge(s_consts, 1)
            act.wait_ge(s_loaded, LOADED)
            act.wait_ge(s_flag, 1)
            fast = act.value_load(flag_i[0:1, 0:1], min_val=0, max_val=1)
            with act.If(fast == 1):
                def keep_sorted(g):
                    act.wait_ge(so["fldps"], g + 2)
                    act.sem_inc(s_tick, 1)
                    ch.restart()
                    A.copy(fields[:, g, :, :], ps_fld[:, 0:TG * 4].rearrange("p (j f) -> p j f", f=4)).then_inc(so["fldc"], 1)

                def group(g, before=None):
                    act.wait_ge(so["nlo"], g + 1)
                    act.sem_inc(s_tick, 1)
                    one_hot(lo_hot, neg, so["lohot"])
                    if before is not None:
                        keep_sorted(before)
                    act.wait_ge(so["nrl"], g + 1)
                    act.sem_inc(s_tick, 1)
                    one_hot(rank_hot, neg_rank, so["rlhot"])
                    ch.restart()
                group(0)
                with act.Fori(0, NG - 1) as g:
                    group(g + 1, before=g)
                keep_sorted(NG - 1)
            with act.Else():
                act.sem_inc(s_tick, 1)
            for phase in range(2):
                if phase == 1:
                    act.wait_ge(s_flag, 2)
                    fast2 = act.value_load(flag_i[0:1, 1:2], min_val=0, max_val=1)
                    with act.If(fast2 == 1):
                        with act.Fori(0, NG) as g:
                            act.wait_ge(fa["neg"], g + 1)
                            act.sem_inc(s_tick, 1)
                            for j in range(UMIN):
                                ch.do(A.activation(lo_hot[:, j, :], iota_w[:, :], ACT.Square, bias=dense_neg[:, j:j + 1]))
                            ch.wait()
                            A.activation(lo_hot[:, 0:UMIN, :], lo_hot[:, 0:UMIN, :], ACT.Relu, bias=1.0, scale=-1.0
                                         ).then_inc(fa["lohot"], 1)
                            for q in range(DQ):
                                act.wait_ge(fa["tr"], DQ * g + (q + 1))
                                A.copy(turned[:, q, :], ps_lo[q][:, :]).then_inc(fa["trc"], 1)
                            ch.restart()
                    with act.Else():
                        act.sem_inc(s_tick, 1)
                node = (x_node, wide_node)[phase]
                act.wait_ge(s_nodes, phase + 1)
                if phase == 1:
                    act.wait_ge(s_hnode, NC)
                with act.Fori(0, NC) as i:
                    A.copy(xs_c[:, :, :], node[:, bass.ds(i * CB, CB), :]).then_inc(s_xsc, 1)
                    act.wait_ge(s_xTp, i + (phase * NC + 1))
                    act.sem_inc(s_tick, 1)
                    act.wait_ge(s_node, i + (phase * NC + 1))
                    A.copy(xT_c[0:D, 0:4 * P], ps_xT[0][0:D, :])
                    A.copy(xT_c[0:D, 4 * P:CN], ps_xT[1][0:D, 0:CN - 4 * P]).then_inc(s_xTc, 1)
            tmp = agg[:, 0:NB * D].rearrange("p (b d) -> p b d", d=D)
            act.wait_ge(s_exp, 1)
            A.activation(tmp, h_node, ACT.Exp).then_inc(s_act, 1)
            A.activation(deg[:, :], deg[:, :], ACT.Sqrt).then_inc(s_act, 1)
            act.wait_ge(s_exp, 2)
            A.activation(stat[1][:, :], stat[1][:, :], ACT.Ln).then_inc(s_act, 1)
            act.wait_ge(s_exp, 3)
            A.activation(stat[1][:, :], stat[1][:, :], ACT.Sqrt).then_inc(s_act, 1)
            act.wait_ge(s_ztab, 1)
            with act.If(fast2 == 1):
                def squares(b, a, c):
                    for j in range(a, c):
                        ch.do(A.activation(src_hot[:, j, :], iota_w[:, :], ACT.Square, bias=f_neg[b][:, j:j + 1]))

                def reduce(g):
                    ch.wait()
                    A.activation(src_hot, src_hot, ACT.Relu, bias=1.0, scale=-1.0).then_inc(sh["srchot"], 1)
                    act.wait_ge(sh["acc"], g + 1)
                    A.copy(acc_w, ps_accw).then_inc(sh["accc"], 1)
                    ch.restart()

                def rounds(g, b, before=None):
                    if before is not None:
                        act.wait_ge(sh["neg"], before + 1)
                        act.sem_inc(s_tick, 1)
                    for k in range(NQ + 2):
                        if k < NQ:
                            m = (QUADS[k][1] - QUADS[k][0]) * P
                            act.wait_ge(sh["tr"], NQ * g + (k + 1))
                            A.copy(f_dT[k % 2][:, 0:m], ps_dT[:, 0:m]).then_inc(sh["dt"], 1)
                        if 0 < k <= NQ:
                            m = (QUADS[k - 1][1] - QUADS[k - 1][0]) * P
                            act.wait_ge(sh["ttr"], NQ * g + k)
                            A.copy(f_xT[(k - 1) % 2][:, 0:m], ps_rT[:, 0:m]).then_inc(sh["xt"], 1)
                        if k > 1:
                            m = (QUADS[k - 2][1] - QUADS[k - 2][0]) * P
                            act.wait_ge(sh["hp"], NQ * g + (k - 1))
                            act.sem_inc(s_tick, 1)
                            A.activation(f_hid[k % 2][:, 0:m], ps_hid[:, 0:m], ACT.Relu, bias=b_hid[:, 0:1]).then_inc(sh["hs"], 1)
                        if k == NQ:
                            act.wait_ge(sh["xd"], g + 1)
                            A.copy(scaled_rows[b][:, :, 0, :], rows[b][:, :, XS:XY]).then_inc(sh["xfree"][b], 1)
                            A.copy(scaled_rows[b][:, :, 1, :],
                                   ps_y[:, 0:TG * D].rearrange("p (n d) -> p n d", d=D)).then_inc(sh["xdc"], 1)
                        if before is not None and k < NQ:
                            squares(1 - b, *QUADS[k])

                rounds(0, 0)

                def turn(g, b, h):
                    rounds(g + 1, 1 - b, g)
                    reduce(g)
                each_group(act, turn, NG - 1)
                act.wait_ge(sh["neg"], NG)
                act.wait_ge(sh["sc"], NQ * (NG - 1))
                squares(0, 0, TG)
                reduce(NG - 1)
            with act.Else():
                with act.Fori(0, NG) as g:
                    done = 0
                    for u, (a, b) in enumerate(UNITS):
                        nch = len(CHUNKS[u])
                        for s in range(nch + 1):
                            if s < nch:
                                m = (CHUNKS[u][s][1] - CHUNKS[u][s][0]) * P
                                act.wait_ge(gs["tr"], NCH * g + (done + s + 1))
                                A.copy(g_xT[s % 2][0:2 * ROW, 0:m], ps_t[s % 2][0:2 * ROW, 0:m]).then_inc(gs["xt"], 1)
                            if s > 0:
                                c = s - 1
                                m = (CHUNKS[u][c][1] - CHUNKS[u][c][0]) * P
                                act.wait_ge(gs["hp"], NCH * g + (done + c + 1))
                                act.sem_inc(s_tick, 1)
                                act.wait_ge(gs["vd"], NCH * g + (done + max(c - 1, 0) + 1))
                                A.activation(g_hid[c % 2][:, 0:m], ps_h[c % 2][:, 0:m], ACT.Relu,
                                             bias=b_hid[:, 0:1]).then_inc(gs["hs"], 1)
                        act.wait_ge(gs["scat"][u], g + 1)
                        act.sem_inc(s_tick, 1)
                        act.wait_ge(gs["sp"], 2 * g + (u + 1))
                        A.copy(msum[u][:, 0:b - a, :],
                               ps_s[:, 0:(b - a) * D].rearrange("p (n d) -> p n d", d=D)).then_inc(gs["ms"], 1)
                        done += nch
            act.wait_ge(s_exp, 4)
            A.activation(stat[1][:, :], stat[1][:, :], ACT.Sqrt).then_inc(s_act, 1)

        @block.tensor
        def _(pe):
            mm = nc.tensor.matmul

            def wait(s, value):
                pe.wait_ge(s, value)
                pe.sem_inc(s_tick, 1)

            pe.wait_ge(s_consts, 1)
            mm(ps_acc[:, 0:NG], ones[0:1, :], first_f[0:1, :], start=True, stop=True).then_inc(s_row, 1)
            pe.wait_ge(s_flag, 1)
            pe.wait_ge(s_loaded, LOADED)

            def sums_by_relation(n, counts, s_acc, typ_x=typ_x, dst_hot=dst_hot, ps_acc=ps_acc):
                if counts:
                    for j in range(n):
                        mm(ps_cnt[0:R, 0:W], typ_hot[:, j, :], dst_hot[:, j, :], start=j == 0, stop=j == n - 1)
                for j in range(n):
                    last = mm(ps_acc[:, 0:W], typ_x[:, j, :, :].rearrange("p r d -> p (r d)"),
                              dst_hot[:, j, :], start=j == 0, stop=j == n - 1)
                last.then_inc(s_acc, 1)

            def relational_general(phase):
                s = gen[phase]
                with pe.Fori(0, NG) as g:
                    for u, (a, b) in enumerate(UNITS):
                        n = b - a
                        if phase == 0:
                            wait(s["hhot"], 2 * g + (u + 1))
                            for j in range(n):
                                last = mm(ps_hist[:, 0:NB], lo_hot_u[:, j, :], blk_hot_u[:, j, :], start=j == 0, stop=j == n - 1)
                            last.then_inc(s["hist"], 1)
                        with pe.Fori(0, NW) as w:
                            wait(s["hot"], g * (2 * NW) + w + (u * NW + 1))
                            sums_by_relation(n, phase == 0, s["acc"])

            def relational_and_sort():
                def to_ranks(g):
                    wait(so["fld"], g + 1)
                    wait(so["rlhot"], g + 1)
                    for j in range(TG):
                        last = mm(ps_fld[:, 0:TG * 4], rank_hot[:, j, :], x_hot[:, j, :, :].rearrange("p r f -> p (r f)"),
                                  start=j == 0, stop=j == TG - 1)
                    last.then_inc(so["fldps"], 1)

                def group(g, before=None):
                    def layer(u):
                        wait(so["hot"], 2 * g + (u + 1))
                        sums_by_relation(UNITS[u][1] - UNITS[u][0], True, so["acc"])

                    wait(so["blkhot"], g + 1)
                    for j in range(TG):
                        last = mm(ps_tot[0:NB, 0:P], blk_hot[:, j, :], ones_b[:, :], start=j == 0, stop=j == TG - 1)
                    last.then_inc(so["tot"], 1)
                    for j in range(TG):
                        mm(ps_rank[:, 0:NB], after_b[:, :], blk_hot[:, j, :], start=j == 0, stop=False)
                    layer(0)
                    wait(so["totc"], g + 1)
                    mm(ps_rank[:, 0:NB], tot_T, after[0:NB, 0:NB], start=False, stop=True).then_inc(so["base"], 1)
                    if before is not None:
                        to_ranks(before)
                    layer(1)
                    wait(so["lohot"], g + 1)
                    for j in range(TG):
                        last = mm(ps_hist[:, 0:NB], lo_hot[:, j, :], blk_hot[:, j, :], start=j == 0, stop=j == TG - 1)
                    last.then_inc(so["hist"], 1)
                group(0)
                with pe.Fori(0, NG - 1) as g:
                    group(g + 1, before=g)
                to_ranks(NG - 1)
                wait(so["rows"], 1)
                for k in range(ROWS):
                    a, b = k * GR * TG, min((k + 1) * GR, NG) * TG
                    last = mm(bank[k][:, 0:b - a], ones[0:1, :], row_f[0:1, a:b], start=True, stop=True)
                last.then_inc(so["rowsps"], 1)

            def relational_sorted():
                second = UNITS[1][0]

                def half(g, u):
                    wait(fa["hot"], 2 * g + (u + 1))
                    if u:
                        sums_by_relation(UMIN, False, fa["acc"], typ_x1, dst_hot1, ps_acc1)
                    else:
                        sums_by_relation(UMAX, False, fa["acc"])

                def turn_low(g):
                    wait(fa["lohot"], g + 1)
                    for q in range(DQ):
                        for j in range(4):
                            last = mm(ps_lo[q][:, j * P:(j + 1) * P], lo_hot[:, 4 * q + j, :], ident_b[:, :], start=True, stop=True)
                        last.then_inc(fa["tr"], 1)

                def products(g):
                    regs = nc.values_load_multi_w_load_instructions(
                        block_table[bass.ds(g, 1), second:TG], engines=[mybir.EngineType.PE], min_val=0, max_val=NB - 1,
                        skip_runtime_bounds_check_because="a node's number shifted right by 7 is below NB")[1]
                    h_all = wide_node[:, :, :].rearrange("p b d -> p (b d)")
                    for q in range(DQ):
                        wait(fa["trc"], DQ * g + (q + 1))
                        for j in range(4):
                            last = mm(ps_rows[q][:, j * SPAN * D:(j + 1) * SPAN * D], turned[:, q, j * P:(j + 1) * P],
                                      h_all[:, bass.ds(regs[4 * q + j] * D, SPAN * D)], start=True, stop=True)
                    last.then_inc(fa["rows"], 1)

                turn_low(0)
                products(0)
                with pe.Fori(0, NG - 1) as g:
                    half(g, 0)
                    turn_low(g + 1)
                    half(g, 1)
                    products(g + 1)
                for u in range(2):
                    half(NG - 1, u)

            def nodes(phase):
                def inverse(i):
                    wait(s_inv, i + (phase * NC + 1))
                    for h in range(2):
                        last = mm(ps_E[h][:, 0:CN // 2], expand[:, :], inv_c[:, h * CN // 2:(h + 1) * CN // 2],
                                  start=True, stop=True)
                    last.then_inc(s_E, 1)

                def step(i, more=True):
                    wait(s_xsc, i + (phase * NC + 1))
                    for b in range(CB):
                        last = nc.tensor.transpose(ps_xT[b // 4][0:D, (b % 4) * P:(b % 4 + 1) * P], xs_c[:, b, :], ident[:, :])
                    last.then_inc(s_xTp, 1)
                    wait(s_aggc, i + (phase * NC + 1))
                    wait(s_xTc, i + (phase * NC + 1))
                    for b in range(CB):
                        o = ps_o[:, b * D:(b + 1) * D]
                        mm(o, agg_c[:, b * P:(b + 1) * P], wrel[phase][:, :], start=True, stop=False)
                        last = mm(o, xT_c[:, b * P:(b + 1) * P], root[phase][:, :], start=False, stop=True)
                        if phase == 0:
                            last = mm(ps_o[:, CB * D + b:CB * D + b + 1], cnt_c[:, b * P:(b + 1) * P], ones[0:R, 0:1],
                                      start=True, stop=True)
                    last.then_inc(s_node, 1)
                    if more:
                        inverse(i + 1)

                inverse(0)
                with pe.Fori(0, NC - 1) as i:
                    step(i)
                step(NC - 1, more=False)

            def hidden_layers(tiles, s, rows, xT, hid, at, n0, n_all, v_at, v_wait):
                nch = len(tiles)
                for k in range(nch + 2):
                    if k < nch:
                        ca, cb = tiles[k]
                        for j in range(ca, cb):
                            last = nc.tensor.transpose(ps_t[k % 2][0:2 * ROW, (j - ca) * P:(j - ca + 1) * P],
                                                       rows[:, j, :], ident[:, :])
                        last.then_inc(s[at], 1)
                    if 0 < k <= nch:
                        c = k - 1
                        m = (tiles[c][1] - tiles[c][0]) * P
                        wait(s["xt"], n_all + (n0 + c + 1))
                        mm(ps_h[c % 2][:, 0:m], w_hid[:, :], xT[c % 2][0:2 * ROW, 0:m],
                           start=True, stop=True).then_inc(s["hp"], 1)
                    if k > 1:
                        c = k - 2
                        ca, cb = tiles[c]
                        wait(s["hs"], n_all + (n0 + c + 1))
                        if c == 0:
                            wait(s["vfree"], v_wait)
                        for j in range(ca, cb):
                            last = mm(v_at(j), hid[c % 2][:, (j - ca) * P:(j - ca + 1) * P], w_out[:, :], start=True, stop=True)
                        last.then_inc(s["vd"], 1)

            def sheaf_general():
                with pe.Fori(0, NG) as g:
                    done = 0
                    for u, (a, b) in enumerate(UNITS):
                        n = b - a
                        wait(gs["same"], 2 * g + (u + 1))
                        for c, (ca, cb) in enumerate(CHUNKS[u]):
                            wait(gs["rused"], NCH * g + (done + c + 1))
                            for j in range(ca, cb):
                                last = mm(ps_r[:, (j - ca) * P:(j - ca + 1) * P], srcf[:, j:j + 1].to_broadcast([P, P]),
                                          ident[:, :], start=True, stop=True)
                            last.then_inc(gs["rr"], 1)
                        wait(gs["gat"][u], g * (32 * n) + 32 * n)
                        hidden_layers(CHUNKS[u], gs, xx[u], g_xT, g_hid, "tr", done, NCH * g,
                                      lambda j: ps_v[:, j * 2 * D:(j + 1) * 2 * D], 2 * g + (u + 1))
                        wait(gs["msg"], 2 * g + (u + 1))
                        wait(gs["ms"], 2 * g + (u + 1))
                        for j in range(n):
                            last = mm(ps_s[:, j * D:(j + 1) * D], same[:, j, :], g_msg[u][:, j, 0, :], start=True, stop=True)
                        last.then_inc(gs["sp"], 1)
                        with pe.Fori(0, NW) as w:
                            wait(gs["hot"], g * (2 * NW) + w + (u * NW + 1))
                            for j in range(n):
                                last = mm(ps_acc[0:D, 0:W], g_msg[u][:, j, 1, :], dst_hot[:, j, :], start=j == 0, stop=j == n - 1)
                            last.then_inc(gs["acc"], 1)
                        done += len(CHUNKS[u])

            def sheaf_sorted():
                def acc(g, b):
                    wait(sh["msg"], g + 1)
                    wait(sh["drained"], NQ * g + 2 * NQ)
                    for j in range(TG):
                        for k in range(3):
                            last = mm(ps_accw, hot[b][:, j, :], msg_part[:, j, k, :],
                                      start=j == 0 and k == 0, stop=j == TG - 1 and k == 2)
                    last.then_inc(sh["acc"], 1)

                def rounds(g, b, h, before=None):
                    for k in range(NQ + 3):
                        if k:
                            if k <= NQ:
                                wait(sh["dt"], NQ * g + k)
                        else:
                            wait(sh["hot"], g + 1)
                        if k < NQ:
                            a, c = QUADS[k]
                            for j in range(a, c):
                                last = mm(ps_dT[:, (j - a) * P:(j - a + 1) * P], hot[b][:, j, :], ident_b[:, :], start=True, stop=True)
                            last.then_inc(sh["tr"], 1)
                        if k > 1 and k <= NQ + 1:
                            wait(sh["xt"], NQ * g + (k - 1))
                        if 0 < k <= NQ:
                            a, c = QUADS[k - 1]
                            dT = f_dT[(k - 1) % 2]
                            parts = xwin[b].bitcast(bf16)
                            if k == 1:
                                wait(sh["win"][b], 16 * h + 16)
                                wait(sh["gat"][b], 16 * TG * h + 16 * TG)
                                wait(sh["xdc"], g + 1)
                            for j in range(a, c):
                                for i in range(3):
                                    last = mm(ps_y[:, j * D:(j + 1) * D], dT[:, (j - a) * P:(j - a + 1) * P],
                                              parts[:, 2 * XY + i * D:2 * XY + (i + 1) * D], start=i == 0, stop=i == 2)
                            if k == NQ:
                                last.then_inc(sh["xd"], 1)
                            for j in range(a, c):
                                mm(ps_rT[0:4 * D, (j - a) * P:(j - a + 1) * P], rows[b][:, j, 0:XS].bitcast(bf16), ident_b[:, :],
                                   start=True, stop=True)
                            mm(ps_rT[4 * D:8 * D, 0:(c - a) * P], parts[:, 0:4 * D], dT[:, 0:(c - a) * P],
                               start=True, stop=True).then_inc(sh["ttr"], 1)
                        if k > 2:
                            wait(sh["hs"], NQ * g + (k - 2))
                        if 1 < k <= NQ + 1:
                            m = (QUADS[k - 2][1] - QUADS[k - 2][0]) * P
                            for i in range(2):
                                last = mm(ps_hid[:, 0:m], w_split[i][:, :], f_xT[k % 2][:, 0:m], start=i == 0, stop=i == 1)
                            last.then_inc(sh["hp"], 1)
                        if k == NQ + 1:
                            pe.sem_inc(sh["winfree"][b], 1)
                        if k > 2:
                            a, c = QUADS[k - 3]
                            if k == 3:
                                wait(sh["vfree"], g + 1)
                            for j in range(a, c):
                                o = ps_vv[j // VSPLIT][:, (j % VSPLIT) * 2 * D:(j % VSPLIT + 1) * 2 * D]
                                last = mm(o, f_hid[(k - 3) % 2][:, (j - a) * P:(j - a + 1) * P], w_out[:, :], start=True, stop=True)
                            last.then_inc(sh["vd"], 1)
                        if k < 2 and before is not None:
                            by_source(before, *((2, 5), (5, NQ))[k])

                def by_source(g, first, end):
                    for q in range(first, min(end, NQ)):
                        a, c = SUMMED[q]
                        wait(sh["drained"], NQ * g + (2 * NQ + q - 1))
                        for j in range(a, c):
                            last = mm(ps_sum[q % 2][:, (j - a) * SPAN * D:(j - a + 1) * SPAN * D], src_hot[:, j, :],
                                      msg_blk[:, j, :, :].rearrange("p s d -> p (s d)"), start=True, stop=True)
                        last.then_inc(sh["sc"], 1)

                def back(g):
                    wait(sh["accc"], g + 1)
                    mm(ps_accT, acc_w, ident[:, :], start=True, stop=True).then_inc(sh["accT"], 1)
                    wait(sh["msgblk"], g + 1)
                    wait(sh["srchot"], g + 1)
                    by_source(g, 0, 1)
                    wait(sh["accd"], g + 1)
                    by_source(g, 1, 2)

                rounds(0, 0, 0)
                rounds(1, 1, 0)
                acc(0, 0)
                back(0)

                def turn(i, b, h):
                    rounds(i + 2, b, h + 1, before=i)
                    acc(i + 1, 1 - b)
                    back(i + 1)
                each_group(pe, turn, NG - 2)
                by_source(NG - 2, 2, NQ)
                acc(NG - 1, 0)
                back(NG - 1)
                by_source(NG - 1, 2, NQ)

            fast = pe.value_load(flag_i[0:1, 0:1], min_val=0, max_val=1)
            with pe.If(fast == 1):
                relational_and_sort()
            with pe.Else():
                relational_general(0)
            wait(s_nodes, 1)
            nodes(0)
            wait(s_flag, 2)
            fast2 = pe.value_load(flag_i[0:1, 1:2], min_val=0, max_val=1)
            with pe.If(fast2 == 1):
                relational_sorted()
            with pe.Else():
                relational_general(1)
            wait(s_nodes, 2)
            nodes(1)
            with pe.If(fast2 == 1):
                sheaf_sorted()
            with pe.Else():
                sheaf_general()
            with pe.Fori(0, NC) as i:
                wait(s_aggc, i + (2 * NC + 1))
                for b in range(CB):
                    last = nc.tensor.transpose(ps_o[:, b * D:(b + 1) * D], agg_c[0:D, b * P:(b + 1) * P], ident[0:D, 0:D])
                last.then_inc(s_node, 1)



_INS = ['x', 'src', 'dst', 'edge_type_8', 'L0_gnn_W1', 'L0_gnn_root1', 'L0_gnn_b1', 'L0_gnn_W2', 'L0_gnn_root2', 'L0_gnn_b2', 'L1_gnn_W1', 'L1_gnn_b1', 'L1_gnn_W2', 'L1_gnn_b2']


def kernel(**inputs):
    import numpy as _np
    import concourse.bacc as _bacc
    from concourse import mybir as _mybir
    from concourse.bass_utils import run_bass_kernel_spmd as _run

    nc = _bacc.Bacc("TRN2", target_bir_lowering=False, num_devices=1)
    arrays, args = {}, []
    for name in _INS:
        a = _np.ascontiguousarray(inputs[name])
        arrays[f"in_{name}"] = a
        args.append(nc.dram_tensor(f"in_{name}", a.shape, _mybir.dt.from_np(a.dtype), kind="ExternalInput").ap())
    args.append(nc.dram_tensor("out", (12500, 16), _mybir.dt.float32, kind="ExternalOutput").ap())
    build(nc, *args)
    r = _run(nc, [arrays], core_ids=[0])
    return r.results[0]["out"]
```
